# Optimizing a Trainium2 kernel written in Bass

```python
import numpy as np
import jax
import jax.numpy as jnp

def _softmax(x, axis=-1):
    return jax.nn.softmax(x, axis=axis)

def _gelu(x):
    return jax.nn.gelu(x, approximate=True)

def _silu(x):
    return jax.nn.silu(x)

def _sigmoid(x):
    return jax.nn.sigmoid(x)

def _layernorm(x, axis=-1, eps=1e-05):
    m = jnp.mean(x, axis=axis, keepdims=True)
    v = jnp.var(x, axis=axis, keepdims=True)
    return (x - m) / jnp.sqrt(v + eps)

def _scatter_add(tgt, idx, src, axis=0):
    return tgt.at[idx].add(src)

def _segment_sum(src, seg, n):
    return jax.ops.segment_sum(src, seg, n)
kernel_name = 'mk_hybrid_d1_jaxref_r8_d2dd53'

def setup_inputs(seed: int=0):
    np.random.seed(seed)
    _w = jnp.asarray

    def _L0_attn_a_setup():
        import jax, jax.numpy as jnp
        import numpy as np
        B_, L, D_MODEL = (2, 512, 256)
        H, P, N, G, K = (32, 64, 128, 1, 4)
        EPS = 1e-05
        INTER = H * P
        CONV_DIM = INTER + 2 * G * N
        PROJ = INTER + CONV_DIM + H

        def _silu(x):
            return x * jax.nn.sigmoid(x)

        def _mamba2_mixer(hidden_states, W_in, conv_w, conv_b, dt_bias, A_log, D_param, norm_w, W_out):
            b, l, _ = hidden_states.shape
            proj = jnp.einsum('bld,pd->blp', hidden_states, W_in)
            gate = proj[..., :INTER]
            hBC = proj[..., INTER:INTER + CONV_DIM]
            dt = proj[..., INTER + CONV_DIM:]
            xc = jnp.transpose(hBC, (0, 2, 1))
            conv = jax.lax.conv_general_dilated(xc, conv_w[:, None, :], window_strides=(1,), padding=[(K - 1, 0)], dimension_numbers=('NCH', 'OIH', 'NCH'), feature_group_count=CONV_DIM)
            hBC = _silu(jnp.transpose(conv + conv_b[None, :, None], (0, 2, 1)))
            xs = hBC[..., :INTER].reshape(b, l, H, P)
            Bm = hBC[..., INTER:INTER + G * N].reshape(b, l, G, N)
            Cm = hBC[..., INTER + G * N:].reshape(b, l, G, N)
            Bh = jnp.repeat(Bm, H // G, axis=2)
            Ch = jnp.repeat(Cm, H // G, axis=2)
            dt = jax.nn.softplus(dt + dt_bias)
            A = -jnp.exp(A_log)
            dA = jnp.exp(dt * A)

            def step(h, inp):
                dA_t, dt_t, x_t, B_t, C_t = inp
                u = (dt_t[:, :, None] * x_t)[..., None] * B_t[:, :, None, :]
                h = dA_t[:, :, None, None] * h + u
                y = jnp.einsum('bhpn,bhn->bhp', h, C_t)
                return (h, y)
            tm = lambda a: jnp.moveaxis(a, 1, 0)
            h0 = jnp.zeros((b, H, P, N), hidden_states.dtype)
            _, ys = jax.lax.scan(step, h0, (tm(dA), tm(dt), tm(xs), tm(Bh), tm(Ch)))
            y = jnp.moveaxis(ys, 0, 1) + D_param[None, None, :, None] * xs
            y = y.reshape(b, l, INTER)
            g = y * _silu(gate)
            g = g * jax.lax.rsqrt(jnp.mean(g * g, axis=-1, keepdims=True) + EPS) * norm_w
            return jnp.einsum('bli,di->bld', g, W_out)
        key = jax.random.key(seed)
        ks = jax.random.split(key, 5)
        hidden_states = jax.random.normal(ks[0], (B_, L, D_MODEL), jnp.float32)
        W_in = jax.random.normal(ks[1], (PROJ, D_MODEL), jnp.float32) * 0.02
        conv_w = jax.random.normal(ks[2], (CONV_DIM, K), jnp.float32) * 0.1
        conv_b = jnp.zeros((CONV_DIM,), jnp.float32)
        dt_bias = jnp.ones((H,), jnp.float32)
        A_log = jnp.log(jnp.arange(1, H + 1, dtype=jnp.float32))
        D_param = jnp.ones((H,), jnp.float32)
        norm_w = jnp.ones((INTER,), jnp.float32)
        W_out = jax.random.normal(ks[3], (D_MODEL, INTER), jnp.float32) * 0.02
        return dict(hidden_states=hidden_states, W_in=W_in, conv_w=conv_w, conv_b=conv_b, dt_bias=dt_bias, A_log=A_log, D_param=D_param, norm_w=norm_w, W_out=W_out)
    _L0_attn_a_in = _L0_attn_a_setup()

    def _L0_attn_b_setup():
        import jax, jax.numpy as jnp
        import numpy as np
        B, S, D = (2, 256, 256)
        H = 16
        HD = D // H
        key = jax.random.key(seed)
        k1, k2, k3 = jax.random.split(key, 3)
        x = jax.random.normal(k1, (B, S, D), dtype=jnp.float32)
        w_qkv = jax.random.normal(k2, (D, 3 * D), dtype=jnp.float32) * (1.0 / np.sqrt(D))
        b_qkv = jnp.zeros((3 * D,), dtype=jnp.float32)
        w_out = jax.random.normal(k3, (D, D), dtype=jnp.float32) * (1.0 / np.sqrt(D))
        b_out = jnp.zeros((D,), dtype=jnp.float32)
        return {'x': x, 'w_qkv': w_qkv, 'b_qkv': b_qkv, 'w_out': w_out, 'b_out': b_out}
    _L0_attn_b_in = _L0_attn_b_setup()

    def _L0_ffn_setup():
        import jax, jax.numpy as jnp
        import numpy as np
        HIDDEN = 256
        INTER = 96
        N_EXPERTS = 32
        TOP_K = 8
        key = jax.random.key(seed)
        k = jax.random.split(key, 5)
        s = 1.0 / np.sqrt(HIDDEN)
        return {'hidden_states': jax.random.normal(k[0], (1, 128, HIDDEN), jnp.float32), 'gate_w': jax.random.normal(k[1], (HIDDEN, N_EXPERTS), jnp.float32) * s, 'w_gate': jax.random.normal(k[2], (N_EXPERTS, HIDDEN, INTER), jnp.float32) * s, 'w_up': jax.random.normal(k[3], (N_EXPERTS, HIDDEN, INTER), jnp.float32) * s, 'w_down': jax.random.normal(k[4], (N_EXPERTS, INTER, HIDDEN), jnp.float32) * (1.0 / np.sqrt(INTER))}
    _L0_ffn_in = _L0_ffn_setup()
    _d = {'L0_attn_a_hidden_states': _L0_attn_a_in['hidden_states'], 'L0_attn_a_W_in': _L0_attn_a_in['W_in'], 'L0_attn_a_conv_w': _L0_attn_a_in['conv_w'], 'L0_attn_a_conv_b': _L0_attn_a_in['conv_b'], 'L0_attn_a_dt_bias': _L0_attn_a_in['dt_bias'], 'L0_attn_a_A_log': _L0_attn_a_in['A_log'], 'L0_attn_a_D_param': _L0_attn_a_in['D_param'], 'L0_attn_a_norm_w': _L0_attn_a_in['norm_w'], 'L0_attn_a_W_out': _L0_attn_a_in['W_out'], 'L0_attn_b_w_qkv': _L0_attn_b_in['w_qkv'], 'L0_attn_b_b_qkv': _L0_attn_b_in['b_qkv'], 'L0_attn_b_w_out': _L0_attn_b_in['w_out'], 'L0_attn_b_b_out': _L0_attn_b_in['b_out'], 'L0_ffn_gate_w': _L0_ffn_in['gate_w'], 'L0_ffn_w_gate': _L0_ffn_in['w_gate'], 'L0_ffn_w_up': _L0_ffn_in['w_up'], 'L0_ffn_w_down': _L0_ffn_in['w_down']}
    _x0 = _d['L0_attn_a_hidden_states']
    _d['L0_attn_a_hidden_states'] = jax.random.normal(jax.random.fold_in(jax.random.key(seed), 1), (8, 256, 256), dtype=_x0.dtype)
    del _x0
    return _d

def reference(L0_attn_a_hidden_states, L0_attn_a_W_in, L0_attn_a_conv_w, L0_attn_a_conv_b, L0_attn_a_dt_bias, L0_attn_a_A_log, L0_attn_a_D_param, L0_attn_a_norm_w, L0_attn_a_W_out, L0_attn_b_w_qkv, L0_attn_b_b_qkv, L0_attn_b_w_out, L0_attn_b_b_out, L0_ffn_gate_w, L0_ffn_w_gate, L0_ffn_w_up, L0_ffn_w_down):

    def _L0_attn_a_ref(hidden_states, W_in, conv_w, conv_b, dt_bias, A_log, D_param, norm_w, W_out):
        import jax, jax.numpy as jnp
        import numpy as np
        B_, L, D_MODEL = (2, 512, 256)
        H, P, N, G, K = (32, 64, 128, 1, 4)
        EPS = 1e-05
        INTER = H * P
        CONV_DIM = INTER + 2 * G * N
        PROJ = INTER + CONV_DIM + H

        def _silu(x):
            return x * jax.nn.sigmoid(x)

        def _mamba2_mixer(hidden_states, W_in, conv_w, conv_b, dt_bias, A_log, D_param, norm_w, W_out):
            b, l, _ = hidden_states.shape
            proj = jnp.einsum('bld,pd->blp', hidden_states, W_in)
            gate = proj[..., :INTER]
            hBC = proj[..., INTER:INTER + CONV_DIM]
            dt = proj[..., INTER + CONV_DIM:]
            xc = jnp.transpose(hBC, (0, 2, 1))
            conv = jax.lax.conv_general_dilated(xc, conv_w[:, None, :], window_strides=(1,), padding=[(K - 1, 0)], dimension_numbers=('NCH', 'OIH', 'NCH'), feature_group_count=CONV_DIM)
            hBC = _silu(jnp.transpose(conv + conv_b[None, :, None], (0, 2, 1)))
            xs = hBC[..., :INTER].reshape(b, l, H, P)
            Bm = hBC[..., INTER:INTER + G * N].reshape(b, l, G, N)
            Cm = hBC[..., INTER + G * N:].reshape(b, l, G, N)
            Bh = jnp.repeat(Bm, H // G, axis=2)
            Ch = jnp.repeat(Cm, H // G, axis=2)
            dt = jax.nn.softplus(dt + dt_bias)
            A = -jnp.exp(A_log)
            dA = jnp.exp(dt * A)

            def step(h, inp):
                dA_t, dt_t, x_t, B_t, C_t = inp
                u = (dt_t[:, :, None] * x_t)[..., None] * B_t[:, :, None, :]
                h = dA_t[:, :, None, None] * h + u
                y = jnp.einsum('bhpn,bhn->bhp', h, C_t)
                return (h, y)
            tm = lambda a: jnp.moveaxis(a, 1, 0)
            h0 = jnp.zeros((b, H, P, N), hidden_states.dtype)
            _, ys = jax.lax.scan(step, h0, (tm(dA), tm(dt), tm(xs), tm(Bh), tm(Ch)))
            y = jnp.moveaxis(ys, 0, 1) + D_param[None, None, :, None] * xs
            y = y.reshape(b, l, INTER)
            g = y * _silu(gate)
            g = g * jax.lax.rsqrt(jnp.mean(g * g, axis=-1, keepdims=True) + EPS) * norm_w
            return jnp.einsum('bli,di->bld', g, W_out)
        return _mamba2_mixer(hidden_states, W_in, conv_w, conv_b, dt_bias, A_log, D_param, norm_w, W_out)

    def _L0_attn_b_ref(x, w_qkv, b_qkv, w_out, b_out):
        import jax, jax.numpy as jnp
        import numpy as np
        B, S, D = (2, 256, 256)
        H = 16
        HD = D // H
        batch, seq_len, channels = x.shape
        qkv = x @ w_qkv + b_qkv
        q, k, v = jnp.split(qkv, 3, axis=-1)

        def heads(t):
            return t.reshape(batch, seq_len, H, HD).transpose(0, 2, 1, 3)
        q, k, v = (heads(q), heads(k), heads(v))
        scale = 1.0 / np.sqrt(HD).astype(np.float32)
        attn = jnp.einsum('bhqd,bhkd->bhqk', q, k) * scale
        causal = jnp.tril(jnp.ones((seq_len, seq_len), dtype=bool))
        attn = jnp.where(causal, attn, -jnp.inf)
        attn = jax.nn.softmax(attn, axis=-1)
        y = jnp.einsum('bhqk,bhkd->bhqd', attn, v)
        y = y.transpose(0, 2, 1, 3).reshape(batch, seq_len, channels)
        return y @ w_out + b_out

    def _L0_ffn_ref(hidden_states, gate_w, w_gate, w_up, w_down):
        import jax, jax.numpy as jnp
        import numpy as np
        HIDDEN = 256
        INTER = 96
        N_EXPERTS = 32
        TOP_K = 8
        B, S, H = hidden_states.shape
        E = gate_w.shape[1]
        x = hidden_states.reshape(-1, H)
        T = x.shape[0]
        K = TOP_K
        P = T * K
        C = 2 * (P // E)
        probs = jax.nn.softmax(x @ gate_w, axis=-1)
        w, sel = jax.lax.top_k(probs, K)
        w = w / jnp.sum(w, axis=-1, keepdims=True)
        flat_e = sel.reshape(-1)
        flat_t = jnp.repeat(jnp.arange(T), K)
        flat_w = w.reshape(-1)
        order = jnp.argsort(flat_e)
        se = flat_e[order]
        start = jnp.searchsorted(se, jnp.arange(E))
        pos = jnp.arange(P) - start[se]
        slot = jnp.where(pos < C, se * C + pos, E * C)
        slot_pair = jnp.full((E * C,), P, dtype=jnp.int32).at[slot].set(order.astype(jnp.int32), mode='drop')
        t_slot = jnp.concatenate([flat_t, jnp.array([T])])[slot_pair]
        w_slot = jnp.concatenate([flat_w, jnp.zeros((1,), flat_w.dtype)])[slot_pair]
        x_pad = jnp.concatenate([x, jnp.zeros((1, H), x.dtype)], axis=0)
        xg = x_pad[t_slot].reshape(E, C, H)
        g = jnp.einsum('ech,ehi->eci', xg, w_gate)
        u = jnp.einsum('ech,ehi->eci', xg, w_up)
        y = jnp.einsum('eci,eih->ech', jax.nn.silu(g) * u, w_down).reshape(E * C, H)
        out = jnp.zeros((T + 1, H), x.dtype).at[t_slot].add(w_slot[:, None] * y)
        return out[:T].reshape(B, S, H)
    x = L0_attn_a_hidden_states
    x = x + _L0_attn_a_ref(_layernorm(x, axis=-1), L0_attn_a_W_in, L0_attn_a_conv_w, L0_attn_a_conv_b, L0_attn_a_dt_bias, L0_attn_a_A_log, L0_attn_a_D_param, L0_attn_a_norm_w, L0_attn_a_W_out)
    x = x + _L0_ffn_ref(_layernorm(x, axis=-1), L0_ffn_gate_w, L0_ffn_w_gate, L0_ffn_w_up, L0_ffn_w_down)
    x = x + _L0_attn_b_ref(_layernorm(x, axis=-1), L0_attn_b_w_qkv, L0_attn_b_b_qkv, L0_attn_b_w_out, L0_attn_b_b_out)
    x = x + _L0_ffn_ref(_layernorm(x, axis=-1), L0_ffn_gate_w, L0_ffn_w_gate, L0_ffn_w_up, L0_ffn_w_down)
    return x

_drawn_inputs = setup_inputs


def setup_inputs(seed=0):
    import zlib

    import numpy as np

    out = dict(_drawn_inputs(seed))
    spreads = {'L0_attn_a_conv_b': (0.0, 0.1),
     'L0_attn_a_dt_bias': (1.0, 0.2),
     'L0_attn_a_D_param': (1.0, 0.2),
     'L0_attn_a_norm_w': (1.0, 0.2),
     'L0_attn_b_b_qkv': (0.0, 0.1),
     'L0_attn_b_b_out': (0.0, 0.1)}
    factors = {}
    for name, (base, spread) in spreads.items():
        noise = np.random.default_rng([zlib.crc32(name.encode()), seed]).standard_normal(out[name].shape)
        drawn = base * np.exp(spread * noise) if base else spread * noise
        out[name] = jnp.asarray(drawn.astype(out[name].dtype))
    for name, factor in factors.items():
        out[name] = (out[name] * factor).astype(out[name].dtype)
    return out
```

```python
from contextlib import ExitStack

import concourse.bass as bass
from concourse import mybir

ALU = mybir.AluOpType
ACT = mybir.ActivationFunctionType
AXX = mybir.AxisListType.X
F32 = mybir.dt.float32
BF16 = mybir.dt.bfloat16
ds = bass.ds

P = 128
B, L, D = 8, 256, 256
T = B * L
NT = T // P
KD = D // P
TB = L // P
NORM_EPS = 1e-5

H, PH, N, TAPS = 32, 64, 128, 4
INTER = H * PH
CONV = INTER + 2 * N
PROJ = INTER + CONV + H
CT = CONV // P
XT = INTER // P
HG = 8
NHG = H // HG

AH, HD = 16, 16
SCALE = HD ** -0.5
NEG = -1.0e30

E, FI, TOPK = 32, 96, 8
CAP = 2 * (T * TOPK // E)
FT = E * FI // P
GT_TOK = 512
NG = T // GT_TOK
PARTS = 3


class Core:

    def __init__(self, nc, stack):
        self.nc, self.stack, self.sems = nc, stack, []

    def sb(self, name, shape, dt=F32):
        return self.stack.enter_context(self.nc.sbuf_tensor(name, shape, dt))

    def sem(self, name):
        self.sems.append(self.stack.enter_context(self.nc.semaphore(name)))
        return self.sems[-1]

    def retire(self):
        with self.nc.Block() as block:
            @block.gpsimd
            def _(pool):
                for s in self.sems:
                    pool.sem_clear(s)


def normalise(nc, tag, c, load=None):
    with ExitStack() as inner:
        ph = Core(nc, inner)
        st = ph.sb(tag + "_stats", [P, NT, 6])
        mean = ph.sb(tag + "_mean", [P, NT])
        half = ph.sb(tag + "_half", [P, NT])
        var = ph.sb(tag + "_var", [P, NT])
        rstd = ph.sb(tag + "_rstd", [P, NT])
        expo = ph.sb(tag + "_expo", [P, NT])
        xh = ph.sb(tag + "_xh", [P, 2, D])
        banks = c.bank
        v = ph.sem(tag + "_v")
        expo_set = ph.sem(tag + "_expo_set")
        rstd_ready = ph.sem(tag + "_rstd_ready")
        xh_ready = ph.sem(tag + "_xh_ready")
        turned = ph.sem(tag + "_turned")
        copied = ph.sem(tag + "_copied")
        with nc.Block() as block:
            @block.vector
            def _(dve):
                if load is not None:
                    dve.wait_ge(load, 16)
                for t in range(NT):
                    dve.bn_stats(st[:, t, :], c.x[:, t, :]).then_inc(v, 1)
                dve.wait_ge(v, NT)
                dve.tensor_tensor(mean[:, :], st[:, :, 1], st[:, :, 4], ALU.add).then_inc(v, 1)
                dve.tensor_tensor(half[:, :], st[:, :, 1], st[:, :, 4], ALU.subtract).then_inc(v, 1)
                dve.tensor_tensor(var[:, :], st[:, :, 2], st[:, :, 5], ALU.add).then_inc(v, 1)
                dve.wait_ge(v, NT + 3)
                dve.tensor_scalar(mean[:, :], mean[:, :], 0.5, None, ALU.mult).then_inc(v, 1)
                dve.scalar_tensor_tensor(half[:, :], half[:, :], 0.25, half[:, :], ALU.mult, ALU.mult).then_inc(v, 1)
                dve.tensor_scalar(var[:, :], var[:, :], 1.0 / D, NORM_EPS, ALU.mult, ALU.add).then_inc(v, 1)
                dve.wait_ge(v, NT + 6)
                dve.tensor_tensor(var[:, :], var[:, :], half[:, :], ALU.add).then_inc(v, 1)
                dve.wait_ge(rstd_ready, 1)
                with dve.Fori(0, NT // 2) as i:
                    for j in range(2):
                        dve.wait_ge(turned, 2 * i + j + 1)
                        dve.tensor_scalar(xh[:, j, :], c.x[:, ds(2 * i + j, 1), :].rearrange("p a d -> p (a d)"),
                                          mean[:, ds(2 * i + j, 1)], rstd[:, ds(2 * i + j, 1)],
                                          ALU.subtract, ALU.mult).then_inc(xh_ready, 1)

            @block.gpsimd
            def _(pool):
                pool.memset(expo[:, :], -0.5).then_inc(expo_set, 1)
                pool.wait_ge(expo_set, 1)
                pool.wait_ge(v, NT + 7)
                pool.tensor_tensor(rstd[:, :], var[:, :], expo[:, :], ALU.pow).then_inc(rstd_ready, 1)

            @block.tensor
            def _(pe):
                pe.sem_inc(turned, 2)
                with pe.Fori(0, NT // 2) as i:
                    for j in range(2):
                        pe.wait_ge(xh_ready, 2 * i + j + 1)
                        pe.wait_ge(copied, 2 * i + j + 1)
                        for k in range(KD):
                            mm = pe.transpose(banks[j][:, k * P:(k + 1) * P], xh[:, j, k * P:(k + 1) * P], c.ident[:, :])
                        mm.then_inc(turned, 1)

            @block.scalar
            def _(act):
                act.sem_inc(copied, 2)
                with act.Fori(0, NT // 2) as i:
                    for j in range(2):
                        act.wait_ge(turned, 2 * i + j + 3)
                        act.activation(c.xnT[:, :, ds((2 * i + j) * P, P)],
                                       banks[j][:, 0:D].rearrange("p (k t) -> p k t", k=KD), ACT.Copy).then_inc(copied, 1)

        ph.retire()


def mixer(nc, c, w):
    with ExitStack() as outer:
        m = Core(nc, outer)
        w_in = m.sb("w_in", [P, KD, PROJ])
        w_out = m.sb("w_out", [P, XT, D])
        nrm_w = m.sb("nrm_w", [P, XT])
        conv_w = m.sb("conv_w_sb", [P, CT, TAPS])
        conv_b = m.sb("conv_b_sb", [P, CT])
        d_row = m.sb("d_row", [P, H])
        dt_tok = m.sb("dt_tok", [P, NT, H])
        loaded_in, loaded_dt, loaded_out = m.sem("loaded_in"), m.sem("loaded_dt"), m.sem("loaded_out")
        cum_parts = nc.dram_tensor("cum_parts", [PARTS, H, T], BF16, kind="Internal").ap()
        ncum_parts = nc.dram_tensor("neg_cum_parts", [PARTS, H, T], BF16, kind="Internal").ap()

        with ExitStack() as inner:
            p = Core(nc, inner)
            banks = c.bank
            z, a, e, u, lg, dt = (p.sb("pre_" + n, [H, T]) for n in ("z", "a", "e", "u", "lg", "dt"))
            r, same = u, lg
            ones = p.sb("pre_ones", [H, L])
            dtb, alog, aneg = (p.sb("pre_" + n, [H, 1]) for n in ("dtb", "alog", "aneg"))
            part = [p.sb(f"pre_part{i}", [H, T], BF16) for i in range(PARTS)]
            npart = [p.sb(f"pre_npart{i}", [H, T], BF16) for i in range(PARTS)]
            (dt_proj, z_ready, nabs_ready, exp_ready, u_ready, ln_ready, less_ready, safe_ready, inv_ready,
             ratio_ready, tiny_ready, term_ready, sum_ready, dt_ready, a_ready, da_ready, ones_ready, cum_ready,
             part_ready, rest_ready, npart_ready, dt_turned, dt_copied, saved) = (
                p.sem("pre_" + n) for n in (
                    "dt_proj", "z", "nabs", "exp", "u", "ln", "less", "safe", "inv", "ratio", "tiny", "term", "sum",
                    "dt", "a", "da", "ones", "cum", "part", "rest", "npart", "dt_turned", "dt_copied", "saved"))
            with nc.Block() as block:
                @block.sync
                def _(sp):
                    sp.dma_start(dtb[:, :], w["dt_bias"]).then_inc(loaded_dt, 16)
                    sp.dma_start(alog[:, :], w["A_log"]).then_inc(loaded_dt, 16)
                    sp.dma_start(w_in[:, :, PROJ - H:PROJ], w["w_in"][:, :, PROJ - H:PROJ]).then_inc(loaded_dt, 16)
                    for k in range(KD):
                        sp.dma_start(w_in[:, k, 0:PROJ - H], w["w_in"][:, k, 0:PROJ - H]).then_inc(loaded_in, 16)
                    sp.dma_start(conv_w[:, :, :], w["conv_w"]).then_inc(loaded_in, 16)
                    sp.dma_start(conv_b[:, :], w["conv_b"]).then_inc(loaded_in, 16)
                    sp.dma_start(d_row[:, :], w["D"].partition_broadcast(P)).then_inc(loaded_in, 16)
                    sp.dma_start(w_out[:, :, :], w["w_out"]).then_inc(loaded_out, 16)
                    sp.dma_start(nrm_w[:, :], w["norm_w"]).then_inc(loaded_out, 16)
                    for i in range(PARTS):
                        sp.wait_ge(part_ready, i + 1)
                        sp.dma_start(cum_parts[i], part[i][:, :]).then_inc(saved, 16)
                        sp.wait_ge(npart_ready, i + 1)
                        sp.dma_start(ncum_parts[i], npart[i][:, :]).then_inc(saved, 16)
                    sp.wait_ge(saved, 32 * PARTS)

                @block.gpsimd
                def _(pool):
                    pool.memset(ones[:, :], 1.0).then_inc(ones_ready, 1)

                @block.tensor
                def _(pe):
                    pe.wait_ge(loaded_dt, 48)
                    for q in range(T // 512):
                        for k in range(KD):
                            mm = pe.matmul(banks[q][0:H, :], w_in[:, k, PROJ - H:PROJ],
                                           c.xnT[:, k, q * 512:(q + 1) * 512], start=(k == 0), stop=(k == KD - 1))
                        mm.then_inc(dt_proj, 1)
                    pe.wait_ge(dt_ready, 1)
                    for t in range(NT):
                        mm = pe.transpose(banks[7][:, t * H:(t + 1) * H], dt[:, t * P:(t + 1) * P], c.ident[0:H, 0:H])
                    mm.then_inc(dt_turned, 1)

                @block.scalar
                def _(act):
                    act.wait_ge(loaded_dt, 48)
                    act.activation(a[:, 0:1], alog[:, :], ACT.Exp).then_inc(a_ready, 1)
                    act.wait_ge(nabs_ready, 1)
                    act.activation(e[:, :], e[:, :], ACT.Exp).then_inc(exp_ready, 1)
                    act.wait_ge(u_ready, 1)
                    act.activation(lg[:, :], u[:, :], ACT.Ln).then_inc(ln_ready, 1)
                    act.wait_ge(dt_turned, 1)
                    act.activation(dt_tok[:, :, :], banks[7][:, :].rearrange("p (t h) -> p t h", h=H), ACT.Copy).then_inc(dt_copied, 1)
                    for i in range(PARTS):
                        act.wait_ge(part_ready, i + 1)
                        act.activation(npart[i][:, :], part[i][:, :], ACT.Copy, scale=-1.0).then_inc(npart_ready, 1)

                @block.vector
                def _(dve):
                    dve.wait_ge(loaded_dt, 48)
                    dve.wait_ge(a_ready, 1)
                    dve.tensor_scalar(aneg[:, :], a[:, 0:1], -1.0, None, ALU.mult).then_inc(a_ready, 1)
                    for q in range(T // 512):
                        dve.wait_ge(dt_proj, q + 1)
                        dve.tensor_scalar(z[:, q * 512:(q + 1) * 512], banks[q][0:H, :], dtb[:, 0:1], None, ALU.add).then_inc(z_ready, 1)
                    dve.wait_ge(z_ready, 4)
                    dve.scalar_tensor_tensor(e[:, :], z[:, :], -1.0, z[:, :], ALU.mult, ALU.min).then_inc(nabs_ready, 1)
                    dve.wait_ge(exp_ready, 1)
                    dve.tensor_scalar(u[:, :], e[:, :], 1.0, None, ALU.add).then_inc(u_ready, 1)
                    dve.wait_ge(ln_ready, 1)
                    dve.tensor_scalar(a[:, :], u[:, :], -1.0, None, ALU.add).then_inc(less_ready, 1)
                    dve.wait_ge(less_ready, 1)
                    dve.scalar_tensor_tensor(r[:, :], a[:, :], 0.0, a[:, :], ALU.is_equal, ALU.add).then_inc(safe_ready, 1)
                    dve.scalar_tensor_tensor(dt[:, :], a[:, :], 0.0, e[:, :], ALU.is_equal, ALU.mult).then_inc(tiny_ready, 1)
                    dve.wait_ge(safe_ready, 1)
                    dve.reciprocal(r[:, :], r[:, :]).then_inc(inv_ready, 1)
                    dve.wait_ge(inv_ready, 1)
                    dve.tensor_tensor(r[:, :], r[:, :], e[:, :], ALU.mult).then_inc(ratio_ready, 1)
                    dve.wait_ge(ratio_ready, 1)
                    dve.tensor_tensor(lg[:, :], lg[:, :], r[:, :], ALU.mult).then_inc(term_ready, 1)
                    dve.wait_ge(term_ready, 1)
                    dve.wait_ge(tiny_ready, 1)
                    dve.tensor_tensor(lg[:, :], lg[:, :], dt[:, :], ALU.add).then_inc(sum_ready, 1)
                    dve.wait_ge(sum_ready, 1)
                    dve.scalar_tensor_tensor(dt[:, :], z[:, :], 0.0, lg[:, :], ALU.max, ALU.add).then_inc(dt_ready, 1)
                    dve.wait_ge(dt_ready, 1)
                    dve.wait_ge(a_ready, 2)
                    dve.tensor_scalar(a[:, :], dt[:, :], aneg[:, 0:1], None, ALU.mult).then_inc(da_ready, 1)
                    dve.wait_ge(da_ready, 1)
                    dve.wait_ge(ones_ready, 1)
                    for b in range(B):
                        dve.tensor_tensor_scan(z[:, b * L:(b + 1) * L], ones[:, :], a[:, b * L:(b + 1) * L], 0.0,
                                               ALU.mult, ALU.add).then_inc(cum_ready, 1)
                    dve.wait_ge(cum_ready, B)
                    for i in range(PARTS):
                        dve.tensor_copy(part[i][:, :], z[:, :]).then_inc(part_ready, 1)
                        dve.wait_ge(part_ready, i + 1)
                        if i < PARTS - 1:
                            dve.tensor_tensor(z[:, :], z[:, :], part[i][:, :], ALU.subtract).then_inc(rest_ready, 1)
                            dve.wait_ge(rest_ready, i + 1)

            p.retire()

        with ExitStack() as inner:
            mixer_loop(nc, c, w_in, w_out, nrm_w, conv_w, conv_b, d_row, dt_tok, loaded_in, loaded_out,
                       cum_parts, ncum_parts, Core(nc, inner))
        m.retire()


def mixer_loop(nc, c, w_in, w_out, nrm_w, conv_w, conv_b, d_row, dt_tok, loaded_in, loaded_out, cum_parts, ncum_parts, p):
    OFF_X, OFF_B = INTER, 2 * INTER
    PAIRS = [(XT, XT + 1)] + [(2 * i, 2 * i + 1) for i in range(XT // 2)]
    NP = len(PAIRS)
    GU = TB * INTER // 512
    XU = TB * XT // 4
    EU = 3 * H // 4
    TR = EU // 3
    ES = 6

    xb = p.sb("xb", [P, KD, L])
    cv = p.sb("cv", [P, CT, L])
    stage = p.sb("stage", [P, 2, 512])
    xdt = p.sb("xdt", [P, TB, INTER])
    yg = p.sb("yg", [P, TB, INTER])
    gate = p.sb("gate", [P, TB, INTER])
    sc = p.sb("sc", [P, ES, 512])
    gsb = p.sb("gsb", [P, 3 * P])
    gT = p.sb("gT", [P, TB, XT, P])
    lrow = p.sb("lrow", [2 * PARTS, 2, HG, L], BF16)
    rrow = p.sb("rrow", [2 * PARTS, 2, HG, L], BF16)
    ssp = p.sb("ssp", [P, TB, NHG])
    junk = p.sb("junk", [P, TB, 512], BF16)
    ms = p.sb("ms", [P, TB])
    rs = p.sb("rs", [P, TB])
    expo = p.sb("m_expo", [P, TB])
    bank = c.bank

    sem = p.sem
    w_scaled = sem("w_out_scaled")
    consts = sem("mx_consts")
    xb_ready, pair_ready, tap_done, tap_dve = sem("xb_ready"), sem("pair_ready"), sem("tap_done"), sem("tap_dve")
    conv_done, silu_done = sem("conv_done"), sem("silu_done")
    gate_ready, gate_done = sem("gate_ready"), sem("gate_done")
    g_ready, g_done = sem("g_ready"), sem("g_done")
    xturn_ready, xturn_done = sem("xturn_ready"), sem("xturn_done")
    turn_ready, turn_done = sem("turn_ready"), sem("turn_done")
    xdt_done, dx_done = sem("xdt_done"), sem("dx_done")
    rows = [sem("rows0"), sem("rows1")]
    e_ready, exp_done, m_done, y_done, y_added = sem("e_ready"), sem("exp_done"), sem("m_done"), sem("y_done"), sem("y_added")
    gated, squared = sem("gated"), sem("squared")
    out_ready, x_added = sem("out_ready"), sem("x_added")
    ss_ready, ms_ready, rs_ready = sem("ss_ready"), sem("ms_ready"), sem("rs_ready")
    GR, GD, XT_D, TD, XD, ER, XP, YD, YA, OR, XA, SQ = 1, 1, 1, 2, 2, 12, 2, 2, 1, 2, 1, 2

    with nc.Block() as block:
        @block.sync
        def _(sp):
            with sp.Fori(0, B) as b:
                for g in range(NHG):
                    sp.wait_ge(consts, 3)
                    sp.wait_ge(e_ready, EU * b + 6 * g - 6 + ER)
                    sp.dma_start(rrow[0:2 * PARTS:2, g % 2, :, :],
                                 cum_parts[:, g * HG:(g + 1) * HG, ds(b * L, L)]).then_inc(rows[g % 2], 16)
                    sp.dma_start(lrow[1:2 * PARTS:2, g % 2, :, :],
                                 ncum_parts[:, g * HG:(g + 1) * HG, ds(b * L, L)]).then_inc(rows[g % 2], 16)

        @block.tensor
        def _(pe):
            pe.sem_inc(gate_ready, GR)
            pe.sem_inc(e_ready, ER)
            pe.sem_inc(y_done, YD)
            pe.sem_inc(out_ready, OR)
            pe.wait_ge(loaded_in, 16 * (KD + 3))
            with pe.Fori(0, B) as b:
                for u, pr in enumerate(PAIRS):
                    if u < 2:
                        pe.wait_ge(xturn_done, XU * b + XT_D)
                    else:
                        pe.wait_ge(conv_done, NP * b + u - 1)
                    for j, ch in enumerate(pr):
                        for k in range(KD):
                            o = OFF_X + ch * P
                            mm = pe.matmul(bank[u % 2][:, j * L:(j + 1) * L], w_in[:, k, o:o + P],
                                           c.xnT[:, k, ds(b * L, L)], start=(k == 0), stop=(k == KD - 1))
                    mm.then_inc(pair_ready, 1)
                pe.wait_ge(silu_done, NP * b + 1)
                pe.wait_ge(turn_done, XU * b + TD)
                pe.matmul(bank[6][:, 0:L], cv[:, XT, 0:P], cv[:, XT + 1, :], start=True, stop=True)
                pe.matmul(bank[6][:, L:L + P], cv[:, XT, P:L], cv[:, XT + 1, P:L], start=True, stop=True).then_inc(g_ready, 1)
                pe.wait_ge(xb_ready, b + 1)
                for g in range(GU):
                    t, n = divmod(g, GU // TB)
                    u = NP + g
                    if g < 2:
                        pe.wait_ge(conv_done, NP * b + u - 1)
                    else:
                        pe.wait_ge(gate_done, GU * b + g - 1 + GD)
                    for k in range(KD):
                        mm = pe.matmul(bank[u % 2][:, :], xb[:, k, t * P:(t + 1) * P],
                                       w_in[:, k, n * 512:(n + 1) * 512], start=(k == 0), stop=(k == KD - 1))
                    mm.then_inc(gate_ready, 1)
                for v in range(XU):
                    t, q = divmod(v, XU // TB)
                    u = NP + GU + v
                    pe.wait_ge(silu_done, NP * b + 2 * q + 3)
                    if v < 2:
                        pe.wait_ge(gate_done, GU * b + GU - 1 + v + GD)
                    else:
                        pe.wait_ge(xturn_done, XU * b + v - 1 + XT_D)
                    for j in range(4):
                        mm = pe.transpose(bank[u % 2][:, j * P:(j + 1) * P], cv[:, 4 * q + j, t * P:(t + 1) * P], c.ident[:, :])
                    mm.then_inc(xturn_ready, 1)

                def scores(tr):
                    g, first = tr // 2, 4 * (tr % 2)
                    if tr % 2 == 0:
                        pe.wait_ge(rows[g % 2], 64 * b + 32 * (g // 2 + 1))
                    for n in range(3):
                        u = 3 * tr + n
                        pe.wait_ge(exp_done, EU * b + u - 1 + XP)
                        cols = bank[2 + u % 2][:, :].rearrange("p (j l) -> p j l", l=(L if n < 2 else P))[:, :, 0:P]
                        nj = 2 if n < 2 else 4
                        pe.matmul(cols, c.identb[:, :], c.before[:, :].unsqueeze(1).broadcast_to([P, nj, P]),
                                  start=True, stop=False, skip_group_check=True)
                        if n < 2:
                            for j in range(2):
                                h = first + 2 * n + j
                                mm = pe.matmul(bank[2 + u % 2][:, j * L:(j + 1) * L], lrow[:, g % 2, h, 0:P],
                                               rrow[:, g % 2, h, :], start=False, stop=True, skip_group_check=True)
                        else:
                            for j in range(4):
                                h = first + j
                                mm = pe.matmul(bank[2 + u % 2][:, j * P:(j + 1) * P], lrow[:, g % 2, h, P:L],
                                               rrow[:, g % 2, h, P:L], start=False, stop=True, skip_group_check=True)
                        mm.then_inc(e_ready, 1)

                def outputs(tr):
                    g, first = tr // 2, 4 * (tr % 2)
                    if tr % 2 == 0:
                        pe.wait_ge(y_added, NHG * b + g + YA)
                    if tr == 0:
                        pe.wait_ge(x_added, TB * b + XA)
                    if tr == 0:
                        pe.wait_ge(xdt_done, XU * (b + 1) + XD)
                    pe.wait_ge(m_done, EU * b + 3 * (tr + 1))
                    base = 3 * (tr % 2)
                    for j in range(4):
                        col = (first + j) * PH
                        ch = g * 512 + col
                        early = sc[:, base + j // 2, (j % 2) * L:(j % 2 + 1) * L]
                        late = sc[:, base + 2, j * P:(j + 1) * P]
                        pe.matmul(bank[4][:, col:col + PH], early[:, 0:P], xdt[:, 0, ch:ch + PH], start=True, stop=True)
                        pe.matmul(bank[5][:, col:col + PH], early[:, P:L], xdt[:, 0, ch:ch + PH], start=True, stop=False)
                        mm = pe.matmul(bank[5][:, col:col + PH], late, xdt[:, 1, ch:ch + PH], start=False, stop=True)
                    mm.then_inc(y_done, 1)

                scores(0)
                for tr in range(TR):
                    if tr + 1 < TR:
                        scores(tr + 1)
                    outputs(tr)
                pe.wait_ge(w_scaled, 1)
                pe.wait_ge(g_done, b + 1)
                for t in range(TB):
                    for q in range(NHG):
                        v = t * NHG + q
                        pe.wait_ge(gated, TB * NHG * b + 2 * q + t + 1)
                        pe.wait_ge(turn_done, XU * b + v - 1 + TD)
                        for j in range(4):
                            ch = 4 * q + j
                            mm = pe.transpose(bank[6 + v % 2][:, j * P:(j + 1) * P], yg[:, t, ch * P:(ch + 1) * P], c.ident[:, :])
                        mm.then_inc(turn_ready, 1)
                pe.wait_ge(y_added, NHG * (b + 1) + YA)
                for t in range(TB):
                    pe.wait_ge(turn_done, XU * b + (t + 1) * NHG + TD)
                    for ch in range(XT):
                        mm = pe.matmul(bank[4 + t][:, 0:D], gT[:, t, ch, :], w_out[:, ch, :],
                                       start=(ch == 0), stop=(ch == XT - 1))
                    mm.then_inc(out_ready, 1)

        @block.scalar
        def _(act):
            act.sem_inc(gate_done, GD)
            act.sem_inc(xturn_done, XT_D)
            act.sem_inc(turn_done, TD)
            act.sem_inc(exp_done, XP)
            act.sem_inc(squared, SQ)
            act.wait_ge(loaded_in, 16 * (KD + 3))
            with act.Fori(0, B) as b:
                for u, pr in enumerate(PAIRS + [None]):
                    if pr is not None:
                        act.wait_ge(pair_ready, NP * b + u + 1)
                        for j, ch in enumerate(pr):
                            ins = act.activation(cv[:, ch, :], bank[u % 2][:, j * L:(j + 1) * L], ACT.Identity,
                                                 bias=conv_b[:, ch:ch + 1], scale=conv_w[:, ch, TAPS - 1:TAPS])
                        ins.then_inc(tap_done, 1)
                    if u >= 1:
                        q = PAIRS[u - 1]
                        act.wait_ge(conv_done, NP * b + u)
                        act.activation(cv[:, q[0]:q[1] + 1, :], cv[:, q[0]:q[1] + 1, :], ACT.Silu).then_inc(silu_done, 1)
                for g in range(GU):
                    t, n = divmod(g, GU // TB)
                    act.wait_ge(gate_ready, GU * b + g + 1 + GR)
                    act.activation(gate[:, t, n * 512:(n + 1) * 512], bank[(NP + g) % 2][:, :], ACT.Silu).then_inc(gate_done, 1)
                for v in range(XU):
                    act.wait_ge(xturn_ready, XU * b + v + 1)
                    act.wait_ge(xdt_done, XU * b + v - 1 + XD)
                    act.activation(stage[:, v % 2, :], bank[(NP + GU + v) % 2][:, :], ACT.Copy).then_inc(xturn_done, 1)

                def squares(g):
                    for t in range(TB):
                        act.wait_ge(gated, 2 * NHG * b + 2 * g + t + 1)
                        act.wait_ge(squared, TB * NHG * b + 2 * g + t - 1 + SQ)
                        act.activation(junk[:, t, :], yg[:, t, g * 512:(g + 1) * 512], ACT.Square,
                                       accum_out=ssp[:, t, g:g + 1]).then_inc(squared, 1)

                for u in range(EU):
                    act.wait_ge(e_ready, EU * b + u + 1 + ER)
                    if u % 3 == 0:
                        act.wait_ge(y_done, TR * b + u // 3 - 1 + YD)
                    act.activation(sc[:, u % ES, :], bank[2 + u % 2][:, :], ACT.Exp).then_inc(exp_done, 1)
                    if u % 6 == 5 and u >= 11:
                        squares(u // 6 - 1)
                squares(NHG - 1)
                for v in range(XU):
                    t, q = divmod(v, NHG)
                    act.wait_ge(turn_ready, XU * b + v + 1)
                    if q == 0:
                        act.wait_ge(out_ready, TB * b + t - 1 + OR)
                    act.activation(gT[:, t, 4 * q:4 * q + 4, :], bank[6 + v % 2][:, :].rearrange("p (a t) -> p a t", a=4),
                                   ACT.Copy).then_inc(turn_done, 1)

        @block.gpsimd
        def _(pool):
            pool.memset(lrow[:, :, :, :], 1.0).then_inc(consts, 1)
            pool.memset(rrow[:, :, :, :], 1.0).then_inc(consts, 1)
            pool.memset(expo[:, :], -0.5).then_inc(consts, 1)
            pool.sem_inc(xdt_done, XD)
            pool.wait_ge(loaded_out, 32)
            pool.tensor_tensor(w_out[:, :, :], w_out[:, :, :], nrm_w[:, :].unsqueeze(2).broadcast_to([P, XT, D]), ALU.mult)\
                .then_inc(w_scaled, 1)
            pool.wait_ge(consts, 3)
            pool.wait_ge(loaded_in, 16 * (KD + 3))
            with pool.Fori(0, B) as b:
                pool.wait_ge(gate_ready, GU * b + GR)
                pool.tensor_copy(xb[:, :, :], c.xnT[:, :, ds(b * L, L)]).then_inc(xb_ready, 1)
                for v in range(XU):
                    t, q = divmod(v, XU // TB)
                    if v == 0:
                        pool.wait_ge(y_done, TR * b + YD)
                        pool.wait_ge(out_ready, TB * b + OR)
                    pool.wait_ge(xturn_done, XU * b + v + 1 + XT_D)
                    src = stage[:, v % 2, :].rearrange("p (h d) -> p h d", d=PH)
                    hs, cs = slice(HG * q, HG * q + HG), slice(q * 512, (q + 1) * 512)
                    pool.tensor_tensor(yg[:, t, cs].rearrange("p (h d) -> p h d", d=PH), src,
                                       d_row[:, hs].unsqueeze(2).broadcast_to([P, HG, PH]), ALU.mult).then_inc(dx_done, 1)
                    pool.tensor_tensor(xdt[:, t, cs].rearrange("p (h d) -> p h d", d=PH), src,
                                       dt_tok[:, ds(TB * b + t, 1), hs].rearrange("p a h -> p (a h)").unsqueeze(2).broadcast_to([P, HG, PH]),
                                       ALU.mult).then_inc(xdt_done, 1)
                for g in range(NHG):
                    pool.wait_ge(y_added, NHG * b + g + 1 + YA)
                    pool.wait_ge(gate_done, GU * (b + 1) + GD)
                    for t in range(TB):
                        part = slice(g * 512, (g + 1) * 512)
                        pool.tensor_tensor(yg[:, t, part], yg[:, t, part], gate[:, t, part], ALU.mult).then_inc(gated, 1)
                pool.wait_ge(ms_ready, b + 1)
                pool.tensor_tensor(rs[:, :], ms[:, :], expo[:, :], ALU.pow).then_inc(rs_ready, 1)

        @block.vector
        def _(dve):
            dve.sem_inc(y_added, YA)
            dve.sem_inc(x_added, XA)
            with dve.Fori(0, B) as b:
                for u, pr in enumerate(PAIRS):
                    dve.wait_ge(tap_done, NP * b + u + 1)
                    for k in range(TAPS - 1):
                        back = k + 1
                        if k:
                            dve.wait_ge(tap_dve, 2 * (NP * b + u) + k)
                        for j, ch in enumerate(pr):
                            ins = dve.scalar_tensor_tensor(
                                cv[:, ch, back:L], bank[u % 2][:, j * L:(j + 1) * L - back],
                                conv_w[:, ch, TAPS - 1 - back:TAPS - back], cv[:, ch, back:L], ALU.mult, ALU.add)
                        ins.then_inc(tap_dve if k < TAPS - 2 else conv_done, 1)
                dve.wait_ge(g_ready, b + 1)
                dve.tensor_copy(gsb[:, :], bank[6][:, 0:3 * P]).then_inc(g_done, 1)

                def masked(u):
                    dve.wait_ge(exp_done, EU * b + u + 1 + XP)
                    if u % 3 < 2:
                        s = sc[:, u % ES, :].rearrange("p (h l) -> p h l", h=2)
                        gm = gsb[:, 0:L].unsqueeze(1).broadcast_to([P, 2, L])
                    else:
                        s = sc[:, u % ES, :].rearrange("p (h l) -> p h l", h=4)
                        gm = gsb[:, L:L + P].unsqueeze(1).broadcast_to([P, 4, P])
                    dve.tensor_tensor(s, s, gm, ALU.mult).then_inc(m_done, 1)

                def add_y(g):
                    dve.wait_ge(y_done, TR * b + 2 * (g + 1) + YD)
                    dve.wait_ge(dx_done, XU * (b + 1))
                    for t in range(TB):
                        part = yg[:, t, g * 512:(g + 1) * 512]
                        ins = dve.tensor_tensor(part, part, bank[4 + t][:, :], ALU.add)
                    ins.then_inc(y_added, 1)

                dve.wait_ge(g_done, b + 1)
                for u in range(EU):
                    masked(u)
                    if u % 6 == 2 and u > 6:
                        add_y(u // 6 - 1)
                add_y(NHG - 1)
                dve.wait_ge(squared, TB * NHG * (b + 1) + SQ)
                dve.reduce_sum(ms[:, :], ssp[:, :, :], axis=AXX).then_inc(ss_ready, 1)
                dve.wait_ge(ss_ready, b + 1)
                dve.tensor_scalar(ms[:, :], ms[:, :], 1.0 / INTER, NORM_EPS, ALU.mult, ALU.add).then_inc(ms_ready, 1)
                dve.wait_ge(rs_ready, b + 1)
                for t in range(TB):
                    dve.wait_ge(out_ready, TB * b + t + 1 + OR)
                    xt = c.x[:, ds(TB * b + t, 1), :].rearrange("p a d -> p (a d)")
                    ins = dve.scalar_tensor_tensor(xt, bank[4 + t][:, 0:D], rs[:, t:t + 1], xt, ALU.mult, ALU.add)
                    ins.then_inc(x_added, 1)
    p.retire()


def route(nc, c, tag, wT, w_router, loaded):
    with ExitStack() as inner:
        p = Core(nc, inner)
        sb, sem = (lambda n, *r: p.sb(f"{tag}_{n}", *r)), (lambda n: p.sem(f"{tag}_r_{n}"))
        bank = c.bank
        lgT = sb("lgT", [E, T])
        lg = sb("lg", [P, NT, E])
        top, tot, inv = sb("top", [P, NT]), sb("tot", [P, NT]), sb("inv", [P, NT])
        best, rest, pick = sb("best", [P, NT, TOPK]), sb("rest", [P, NT, E]), sb("pick", [P, NT, E])
        pickb = sb("pickb", [P, NT, E], BF16)
        parts, partsf = sb("parts", [P, NT, PARTS, E], BF16), sb("partsf", [P, NT, PARTS, E])
        (lg_ready, lgT_ready, turned, max_ready, sub_ready, exp_ready, sum_ready, inv_ready, prob_ready, best_ready,
         rest_ready, pick_ready, pickb_ready, wsum_ready, winv_ready, w_ready, pos_ready, kept_ready, part_ready,
         left_ready, wide_ready, w_turned, done) = (sem(n) for n in (
             "lg", "lgT", "turned", "max", "sub", "exp", "sum", "inv", "prob", "best", "rest", "pick", "pickb",
             "wsum", "winv", "w", "pos", "kept", "part", "left", "wide", "w_turned", "done"))
        wide = lambda t2: t2[:, :].unsqueeze(2).broadcast_to([P, NT, E])
        with nc.Block() as block:
            @block.tensor
            def _(pe):
                pe.wait_ge(loaded, 16)
                for q in range(T // 512):
                    for k in range(KD):
                        mm = pe.matmul(bank[q][0:E, :], w_router[:, k, :], c.xnT[:, k, q * 512:(q + 1) * 512],
                                       start=(k == 0), stop=(k == KD - 1))
                    mm.then_inc(lg_ready, 1)
                for t in range(NT):
                    if t % 4 == 0:
                        pe.wait_ge(lgT_ready, t // 4 + 1)
                    mm = pe.transpose(bank[4][:, t * E:(t + 1) * E], lgT[:, t * P:(t + 1) * P], c.ident[0:E, 0:E])
                mm.then_inc(turned, 1)
                pe.wait_ge(pickb_ready, 1)
                pe.matmul(bank[5][:, :], c.earlier[:, :], pickb[:, :, :], start=True, stop=True)
                for t in range(NT - 1):
                    mm = pe.matmul(bank[5][:, (t + 1) * E:], c.onesb[:, :],
                                   pickb[:, t:t + 1, :].broadcast_to([P, NT - 1 - t, E]),
                                   start=False, stop=True, skip_group_check=True)
                mm.then_inc(pos_ready, 1)
                pe.wait_ge(wide_ready, 1)
                for t in range(NT):
                    mm = pe.transpose(bank[t // 4][0:PARTS * E, (t % 4) * P:(t % 4 + 1) * P],
                                      partsf[:, t, :, :].rearrange("p i e -> p (i e)"), c.ident[:, :])
                    if t % 4 == 3:
                        mm.then_inc(w_turned, 1)

            @block.scalar
            def _(act):
                for q in range(T // 512):
                    act.wait_ge(lg_ready, q + 1)
                    act.activation(lgT[:, q * 512:(q + 1) * 512], bank[q][0:E, :], ACT.Copy).then_inc(lgT_ready, 1)
                act.wait_ge(sub_ready, 1)
                act.activation(lg[:, :, :], lg[:, :, :], ACT.Exp).then_inc(exp_ready, 1)
                act.wait_ge(part_ready, PARTS)
                act.activation(partsf[:, :, :, :], parts[:, :, :, :], ACT.Copy).then_inc(wide_ready, 1)
                for q in range(4):
                    act.wait_ge(w_turned, q + 1)
                    act.activation(wT[:, q * 512:(q + 1) * 512], bank[q][0:PARTS * E, :], ACT.Copy).then_inc(done, 1)

            @block.vector
            def _(dve):
                logits = bank[4][:, :].rearrange("p (t e) -> p t e", e=E)
                dve.wait_ge(turned, 1)
                dve.reduce_max(top[:, :], logits, axis=AXX).then_inc(max_ready, 1)
                dve.wait_ge(max_ready, 1)
                dve.tensor_tensor(lg[:, :, :], logits, wide(top), ALU.subtract).then_inc(sub_ready, 1)
                dve.wait_ge(exp_ready, 1)
                dve.reduce_sum(tot[:, :], lg[:, :, :], axis=AXX).then_inc(sum_ready, 1)
                dve.wait_ge(sum_ready, 1)
                dve.reciprocal(inv[:, :], tot[:, :]).then_inc(inv_ready, 1)
                dve.wait_ge(inv_ready, 1)
                dve.tensor_tensor(lg[:, :, :], lg[:, :, :], wide(inv), ALU.mult).then_inc(prob_ready, 1)
                dve.wait_ge(prob_ready, 1)
                for t in range(NT):
                    dve.max(best[:, t, :], lg[:, t, :]).then_inc(best_ready, 1)
                for t in range(NT):
                    dve.wait_ge(best_ready, t + 1)
                    dve.match_replace(out=rest[:, t, :], in_to_replace=best[:, t, :], in_values=lg[:, t, :], imm_value=-1.0).then_inc(rest_ready, 1)
                dve.wait_ge(rest_ready, NT)
                dve.tensor_scalar(pickb[:, :, :], rest[:, :, :], 0.0, None, ALU.is_lt).then_inc(pickb_ready, 1)
                dve.tensor_scalar(pick[:, :, :], rest[:, :, :], 0.0, None, ALU.is_lt).then_inc(pick_ready, 1)
                dve.reduce_sum(tot[:, :], best[:, :, :], axis=AXX).then_inc(wsum_ready, 1)
                dve.wait_ge(wsum_ready, 1)
                dve.reciprocal(inv[:, :], tot[:, :]).then_inc(winv_ready, 1)
                dve.wait_ge(winv_ready, 1)
                dve.wait_ge(pick_ready, 1)
                dve.tensor_tensor(lg[:, :, :], lg[:, :, :], wide(inv), ALU.mult).then_inc(w_ready, 1)
                dve.wait_ge(w_ready, 1)
                dve.tensor_tensor(lg[:, :, :], lg[:, :, :], pick[:, :, :], ALU.mult).then_inc(w_ready, 1)
                dve.wait_ge(w_ready, 2)
                dve.wait_ge(pos_ready, 1)
                dve.scalar_tensor_tensor(lg[:, :, :], bank[5][:, :].rearrange("p (t e) -> p t e", e=E), float(CAP),
                                         lg[:, :, :], ALU.is_lt, ALU.mult).then_inc(kept_ready, 1)
                dve.wait_ge(kept_ready, 1)
                for i in range(PARTS):
                    dve.tensor_copy(parts[:, :, i, :], lg[:, :, :]).then_inc(part_ready, 1)
                    if i < PARTS - 1:
                        dve.wait_ge(part_ready, i + 1)
                        dve.tensor_tensor(lg[:, :, :], lg[:, :, :], parts[:, :, i, :], ALU.subtract).then_inc(left_ready, 1)
                        dve.wait_ge(left_ready, i + 1)
        p.retire()


def experts(nc, c, tag, w_gate, w_up, w_down, w_router, loaded_router, loaded_experts):
    with ExitStack() as inner:
        p = Core(nc, inner)
        wT = p.sb(tag + "_wT", [PARTS * E, T], BF16)
        route(nc, c, tag, wT, w_router, loaded_router)
        bank = c.bank
        NS = 3
        act_g = p.sb(tag + "_act", [P, NS, GT_TOK])
        hid = p.sb(tag + "_hid", [P, NS, GT_TOK])
        (gate_ready, up_ready, wide_ready, silu_done, prod_done, hid_done, hid_used, y_ready, x_added) = (
            p.sem(f"{tag}_{n}") for n in ("gate", "up", "wide", "silu", "prod", "hid", "hid_used", "y", "x_added"))
        SD, PD, HD_, HU, XA = 2, 2, 2, NS, 1
        with nc.Block() as block:
            @block.tensor
            def _(pe):
                pe.sem_inc(hid_used, HU)
                pe.wait_ge(loaded_experts, 64)
                with pe.Fori(0, NG) as g:
                    def up(j):
                        pe.wait_ge(silu_done, FT * g + j - 1 + SD)
                        for k in range(KD):
                            mm = pe.matmul(bank[j % 2][:, :], w_gate[:, k, j * P:(j + 1) * P],
                                           c.xnT[:, k, ds(g * GT_TOK, GT_TOK)], start=(k == 0), stop=(k == KD - 1))
                        mm.then_inc(gate_ready, 1)
                        pe.wait_ge(prod_done, FT * g + j - 1 + PD)
                        for k in range(KD):
                            mm = pe.matmul(bank[2 + j % 2][:, :], w_up[:, k, j * P:(j + 1) * P],
                                           c.xnT[:, k, ds(g * GT_TOK, GT_TOK)], start=(k == 0), stop=(k == KD - 1))
                        mm.then_inc(up_ready, 1)
                        pe.wait_ge(hid_done, FT * g + j - 1 + HD_)
                        pe.matmul(bank[4 + j % 2][:, :], c.spread[:, j * P:(j + 1) * P], wT[:, ds(g * GT_TOK, GT_TOK)],
                                  start=True, stop=True).then_inc(wide_ready, 1)

                    def down(j):
                        if j == 0:
                            pe.wait_ge(x_added, g + XA)
                        pe.wait_ge(hid_done, FT * g + j + 1 + HD_)
                        for t in range(GT_TOK // P):
                            mm = pe.matmul(bank[6 + t // 2][:, (t % 2) * D:(t % 2 + 1) * D], hid[:, j % NS, t * P:(t + 1) * P],
                                           w_down[:, j, :], start=(j == 0 and t % 2 == 0), stop=(j == FT - 1),
                                           skip_group_check=True)
                        mm.then_inc(hid_used, 1)

                    up(0)
                    for j in range(FT):
                        if j + 1 < FT:
                            up(j + 1)
                        down(j)

            @block.scalar
            def _(act):
                act.sem_inc(silu_done, SD)
                with act.Fori(0, NG) as g:
                    for j in range(FT):
                        act.wait_ge(gate_ready, FT * g + j + 1)
                        act.wait_ge(hid_used, FT * g + j - NS + 1 + HU)
                        act.activation(act_g[:, j % NS, :], bank[j % 2][:, :], ACT.Silu).then_inc(silu_done, 1)

            @block.vector
            def _(dve):
                dve.sem_inc(prod_done, PD)
                dve.sem_inc(hid_done, HD_)
                dve.sem_inc(x_added, XA)
                with dve.Fori(0, NG) as g:
                    def product(j):
                        dve.wait_ge(silu_done, FT * g + j + 1 + SD)
                        dve.wait_ge(up_ready, FT * g + j + 1)
                        dve.tensor_tensor(act_g[:, j % NS, :], act_g[:, j % NS, :], bank[2 + j % 2][:, :], ALU.mult).then_inc(prod_done, 1)

                    def weigh(j):
                        dve.wait_ge(prod_done, FT * g + j + 1 + PD)
                        dve.wait_ge(wide_ready, FT * g + j + 1)
                        dve.wait_ge(hid_used, FT * g + j - NS + 1 + HU)
                        dve.tensor_tensor(hid[:, j % NS, :], act_g[:, j % NS, :], bank[4 + j % 2][:, :], ALU.mult).then_inc(hid_done, 1)

                    for j in range(FT):
                        product(j)
                        weigh(j)
                    dve.wait_ge(hid_used, FT * (g + 1) + HU)
                    for t in range(GT_TOK // P):
                        xt = c.x[:, ds(GT_TOK // P * g + t, 1), :].rearrange("p a d -> p (a d)")
                        ins = dve.tensor_tensor(xt, xt, bank[6 + t // 2][:, (t % 2) * D:(t % 2 + 1) * D], ALU.add)
                    ins.then_inc(x_added, 1)
        p.retire()


def attention(nc, c, w):
    with ExitStack() as inner:
        p = Core(nc, inner)
        sb, sem = (lambda n, *r: p.sb("at_" + n, *r)), (lambda n: p.sem("at_" + n))
        wqk, wv, wo = sb("wqk", [P, KD, 2 * D]), sb("wv", [P, KD, D]), sb("wo", [P, KD, D])
        bqk, bv, bo = sb("bqk", [P, 4]), sb("bv", [1, D]), sb("bo", [1, D])
        rmask = sb("rmask", [P, 8])
        ones = sb("ones", [1, P])
        xb = sb("xb", [P, KD, L])
        q_sb, k_sb = sb("q", [P, 2, L]), sb("k", [P, 2, L])
        kz = sb("kz", [P, 2, 8, L])
        v_sb = sb("v", [P, TB, D])
        NU = 12
        UNITS = [(0, 4 * i, 4) for i in range(4)] + [(1, 2 * i, 2) for i in range(8)]
        NPS = 3
        pr = sb("probs", [P, NPS, 512])
        pT = sb("probsT", [P, NPS, 512])
        mx, nb = sb("mx", [P, TB, AH]), sb("nb", [P, TB, AH])
        den, rden = sb("den", [P, TB, AH]), sb("rden", [P, TB, AH])
        y, yT = sb("y", [P, TB, D]), sb("yT", [P, KD, L])
        bank = c.bank
        loaded = sem("loaded")
        (ones_ready, xb_ready, qk_ready, qk_done, kz_done, v_ready, v_done, s_ready, max_done, nb_done, exp_done,
         pT_ready, pT_done, y_ready, inv_done, y_done, yT_ready, yT_done, out_ready, x_added) = (sem(n) for n in (
             "ones", "xb", "qk", "qk_done", "kz", "v_ready", "v_done", "s", "max", "nb", "exp",
             "pT_ready", "pT_done", "y_ready", "inv", "y_done", "yT_ready", "yT_done", "out", "x_added"))
        OUT, XA, PTD, PTR, ED, YD, SR, QK, VR, YR = 1, 1, 2, 3, 2, 1, 1, 1, 1, 3
        with nc.Block() as block:
            @block.sync
            def _(sp):
                for dst, n in ((wqk, "wqk"), (wv, "wv"), (wo, "wo"), (bqk, "bqk"), (bv, "bv"), (bo, "bo"), (rmask, "rmask")):
                    sp.dma_start(dst[:], w[n]).then_inc(loaded, 16)

            @block.gpsimd
            def _(pool):
                pool.memset(ones[:, :], 1.0).then_inc(ones_ready, 1)
                pool.wait_ge(loaded, 112)
                with pool.Fori(0, B) as b:
                    pool.wait_ge(v_ready, TB * b + VR)
                    pool.tensor_copy(xb[:, :, :], c.xnT[:, :, ds(b * L, L)]).then_inc(xb_ready, 1)
                    pool.wait_ge(qk_done, 2 * b + 2)
                    pool.wait_ge(s_ready, NU * b + SR)
                    for i in range(2):
                        pool.tensor_tensor(kz[:, i, :, :], k_sb[:, i:i + 1, :].broadcast_to([P, 8, L]),
                                           rmask[:, :].unsqueeze(2).broadcast_to([P, 8, L]), ALU.mult).then_inc(kz_done, 1)

            @block.tensor
            def _(pe):
                pe.sem_inc(v_ready, VR)
                pe.sem_inc(s_ready, SR)
                pe.sem_inc(out_ready, OUT)
                pe.sem_inc(y_ready, YR)
                pe.wait_ge(loaded, 112)
                pe.wait_ge(ones_ready, 1)
                with pe.Fori(0, B) as b:
                    for i in range(2):
                        pe.wait_ge(x_added, TB * b + XA)
                        for j in range(2):
                            for k in range(KD):
                                mm = pe.matmul(bank[i][:, j * L:(j + 1) * L], wqk[:, k, (2 * i + j) * P:(2 * i + j + 1) * P],
                                               c.xnT[:, k, ds(b * L, L)], start=(k == 0), stop=(k == KD - 1))
                        mm.then_inc(qk_ready, 1)
                    pe.wait_ge(xb_ready, b + 1)
                    for t in range(TB):
                        pe.wait_ge(qk_done, 2 * b + t + 1)
                        pe.matmul(bank[t][:, 0:D], ones[:, :], bv[:, :], start=True, stop=False)
                        for k in range(KD):
                            mm = pe.matmul(bank[t][:, 0:D], xb[:, k, t * P:(t + 1) * P], wv[:, k, :], start=False, stop=(k == KD - 1))
                        mm.then_inc(v_ready, 1)
                    pe.wait_ge(kz_done, 2 * b + 2)

                    def scores(u):
                        t, h, n = UNITS[u]
                        w_ = (t + 1) * P
                        pe.wait_ge(exp_done, NU * b + u - 1 + ED)
                        bk = bank[2 + u % 2]
                        pe.matmul(bk[:, :], q_sb[:, h // 8, t * P:(t + 1) * P], kz[:, h // 8, h % 8:h % 8 + n, 0:w_],
                                  start=True, stop=True, skip_group_check=True)
                        diag = bk[:, :].rearrange("p (j l) -> p j l", l=w_)[:, :, t * P:w_]
                        pe.matmul(diag, c.identb[:, :], c.after[:, :].unsqueeze(1).broadcast_to([P, n, P]),
                                  start=False, stop=True, skip_group_check=True).then_inc(s_ready, 1)

                    def turn(u):
                        pe.wait_ge(exp_done, NU * b + u + 1 + ED)
                        pe.wait_ge(pT_done, NU * b + u - 1 + PTD)
                        for j in range(4):
                            mm = pe.transpose(bank[4 + u % 2][:, j * P:(j + 1) * P], pr[:, u % NPS, j * P:(j + 1) * P], c.ident[:, :])
                        mm.then_inc(pT_ready, 1)

                    def values(u):
                        t, h, n = UNITS[u]
                        if u == 0:
                            pe.wait_ge(v_done, TB * (b + 1))
                        if u in (0, 4):
                            pe.wait_ge(y_done, TB * b + t + YD)
                        pe.wait_ge(pT_done, NU * b + u + 1 + PTD)
                        for j in range(n):
                            o = bank[6][:, (h + j) * HD:(h + j + 1) * HD]
                            for s in range(t + 1):
                                mm = pe.matmul(o, pT[:, u % NPS, (j * (t + 1) + s) * P:(j * (t + 1) + s + 1) * P],
                                               v_sb[:, s, (h + j) * HD:(h + j + 1) * HD], start=(s == 0), stop=(s == t))
                        mm.then_inc(y_ready, 1)

                    scores(0)
                    scores(1)
                    for u in range(NU):
                        turn(u)
                        if u + 2 < NU:
                            scores(u + 2)
                        if u >= 1:
                            values(u - 1)
                    values(NU - 1)
                    for t in range(TB):
                        pe.wait_ge(y_done, TB * b + t + 1 + YD)
                        for k in range(KD):
                            mm = pe.transpose(bank[7][:, (2 * t + k) * P:(2 * t + k + 1) * P], y[:, t, k * P:(k + 1) * P], c.ident[:, :])
                    mm.then_inc(yT_ready, 1)
                    pe.wait_ge(yT_done, b + 1)
                    for t in range(TB):
                        pe.wait_ge(v_done, TB * (b + 1))
                        pe.matmul(bank[t][:, 0:D], ones[:, :], bo[:, :], start=True, stop=False)
                        for k in range(KD):
                            mm = pe.matmul(bank[t][:, 0:D], yT[:, k, t * P:(t + 1) * P], wo[:, k, :], start=False, stop=(k == KD - 1))
                        mm.then_inc(out_ready, 1)

            @block.scalar
            def _(act):
                act.sem_inc(exp_done, ED)
                act.wait_ge(loaded, 112)
                with act.Fori(0, B) as b:
                    for i, dst in enumerate((q_sb, k_sb)):
                        act.wait_ge(qk_ready, 2 * b + i + 1)
                        for j in range(2):
                            ins = act.activation(dst[:, j, :], bank[i][:, j * L:(j + 1) * L], ACT.Identity, bias=bqk[:, 2 * i + j:2 * i + j + 1])
                        ins.then_inc(qk_done, 1)
                    for t in range(TB):
                        act.wait_ge(v_ready, TB * b + t + 1 + VR)
                        act.activation(v_sb[:, t, :], bank[t][:, 0:D], ACT.Copy).then_inc(v_done, 1)
                    for u, (t, h, n) in enumerate(UNITS):
                        w_ = (t + 1) * P
                        act.wait_ge(nb_done, NU * b + u + 1)
                        act.wait_ge(pT_ready, NU * b + u - NPS + 1 + PTR)
                        for j in range(n):
                            ins = act.activation(pr[:, u % NPS, j * w_:(j + 1) * w_], bank[2 + u % 2][:, j * w_:(j + 1) * w_], ACT.Exp,
                                                 bias=nb[:, t, h + j:h + j + 1], scale=SCALE, accum_out=den[:, t, h + j:h + j + 1])
                        ins.then_inc(exp_done, 1)
                    act.wait_ge(yT_ready, b + 1)
                    act.activation(yT[:, :, :].rearrange("p k (t c) -> p k t c", t=TB),
                                   bank[7][:, :].rearrange("p (t k c) -> p k t c", t=TB, k=KD), ACT.Copy).then_inc(yT_done, 1)

            @block.vector
            def _(dve):
                dve.sem_inc(pT_done, PTD)
                dve.sem_inc(y_done, YD)
                dve.sem_inc(x_added, XA)
                dve.sem_inc(pT_ready, PTR)
                with dve.Fori(0, B) as b:
                    def maxima(u):
                        t, h, n = UNITS[u]
                        dve.wait_ge(s_ready, NU * b + u + 1 + SR)
                        dve.reduce_max(mx[:, t, h:h + n], bank[2 + u % 2][:, :].rearrange("p (j l) -> p j l", j=n), axis=AXX).then_inc(max_done, 1)
                        dve.wait_ge(max_done, NU * b + u + 1)
                        dve.tensor_scalar(nb[:, t, h:h + n], mx[:, t, h:h + n], -SCALE, None, ALU.mult).then_inc(nb_done, 1)

                    def copy(u):
                        dve.wait_ge(pT_ready, NU * b + u + 1 + PTR)
                        dve.wait_ge(y_ready, NU * b + u - NPS + 1 + YR)
                        dve.tensor_copy(pT[:, u % NPS, :], bank[4 + u % 2][:, :]).then_inc(pT_done, 1)

                    def divide(t):
                        dve.wait_ge(exp_done, NU * b + (4, NU)[t] + ED)
                        dve.reciprocal(rden[:, t, :], den[:, t, :]).then_inc(inv_done, 1)
                        dve.wait_ge(inv_done, TB * b + t + 1)
                        dve.wait_ge(y_ready, NU * b + (4, NU)[t] + YR)
                        dve.tensor_tensor(y[:, t, :].rearrange("p (h d) -> p h d", d=HD),
                                          bank[6][:, 0:D].rearrange("p (h d) -> p h d", d=HD),
                                          rden[:, t, :].unsqueeze(2).broadcast_to([P, AH, HD]), ALU.mult).then_inc(y_done, 1)

                    maxima(0)
                    maxima(1)
                    for u in range(NU):
                        copy(u)
                        if u + 2 < NU:
                            maxima(u + 2)
                        if u == 4:
                            divide(0)
                    divide(1)
                    dve.wait_ge(out_ready, TB * (b + 1) + OUT)
                    for t in range(TB):
                        xt = c.x[:, ds(TB * b + t, 1), :].rearrange("p a d -> p (a d)")
                        dve.tensor_tensor(xt, xt, bank[t][:, 0:D], ALU.add).then_inc(x_added, 1)
        p.retire()


def build(nc, a, out):
    with ExitStack() as stack:
        c = Core(nc, stack)
        c.bank = [stack.enter_context(nc.psum_tensor(f"bank{i}", [P, 512], F32)) for i in range(8)]
        c.x = c.sb("x", [P, NT, D])
        c.xnT = c.sb("xnT", [P, KD, T])
        c.ident = c.sb("ident", [P, P])
        c.identb = c.sb("identb", [P, P], BF16)
        c.before = c.sb("before", [P, P], BF16)
        c.after = c.sb("after", [P, P], BF16)
        c.earlier = c.sb("earlier", [P, P], BF16)
        c.onesb = c.sb("onesb", [P, P], BF16)
        loaded = c.sem("x_loaded")
        stored = c.sem("stored")
        xv = a["x"].rearrange("(t p) d -> p t d", p=P)
        with nc.Block() as block:
            @block.sync
            def _(sp):
                sp.dma_start(c.x[:, :, :], xv).then_inc(loaded, 16)
                sp.dma_start(c.ident[:, :], a["ident"]).then_inc(loaded, 16)
                sp.dma_start(c.identb[:, :], a["identb"]).then_inc(loaded, 16)
                sp.dma_start(c.before[:, :], a["before"]).then_inc(loaded, 16)
                sp.dma_start(c.after[:, :], a["after"]).then_inc(loaded, 16)
                sp.dma_start(c.earlier[:, :], a["earlier"]).then_inc(loaded, 16)
                sp.dma_start(c.onesb[:, :], a["onesb"]).then_inc(loaded, 16)
                sp.wait_ge(loaded, 112)
        normalise(nc, "n1", c)
        mixer(nc, c, a)
        m = Core(nc, stack)
        c.spread = m.sb("spread", [PARTS * E, E * FI], BF16)
        w_gate, w_up = m.sb("w_gate", [P, KD, E * FI]), m.sb("w_up", [P, KD, E * FI])
        w_down, w_router = m.sb("w_down", [P, FT, D]), m.sb("w_router", [P, KD, E])
        loaded_router, loaded_experts = m.sem("loaded_router"), m.sem("loaded_experts")
        with nc.Block() as block:
            @block.sync
            def _(sp):
                sp.dma_start(w_router[:, :, :], a["w_router"]).then_inc(loaded_router, 16)
                for dst, n in ((w_gate, "w_gate"), (w_up, "w_up"), (w_down, "w_down"), (c.spread, "spread")):
                    sp.dma_start(dst[:], a[n]).then_inc(loaded_experts, 16)
        ex = (w_gate, w_up, w_down, w_router, loaded_router, loaded_experts)
        if STOP >= 2:
            normalise(nc, "n2", c)
            experts(nc, c, "e1", *ex)
        if STOP >= 3:
            normalise(nc, "n3", c)
            attention(nc, c, a)
        if STOP >= 4:
            normalise(nc, "n4", c)
            experts(nc, c, "e2", *ex)
        with nc.Block() as block:
            @block.sync
            def _(sp):
                sp.dma_start(out.rearrange("(t p) d -> p t d", p=P), c.x[:, :, :]).then_inc(stored, 16)
                sp.wait_ge(stored, 16)


STOP = 4


def kernel(**inputs):
    import numpy as np
    import concourse.bacc as bacc
    from concourse import mybir as mb
    from concourse.bass_utils import run_bass_kernel_spmd as run

    import ml_dtypes
    bf = ml_dtypes.bfloat16
    g = lambda n: np.asarray(inputs[n])
    w_in = g("L0_attn_a_W_in")
    w_qkv = g("L0_attn_b_w_qkv").reshape(KD, P, 3 * D).transpose(1, 0, 2)
    b_qkv = g("L0_attn_b_b_qkv")
    arrays = {
        "x": g("L0_attn_a_hidden_states").reshape(T, D),
        "w_in": w_in.T.reshape(KD, P, PROJ).transpose(1, 0, 2),
        "conv_w": g("L0_attn_a_conv_w").reshape(CT, P, TAPS).transpose(1, 0, 2),
        "conv_b": g("L0_attn_a_conv_b").reshape(CT, P).T,
        "dt_bias": g("L0_attn_a_dt_bias").reshape(H, 1),
        "A_log": g("L0_attn_a_A_log").reshape(H, 1),
        "D": g("L0_attn_a_D_param").reshape(H),
        "norm_w": g("L0_attn_a_norm_w").reshape(XT, P).T,
        "w_out": g("L0_attn_a_W_out").T.reshape(XT, P, D).transpose(1, 0, 2),
        "ident": np.eye(P, dtype=np.float32),
        "identb": np.eye(P).astype(bf),
        "before": (NEG * np.tril(np.ones((P, P)), -1)).astype(bf),
        "after": (NEG * np.triu(np.ones((P, P)), 1)).astype(bf),
        "earlier": np.triu(np.ones((P, P)), 1).astype(bf),
        "onesb": np.ones((P, P)).astype(bf),
        "spread": np.tile(np.repeat(np.eye(E), FI, axis=1), (PARTS, 1)).astype(bf),
        "rmask": np.repeat(np.eye(8, dtype=np.float32), HD, axis=0),
        "w_router": g("L0_ffn_gate_w").reshape(KD, P, E).transpose(1, 0, 2),
        "w_gate": g("L0_ffn_w_gate").transpose(1, 0, 2).reshape(KD, P, E * FI).transpose(1, 0, 2),
        "w_up": g("L0_ffn_w_up").transpose(1, 0, 2).reshape(KD, P, E * FI).transpose(1, 0, 2),
        "w_down": g("L0_ffn_w_down").reshape(FT, P, D).transpose(1, 0, 2),
        "wqk": w_qkv[:, :, 0:2 * D],
        "wv": w_qkv[:, :, 2 * D:],
        "bqk": b_qkv[0:2 * D].reshape(4, P).T,
        "bv": b_qkv[2 * D:].reshape(1, D),
        "wo": g("L0_attn_b_w_out").reshape(KD, P, D).transpose(1, 0, 2),
        "bo": g("L0_attn_b_b_out").reshape(1, D),
    }
    arrays = {n: np.ascontiguousarray(v) for n, v in arrays.items()}
    nc = bacc.Bacc("TRN2", target_bir_lowering=False, num_devices=1)
    a = {n: nc.dram_tensor("in_" + n, v.shape, mb.dt.from_np(v.dtype), kind="ExternalInput").ap() for n, v in arrays.items()}
    out = nc.dram_tensor("out", (T, D), F32, kind="ExternalOutput").ap()
    build(nc, a, out)
    r = run(nc, [{"in_" + n: v for n, v in arrays.items()}], core_ids=[0])
    return r.results[0]["out"].reshape(B, L, D)
```

```python
from contextlib import ExitStack

import concourse.bass as bass
from concourse import mybir

ALU = mybir.AluOpType
ACT = mybir.ActivationFunctionType
AXX = mybir.AxisListType.X
F32 = mybir.dt.float32
BF16 = mybir.dt.bfloat16
F16 = mybir.dt.float16
I32 = mybir.dt.int32
ds = bass.ds

P = 128
B, L, D = 8, 256, 256
T = B * L
NT = T // P
KD = D // P
TB = L // P
NORM_EPS = 1e-5

H, PH, N, TAPS = 32, 64, 128, 4
INTER = H * PH
CONV = INTER + 2 * N
PROJ = INTER + CONV + H
CT = CONV // P
XT = INTER // P
HG = 8
NHG = H // HG

AH, HD = 16, 16
SCALE = HD ** -0.5
NEG = -1.0e30

E, FI, TOPK = 32, 96, 8
CAP = 2 * (T * TOPK // E)
FT = E * FI // P
GT_TOK = 512
NG = T // GT_TOK
PARTS = 3

X_SCALE = 1024.0
TOP = 2.0 ** 14
PASSES = ((0, 0), (0, 1), (1, 0))
EXPONENT = 0x7F800000


class Core:

    def __init__(self, nc, stack):
        self.nc, self.stack, self.sems = nc, stack, []

    def sb(self, name, shape, dt=F32):
        return self.stack.enter_context(self.nc.sbuf_tensor(name, shape, dt))

    def sem(self, name):
        self.sems.append(self.stack.enter_context(self.nc.semaphore(name)))
        return self.sems[-1]

    def retire(self):
        with self.nc.Block() as block:
            @block.gpsimd
            def _(pool):
                for s in self.sems:
                    pool.sem_clear(s)


def normalise(nc, tag, c, load=None):
    with ExitStack() as inner:
        ph = Core(nc, inner)
        st = ph.sb(tag + "_stats", [P, NT, 6])
        mean = ph.sb(tag + "_mean", [P, NT])
        half = ph.sb(tag + "_half", [P, NT])
        var = ph.sb(tag + "_var", [P, NT])
        rstd = ph.sb(tag + "_rstd", [P, NT])
        expo = ph.sb(tag + "_expo", [P, NT])
        xh = ph.sb(tag + "_xh", [P, 2, D])
        banks = c.bank
        v = ph.sem(tag + "_v")
        expo_set = ph.sem(tag + "_expo_set")
        rstd_ready = ph.sem(tag + "_rstd_ready")
        xh_ready = ph.sem(tag + "_xh_ready")
        turned = ph.sem(tag + "_turned")
        high = ph.sem(tag + "_high")
        copied = ph.sem(tag + "_copied")
        with nc.Block() as block:
            @block.vector
            def _(dve):
                if load is not None:
                    dve.wait_ge(load, 16)
                dve.sem_inc(copied, 2)
                for t in range(NT):
                    dve.bn_stats(st[:, t, :], c.x[:, t, :]).then_inc(v, 1)
                dve.wait_ge(v, NT)
                dve.tensor_tensor(mean[:, :], st[:, :, 1], st[:, :, 4], ALU.add).then_inc(v, 1)
                dve.tensor_tensor(half[:, :], st[:, :, 1], st[:, :, 4], ALU.subtract).then_inc(v, 1)
                dve.tensor_tensor(var[:, :], st[:, :, 2], st[:, :, 5], ALU.add).then_inc(v, 1)
                dve.wait_ge(v, NT + 3)
                dve.tensor_scalar(mean[:, :], mean[:, :], 0.5, None, ALU.mult).then_inc(v, 1)
                dve.scalar_tensor_tensor(half[:, :], half[:, :], 0.25, half[:, :], ALU.mult, ALU.mult).then_inc(v, 1)
                dve.tensor_scalar(var[:, :], var[:, :], 1.0 / D, NORM_EPS, ALU.mult, ALU.add).then_inc(v, 1)
                dve.wait_ge(v, NT + 6)
                dve.tensor_tensor(var[:, :], var[:, :], half[:, :], ALU.add).then_inc(v, 1)
                dve.wait_ge(v, NT + 7)
                dve.tensor_scalar(var[:, :], var[:, :], X_SCALE ** -2, None, ALU.mult).then_inc(v, 1)
                dve.wait_ge(rstd_ready, 1)
                with dve.Fori(0, NT // 2) as i:
                    for j in range(2):
                        dve.wait_ge(turned, 2 * i + j + 1)
                        dve.tensor_scalar(xh[:, j, :], c.x[:, ds(2 * i + j, 1), :].rearrange("p a d -> p (a d)"),
                                          mean[:, ds(2 * i + j, 1)], rstd[:, ds(2 * i + j, 1)],
                                          ALU.subtract, ALU.mult).then_inc(xh_ready, 1)
                    for j in range(2):
                        dve.wait_ge(high, 2 * i + j + 1)
                        tok = ds((2 * i + j) * P, P)
                        dve.tensor_tensor(c.xT[:, 1, :, tok], banks[j][:, 0:D].rearrange("p (k t) -> p k t", k=KD),
                                          c.xT[:, 0, :, tok], ALU.subtract).then_inc(copied, 1)

            @block.gpsimd
            def _(pool):
                pool.memset(expo[:, :], -0.5).then_inc(expo_set, 1)
                pool.wait_ge(expo_set, 1)
                pool.wait_ge(v, NT + 8)
                pool.tensor_tensor(rstd[:, :], var[:, :], expo[:, :], ALU.pow).then_inc(rstd_ready, 1)

            @block.tensor
            def _(pe):
                pe.sem_inc(turned, 2)
                with pe.Fori(0, NT // 2) as i:
                    for j in range(2):
                        pe.wait_ge(xh_ready, 2 * i + j + 1)
                        pe.wait_ge(copied, 2 * i + j + 1)
                        for k in range(KD):
                            mm = pe.transpose(banks[j][:, k * P:(k + 1) * P], xh[:, j, k * P:(k + 1) * P], c.ident[:, :])
                        mm.then_inc(turned, 1)

            @block.scalar
            def _(act):
                with act.Fori(0, NT // 2) as i:
                    for j in range(2):
                        act.wait_ge(turned, 2 * i + j + 3)
                        act.activation(c.xT[:, 0, :, ds((2 * i + j) * P, P)],
                                       banks[j][:, 0:D].rearrange("p (k t) -> p k t", k=KD), ACT.Copy).then_inc(high, 1)

        ph.retire()


def split_weights(nc, tag, c, jobs):
    nj = len(jobs)
    scale, unscale = c.sb(tag + "_scale", [P, nj]), c.sb(tag + "_unscale", [P, nj])
    with ExitStack() as inner:
        p = Core(nc, inner)
        raw = [p.sb(f"{tag}_raw_{name}", [P, parts.shape[2]]) for name, _, parts in jobs]
        mx, most = p.sb(tag + "_max", [P, nj]), p.sb(tag + "_most", [P, nj])
        loaded = [p.sem(f"{tag}_loaded_{name}") for name, _, _ in jobs]
        (max_ready, most_ready, floor_ready, power_ready, inverse_ready, scale_ready, high_ready, low_ready) = (
            p.sem(f"{tag}_{n}") for n in ("max", "most", "floor", "power", "inverse", "scale", "high", "low"))
        CH = 1536
        pieces = [(i, a, min(a + CH, parts.shape[2])) for i, (_, _, parts) in enumerate(jobs)
                  for a in range(0, parts.shape[2], CH)]
        with nc.Block() as block:
            @block.sync
            def _(sp):
                for i, (_, dram, _) in enumerate(jobs):
                    sp.dma_start(raw[i][:, :], dram).then_inc(loaded[i], 16)

            @block.gpsimd
            def _(pool):
                pool.wait_ge(max_ready, nj)
                pool.partition_all_reduce(most[:, :], mx[:, :], P, bass.bass_isa.ReduceOp.max).then_inc(most_ready, 1)

            @block.vector
            def _(dve):
                for i in range(nj):
                    dve.wait_ge(loaded[i], 16)
                    dve.reduce_max(mx[:, i:i + 1], raw[i][:, :], axis=AXX, apply_absolute_value=True).then_inc(max_ready, 1)
                dve.wait_ge(most_ready, 1)
                dve.tensor_scalar(most[:, :], most[:, :], 1e-30, None, ALU.max).then_inc(floor_ready, 1)
                dve.wait_ge(floor_ready, 1)
                dve.tensor_scalar(most[:, :].bitcast(I32), most[:, :].bitcast(I32), EXPONENT, None, ALU.bitwise_and)\
                    .then_inc(power_ready, 1)
                dve.wait_ge(power_ready, 1)
                dve.tensor_scalar(unscale[:, :], most[:, :], 1.0 / TOP, None, ALU.mult).then_inc(inverse_ready, 1)
                dve.wait_ge(inverse_ready, 1)
                dve.reciprocal(scale[:, :], unscale[:, :]).then_inc(scale_ready, 1)
                for n, (i, a, b) in enumerate(pieces):
                    dve.wait_ge(high_ready, n + 1)
                    dve.scalar_tensor_tensor(jobs[i][2][:, 1, a:b], raw[i][:, a:b], scale[:, i:i + 1], jobs[i][2][:, 0, a:b],
                                             ALU.mult, ALU.subtract).then_inc(low_ready, 1)

            @block.scalar
            def _(act):
                act.wait_ge(scale_ready, 1)
                for i, a, b in pieces:
                    act.activation(jobs[i][2][:, 0, a:b], raw[i][:, a:b], ACT.Copy, scale=scale[:, i:i + 1]).then_inc(high_ready, 1)
        p.retire()
    return scale, unscale


def split_matmul(pe, out, w, x, start=True):
    for n, (i, j) in enumerate(PASSES):
        for k in range(KD):
            mm = pe.matmul(out, w(i, k), x(j, k), start=(start and n == 0 and k == 0),
                           stop=(n == len(PASSES) - 1 and k == KD - 1))
    return mm


def mixer(nc, c, w):
    with ExitStack() as outer:
        m = Core(nc, outer)
        w_in = m.sb("w_in", [P, 2, KD, PROJ], F16)
        w_out = m.sb("w_out", [P, XT, D])
        nrm_w = m.sb("nrm_w", [P, XT])
        conv_w = m.sb("conv_w_sb", [P, CT, TAPS])
        conv_b = m.sb("conv_b_sb", [P, CT])
        d_row = m.sb("d_row", [P, H])
        dt_tok = m.sb("dt_tok", [P, NT, H])
        loaded_in, loaded_dt, loaded_out = m.sem("loaded_in"), m.sem("loaded_dt"), m.sem("loaded_out")
        _, unscale = split_weights(nc, "mw", m, [("w_in", w["w_in"].rearrange("p k n -> p (k n)"),
                                                  w_in[:, :, :, :].rearrange("p i k n -> p i (k n)"))])
        undo = m.sb("undo_in", [P, 1])
        cum_parts = nc.dram_tensor("cum_parts", [PARTS, H, T], BF16, kind="Internal").ap()
        ncum_parts = nc.dram_tensor("neg_cum_parts", [PARTS, H, T], BF16, kind="Internal").ap()

        with ExitStack() as inner:
            p = Core(nc, inner)
            banks = c.bank
            z, a, e, u, lg, dt = (p.sb("pre_" + n, [H, T]) for n in ("z", "a", "e", "u", "lg", "dt"))
            r, same = u, lg
            ones = p.sb("pre_ones", [H, L])
            dtb, alog, aneg = (p.sb("pre_" + n, [H, 1]) for n in ("dtb", "alog", "aneg"))
            part = [p.sb(f"pre_part{i}", [H, T], BF16) for i in range(PARTS)]
            npart = [p.sb(f"pre_npart{i}", [H, T], BF16) for i in range(PARTS)]
            (dt_proj, z_ready, nabs_ready, exp_ready, u_ready, ln_ready, less_ready, safe_ready, inv_ready,
             ratio_ready, tiny_ready, term_ready, sum_ready, dt_ready, a_ready, da_ready, ones_ready, cum_ready,
             part_ready, rest_ready, npart_ready, dt_turned, dt_copied, saved, undo_ready,
             taps_scaled) = (
                p.sem("pre_" + n) for n in (
                    "dt_proj", "z", "nabs", "exp", "u", "ln", "less", "safe", "inv", "ratio", "tiny", "term", "sum",
                    "dt", "a", "da", "ones", "cum", "part", "rest", "npart", "dt_turned", "dt_copied", "saved", "undo", "taps"))
            with nc.Block() as block:
                @block.sync
                def _(sp):
                    sp.dma_start(dtb[:, :], w["dt_bias"]).then_inc(loaded_dt, 16)
                    sp.dma_start(alog[:, :], w["A_log"]).then_inc(loaded_dt, 16)
                    sp.dma_start(conv_w[:, :, :], w["conv_w"]).then_inc(loaded_in, 16)
                    sp.dma_start(conv_b[:, :], w["conv_b"]).then_inc(loaded_in, 16)
                    sp.dma_start(d_row[:, :], w["D"].partition_broadcast(P)).then_inc(loaded_in, 16)
                    sp.dma_start(w_out[:, :, :], w["w_out"]).then_inc(loaded_out, 16)
                    sp.dma_start(nrm_w[:, :], w["norm_w"]).then_inc(loaded_out, 16)
                    for i in range(PARTS):
                        sp.wait_ge(part_ready, i + 1)
                        sp.dma_start(cum_parts[i], part[i][:, :]).then_inc(saved, 16)
                        sp.wait_ge(npart_ready, i + 1)
                        sp.dma_start(ncum_parts[i], npart[i][:, :]).then_inc(saved, 16)
                    sp.wait_ge(saved, 32 * PARTS)

                @block.gpsimd
                def _(pool):
                    pool.memset(ones[:, :], 1.0).then_inc(ones_ready, 1)

                @block.tensor
                def _(pe):
                    for q in range(T // 512):
                        split_matmul(pe, banks[q][0:H, :], lambda i, k: w_in[:, i, k, PROJ - H:PROJ],
                                     lambda i, k: c.xT[:, i, k, q * 512:(q + 1) * 512]).then_inc(dt_proj, 1)
                    pe.wait_ge(dt_ready, 1)
                    for t in range(NT):
                        mm = pe.transpose(banks[7][:, t * H:(t + 1) * H], dt[:, t * P:(t + 1) * P], c.ident[0:H, 0:H])
                    mm.then_inc(dt_turned, 1)

                @block.scalar
                def _(act):
                    act.wait_ge(loaded_dt, 32)
                    act.activation(a[:, 0:1], alog[:, :], ACT.Exp).then_inc(a_ready, 1)
                    act.wait_ge(nabs_ready, 1)
                    act.activation(e[:, :], e[:, :], ACT.Exp).then_inc(exp_ready, 1)
                    act.wait_ge(u_ready, 1)
                    act.activation(lg[:, :], u[:, :], ACT.Ln).then_inc(ln_ready, 1)
                    act.wait_ge(dt_turned, 1)
                    act.activation(dt_tok[:, :, :], banks[7][:, :].rearrange("p (t h) -> p t h", h=H), ACT.Copy).then_inc(dt_copied, 1)
                    for i in range(PARTS):
                        act.wait_ge(part_ready, i + 1)
                        act.activation(npart[i][:, :], part[i][:, :], ACT.Copy, scale=-1.0).then_inc(npart_ready, 1)

                @block.vector
                def _(dve):
                    dve.tensor_scalar(undo[:, :], unscale[:, :], 1.0 / X_SCALE, None, ALU.mult).then_inc(undo_ready, 1)
                    dve.wait_ge(undo_ready, 1)
                    dve.wait_ge(loaded_dt, 32)
                    dve.wait_ge(a_ready, 1)
                    dve.tensor_scalar(aneg[:, :], a[:, 0:1], -1.0, None, ALU.mult).then_inc(a_ready, 1)
                    for q in range(T // 512):
                        dve.wait_ge(dt_proj, q + 1)
                        dve.tensor_scalar(z[:, q * 512:(q + 1) * 512], banks[q][0:H, :], undo[0:H, 0:1], dtb[:, 0:1],
                                          ALU.mult, ALU.add).then_inc(z_ready, 1)
                    dve.wait_ge(z_ready, 4)
                    dve.scalar_tensor_tensor(e[:, :], z[:, :], -1.0, z[:, :], ALU.mult, ALU.min).then_inc(nabs_ready, 1)
                    dve.wait_ge(exp_ready, 1)
                    dve.tensor_scalar(u[:, :], e[:, :], 1.0, None, ALU.add).then_inc(u_ready, 1)
                    dve.wait_ge(ln_ready, 1)
                    dve.tensor_scalar(a[:, :], u[:, :], -1.0, None, ALU.add).then_inc(less_ready, 1)
                    dve.wait_ge(less_ready, 1)
                    dve.scalar_tensor_tensor(r[:, :], a[:, :], 0.0, a[:, :], ALU.is_equal, ALU.add).then_inc(safe_ready, 1)
                    dve.scalar_tensor_tensor(dt[:, :], a[:, :], 0.0, e[:, :], ALU.is_equal, ALU.mult).then_inc(tiny_ready, 1)
                    dve.wait_ge(safe_ready, 1)
                    dve.reciprocal(r[:, :], r[:, :]).then_inc(inv_ready, 1)
                    dve.wait_ge(inv_ready, 1)
                    dve.tensor_tensor(r[:, :], r[:, :], e[:, :], ALU.mult).then_inc(ratio_ready, 1)
                    dve.wait_ge(ratio_ready, 1)
                    dve.tensor_tensor(lg[:, :], lg[:, :], r[:, :], ALU.mult).then_inc(term_ready, 1)
                    dve.wait_ge(term_ready, 1)
                    dve.wait_ge(tiny_ready, 1)
                    dve.tensor_tensor(lg[:, :], lg[:, :], dt[:, :], ALU.add).then_inc(sum_ready, 1)
                    dve.wait_ge(sum_ready, 1)
                    dve.scalar_tensor_tensor(dt[:, :], z[:, :], 0.0, lg[:, :], ALU.max, ALU.add).then_inc(dt_ready, 1)
                    dve.wait_ge(dt_ready, 1)
                    dve.wait_ge(a_ready, 2)
                    dve.tensor_scalar(a[:, :], dt[:, :], aneg[:, 0:1], None, ALU.mult).then_inc(da_ready, 1)
                    dve.wait_ge(da_ready, 1)
                    dve.wait_ge(ones_ready, 1)
                    dve.wait_ge(loaded_in, 48)
                    dve.tensor_scalar(conv_w[:, :, :], conv_w[:, :, :], undo[:, 0:1], None, ALU.mult).then_inc(taps_scaled, 1)
                    for b in range(B):
                        dve.tensor_tensor_scan(z[:, b * L:(b + 1) * L], ones[:, :], a[:, b * L:(b + 1) * L], 0.0,
                                               ALU.mult, ALU.add).then_inc(cum_ready, 1)
                    dve.wait_ge(cum_ready, B)
                    for i in range(PARTS):
                        dve.tensor_copy(part[i][:, :], z[:, :]).then_inc(part_ready, 1)
                        dve.wait_ge(part_ready, i + 1)
                        if i < PARTS - 1:
                            dve.tensor_tensor(z[:, :], z[:, :], part[i][:, :], ALU.subtract).then_inc(rest_ready, 1)
                            dve.wait_ge(rest_ready, i + 1)

            p.retire()

        with ExitStack() as inner:
            mixer_loop(nc, c, w_in, w_out, nrm_w, conv_w, conv_b, d_row, dt_tok, loaded_in, loaded_out,
                       cum_parts, ncum_parts, undo, Core(nc, inner))
        m.retire()


def mixer_loop(nc, c, w_in, w_out, nrm_w, conv_w, conv_b, d_row, dt_tok, loaded_in, loaded_out, cum_parts, ncum_parts, undo, p):
    PAIRS = [(XT, XT + 1)] + [(2 * i, 2 * i + 1) for i in range(XT // 2)]
    NP = len(PAIRS)
    GU = TB * INTER // 512
    XU = TB * XT // 4
    EU = 3 * H // 4
    TR = EU // 3
    ES = 6
    EARLY = 6

    cv = p.sb("cv", [P, CT, L])
    stage = p.sb("stage", [P, 2, 512])
    xdt = p.sb("xdt", [P, TB, INTER])
    yg = p.sb("yg", [P, TB, INTER])
    gate = p.sb("gate", [P, TB, INTER])
    sc = p.sb("sc", [P, ES, 512])
    gsb = p.sb("gsb", [P, 3 * P])
    gT = p.sb("gT", [P, TB, XT, P])
    lrow = p.sb("lrow", [2 * PARTS, 2, HG, L], BF16)
    rrow = p.sb("rrow", [2 * PARTS, 2, HG, L], BF16)
    ssp = p.sb("ssp", [P, TB, NHG])
    junk = p.sb("junk", [P, TB, 512], BF16)
    ms = p.sb("ms", [P, TB])
    rs = p.sb("rs", [P, TB])
    expo = p.sb("m_expo", [P, TB])
    bank = c.bank

    (w_scaled, consts, pair_ready, tap_done, tap_dve, conv_done, silu_done, gate_ready, gate_done, g_ready, g_done,
     xturn_ready, xturn_done, turn_ready, turn_done, xdt_done, dx_done, e_ready, exp_done, m_dve, m_pool, y_done,
     y_added, gated, squared, out_ready, x_added, ss_ready, ms_ready, rs_ready) = (p.sem("mx_" + n) for n in (
         "w_scaled", "consts", "pair_ready", "tap_done", "tap_dve", "conv_done", "silu_done", "gate_ready",
         "gate_done", "g_ready", "g_done", "xturn_ready", "xturn_done", "turn_ready", "turn_done", "xdt_done",
         "dx_done", "e_ready", "exp_done", "m_dve", "m_pool", "y_done", "y_added", "gated", "squared", "out_ready",
         "x_added", "ss_ready", "ms_ready", "rs_ready"))
    rows = [p.sem("rows0"), p.sem("rows1")]
    START = {"xturn_done": 1, "turn_done": 2, "xdt_done": 2, "dx_done": 2, "e_ready": 12, "exp_done": 2, "y_done": 2,
             "y_added": 1, "gated": 1, "squared": 2, "out_ready": 2, "x_added": 1, "gate_done": 1, "m_pool": 1}
    (XTD, TD, XD, DX, ER, XP, YD, YA, GTD, SQ, OR, XA, GD, MP) = START.values()

    with nc.Block() as block:
        @block.sync
        def _(sp):
            sp.wait_ge(consts, 3)
            with sp.Fori(0, B) as b:
                for g in range(NHG):
                    sp.wait_ge(e_ready, EU * b + 6 * g - 6 + ER)
                    sp.dma_start(rrow[0:2 * PARTS:2, g % 2, :, :],
                                 cum_parts[:, g * HG:(g + 1) * HG, ds(b * L, L)]).then_inc(rows[g % 2], 16)
                    sp.dma_start(lrow[1:2 * PARTS:2, g % 2, :, :],
                                 ncum_parts[:, g * HG:(g + 1) * HG, ds(b * L, L)]).then_inc(rows[g % 2], 16)

        @block.tensor
        def _(pe):
            pe.sem_inc(e_ready, ER)
            pe.sem_inc(y_done, YD)
            pe.sem_inc(out_ready, OR)
            pe.wait_ge(loaded_in, 48)

            def pair(f, u):
                if u < 2:
                    pe.wait_ge(xturn_done, XU * f + XTD)
                else:
                    pe.wait_ge(conv_done, NP * f + u - 1)
                for j, ch in enumerate(PAIRS[u]):
                    o = INTER + ch * P
                    mm = split_matmul(pe, bank[u % 2][:, j * L:(j + 1) * L], lambda i, k: w_in[:, i, k, o:o + P],
                                      lambda i, k: c.xT[:, i, k, ds(f * L, L)])
                mm.then_inc(pair_ready, 1)

            def b_times_c(f):
                pe.wait_ge(silu_done, NP * f + 1)
                pe.wait_ge(turn_done, XU * f + TD)
                pe.matmul(bank[6][:, 0:L], cv[:, XT, 0:P], cv[:, XT + 1, :], start=True, stop=True)
                pe.matmul(bank[6][:, L:L + P], cv[:, XT, P:L], cv[:, XT + 1, P:L], start=True, stop=True).then_inc(g_ready, 1)

            def gates(f, g):
                t, n = divmod(g, GU // TB)
                u = NP + g
                if g < 2:
                    pe.wait_ge(conv_done, NP * f + u - 1)
                else:
                    pe.wait_ge(gate_done, GU * f + g - 1 + GD)
                split_matmul(pe, bank[u % 2][:, :], lambda i, k: c.xT[:, i, k, ds(f * L + t * P, P)],
                             lambda i, k: w_in[:, i, k, n * 512:(n + 1) * 512]).then_inc(gate_ready, 1)

            def x_turn(f, v):
                q, t = divmod(v, TB)
                u = NP + GU + v
                pe.wait_ge(silu_done, NP * (f + 1))
                if v < 2:
                    pe.wait_ge(gate_done, GU * f + GU - 1 + v + GD)
                else:
                    pe.wait_ge(xturn_done, XU * f + v - 1 + XTD)
                for j in range(4):
                    mm = pe.transpose(bank[u % 2][:, j * P:(j + 1) * P], cv[:, 4 * q + j, t * P:(t + 1) * P], c.ident[:, :])
                mm.then_inc(xturn_ready, 1)

            def scores(b, tr):
                g, first = tr // 2, 4 * (tr % 2)
                if tr % 2 == 0:
                    pe.wait_ge(rows[g % 2], 64 * b + 32 * (g // 2 + 1))
                for n in range(3):
                    u = 3 * tr + n
                    pe.wait_ge(exp_done, EU * b + u - 1 + XP)
                    cols = bank[2 + u % 2][:, :].rearrange("p (j l) -> p j l", l=(L if n < 2 else P))[:, :, 0:P]
                    nj = 2 if n < 2 else 4
                    pe.matmul(cols, c.identb[:, :], c.before[:, :].unsqueeze(1).broadcast_to([P, nj, P]),
                              start=True, stop=False, skip_group_check=True)
                    for j in range(nj):
                        h = first + (2 * n + j if n < 2 else j)
                        lo, w = (0, L) if n < 2 else (P, P)
                        mm = pe.matmul(bank[2 + u % 2][:, j * w:(j + 1) * w], lrow[:, g % 2, h, lo:lo + P],
                                       rrow[:, g % 2, h, lo:lo + w], start=False, stop=True, skip_group_check=True)
                    mm.then_inc(e_ready, 1)

            def outputs(b, tr):
                g, first = tr // 2, 4 * (tr % 2)
                if tr % 2 == 0:
                    pe.wait_ge(y_added, NHG * b + g + YA)
                    pe.wait_ge(xdt_done, XU * b + 2 * (g + 1) + XD)
                if tr == 0:
                    pe.wait_ge(x_added, TB * b + XA)
                pe.wait_ge(m_dve, 2 * (TR * b + tr + 1))
                pe.wait_ge(m_pool, TR * b + tr + 1 + MP)
                base = 3 * (tr % 2)
                for j in range(4):
                    col = (first + j) * PH
                    ch = g * 512 + col
                    early = sc[:, base + j // 2, (j % 2) * L:(j % 2 + 1) * L]
                    late = sc[:, base + 2, j * P:(j + 1) * P]
                    pe.matmul(bank[4][:, col:col + PH], early[:, 0:P], xdt[:, 0, ch:ch + PH], start=True, stop=True)
                    pe.matmul(bank[5][:, col:col + PH], early[:, P:L], xdt[:, 0, ch:ch + PH], start=True, stop=False)
                    mm = pe.matmul(bank[5][:, col:col + PH], late, xdt[:, 1, ch:ch + PH], start=False, stop=True)
                mm.then_inc(y_done, 1)

            def g_turn(b, t, q):
                v = t * NHG + q
                pe.wait_ge(gated, TB * NHG * b + 2 * q + t + 1 + GTD)
                pe.wait_ge(turn_done, XU * b + v - 1 + TD)
                for j in range(4):
                    ch = 4 * q + j
                    mm = pe.transpose(bank[6 + v % 2][:, j * P:(j + 1) * P], yg[:, t, ch * P:(ch + 1) * P], c.ident[:, :])
                mm.then_inc(turn_ready, 1)

            def project(b, t):
                if t == 0:
                    pe.wait_ge(y_added, NHG * (b + 1) + YA)
                pe.wait_ge(turn_done, XU * b + (t + 1) * NHG + TD)
                for ch in range(XT):
                    mm = pe.matmul(bank[4 + t][:, 0:D], gT[:, t, ch, :], w_out[:, ch, :],
                                   start=(ch == 0), stop=(ch == XT - 1))
                mm.then_inc(out_ready, 1)

            def turn(b, more):
                for tr in range(TR):
                    if tr + 1 < TR:
                        scores(b, tr + 1)
                    if more and tr < EARLY:
                        pair(b + 1, tr)
                    outputs(b, tr)
                for q in range(NHG):
                    if more and EARLY + q < NP:
                        pair(b + 1, EARLY + q)
                    g_turn(b, 0, q)
                for q in range(NHG):
                    g_turn(b, 1, q)
                    if more and q % 2:
                        gates(b + 1, q // 2)
                project(b, 0)
                if more:
                    gates(b + 1, 2)
                    gates(b + 1, 3)
                project(b, 1)
                if more:
                    for g in range(4, GU):
                        gates(b + 1, g)
                    b_times_c(b + 1)
                    for v in range(XU):
                        x_turn(b + 1, v)
                    scores(b + 1, 0)

            for u in range(NP):
                pair(0, u)
            for g in range(GU):
                gates(0, g)
            b_times_c(0)
            for v in range(XU):
                x_turn(0, v)
            scores(0, 0)
            pe.wait_ge(w_scaled, 1)
            pe.wait_ge(g_done, 1)
            with pe.Fori(0, B - 1) as b:
                turn(b, True)
            turn(B - 1, False)

        @block.scalar
        def _(act):
            act.sem_inc(gate_done, GD)
            act.sem_inc(xturn_done, XTD)
            act.sem_inc(turn_done, TD)
            act.sem_inc(exp_done, XP)
            act.sem_inc(squared, SQ)
            act.wait_ge(loaded_in, 48)

            def tap(f, u):
                act.wait_ge(pair_ready, NP * f + u + 1)
                for j, ch in enumerate(PAIRS[u]):
                    ins = act.activation(cv[:, ch, :], bank[u % 2][:, j * L:(j + 1) * L], ACT.Identity,
                                         bias=conv_b[:, ch:ch + 1], scale=conv_w[:, ch, TAPS - 1:TAPS])
                ins.then_inc(tap_done, 1)

            def conv_silu(f, u):
                q = PAIRS[u]
                act.wait_ge(conv_done, NP * f + u + 1)
                act.activation(cv[:, q[0]:q[1] + 1, :], cv[:, q[0]:q[1] + 1, :], ACT.Silu).then_inc(silu_done, 1)

            def gate_silu(f, g):
                t, n = divmod(g, GU // TB)
                act.wait_ge(gate_ready, GU * f + g + 1)
                act.wait_ge(gated, TB * NHG * f + GTD)
                act.activation(gate[:, t, n * 512:(n + 1) * 512], bank[(NP + g) % 2][:, :], ACT.Silu,
                               scale=undo[:, 0:1]).then_inc(gate_done, 1)

            def x_copy(f, v):
                act.wait_ge(xturn_ready, XU * f + v + 1)
                act.wait_ge(xdt_done, XU * f + v - 1 + XD)
                act.wait_ge(dx_done, XU * f + v - 1 + DX)
                act.activation(stage[:, v % 2, :], bank[(NP + GU + v) % 2][:, :], ACT.Copy).then_inc(xturn_done, 1)

            def exps(b, tr):
                for u in range(3 * tr, 3 * tr + 3):
                    act.wait_ge(e_ready, EU * b + u + 1 + ER)
                    if u % 3 == 0:
                        act.wait_ge(y_done, TR * b + tr - 1 + YD)
                    act.activation(sc[:, u % ES, :], bank[2 + u % 2][:, :], ACT.Exp).then_inc(exp_done, 1)

            def squares(b, g):
                for t in range(TB):
                    act.wait_ge(gated, TB * NHG * b + 2 * g + t + 1 + GTD)
                    act.wait_ge(squared, TB * NHG * b + 2 * g + t - 1 + SQ)
                    act.activation(junk[:, t, :], yg[:, t, g * 512:(g + 1) * 512], ACT.Square,
                                   accum_out=ssp[:, t, g:g + 1]).then_inc(squared, 1)

            def g_copy(b, t, q):
                v = t * NHG + q
                act.wait_ge(turn_ready, XU * b + v + 1)
                if q == 0:
                    act.wait_ge(out_ready, TB * b + t - 1 + OR)
                act.activation(gT[:, t, 4 * q:4 * q + 4, :], bank[6 + v % 2][:, :].rearrange("p (a t) -> p a t", a=4),
                               ACT.Copy).then_inc(turn_done, 1)

            def turn(b, more):
                for tr in range(TR):
                    if tr + 1 < TR:
                        exps(b, tr + 1)
                    if tr in (4, 6):
                        squares(b, tr // 2 - 2)
                    if more and tr < EARLY:
                        tap(b + 1, tr)
                squares(b, 2)
                for q in range(NHG):
                    if more and EARLY + q < NP:
                        tap(b + 1, EARLY + q)
                    if q == NHG - 1:
                        squares(b, 3)
                    g_copy(b, 0, q)
                for q in range(NHG):
                    g_copy(b, 1, q)
                    if more and q % 2:
                        gate_silu(b + 1, q // 2)
                if more:
                    for u in range(NP):
                        conv_silu(b + 1, u)
                    for g in range(2, GU):
                        gate_silu(b + 1, g)
                    for v in range(XU):
                        x_copy(b + 1, v)
                    exps(b + 1, 0)

            for u in range(NP):
                tap(0, u)
                if u:
                    conv_silu(0, u - 1)
            conv_silu(0, NP - 1)
            for g in range(GU):
                gate_silu(0, g)
            for v in range(XU):
                x_copy(0, v)
            exps(0, 0)
            with act.Fori(0, B - 1) as b:
                turn(b, True)
            turn(B - 1, False)

        @block.gpsimd
        def _(pool):
            pool.memset(lrow[:, :, :, :], 1.0).then_inc(consts, 1)
            pool.memset(rrow[:, :, :, :], 1.0).then_inc(consts, 1)
            pool.memset(expo[:, :], -0.5).then_inc(consts, 1)
            pool.sem_inc(dx_done, DX)
            pool.sem_inc(gated, GTD)
            pool.sem_inc(m_pool, MP)
            pool.wait_ge(loaded_in, 48)

            def d_times_x(f, v):
                q, t = divmod(v, TB)
                if v == 0:
                    pool.wait_ge(out_ready, TB * f + OR)
                pool.wait_ge(xturn_done, XU * f + v + 1 + XTD)
                hs, cs = slice(HG * q, HG * q + HG), slice(q * 512, (q + 1) * 512)
                pool.tensor_tensor(yg[:, t, cs].rearrange("p (h d) -> p h d", d=PH),
                                   stage[:, v % 2, :].rearrange("p (h d) -> p h d", d=PH),
                                   d_row[:, hs].unsqueeze(2).broadcast_to([P, HG, PH]), ALU.mult).then_inc(dx_done, 1)

            def decayed(b, tr):
                u = 3 * tr + 2
                pool.wait_ge(exp_done, EU * b + u + 1 + XP)
                pool.wait_ge(g_done, b + 1)
                s = sc[:, u % ES, :].rearrange("p (h l) -> p h l", h=4)
                pool.tensor_tensor(s, s, gsb[:, L:L + P].unsqueeze(1).broadcast_to([P, 4, P]), ALU.mult).then_inc(m_pool, 1)

            def gating(b, g):
                pool.wait_ge(y_added, NHG * b + g + 1 + YA)
                pool.wait_ge(gate_done, GU * (b + 1) + GD)
                for t in range(TB):
                    part = slice(g * 512, (g + 1) * 512)
                    pool.tensor_tensor(yg[:, t, part], yg[:, t, part], gate[:, t, part], ALU.mult).then_inc(gated, 1)

            def turn(b, more):
                for tr in range(TR):
                    if tr + 1 < TR:
                        decayed(b, tr + 1)
                    if tr % 2 == 0 and tr:
                        gating(b, tr // 2 - 1)
                gating(b, NHG - 1)
                pool.wait_ge(ms_ready, b + 1)
                pool.tensor_tensor(rs[:, :], ms[:, :], expo[:, :], ALU.pow).then_inc(rs_ready, 1)
                if more:
                    for v in range(XU):
                        d_times_x(b + 1, v)
                    decayed(b + 1, 0)

            for v in range(XU):
                d_times_x(0, v)
            decayed(0, 0)
            pool.wait_ge(loaded_out, 32)
            pool.tensor_tensor(w_out[:, :, :], w_out[:, :, :], nrm_w[:, :].unsqueeze(2).broadcast_to([P, XT, D]), ALU.mult)\
                .then_inc(w_scaled, 1)
            pool.wait_ge(consts, 3)
            with pool.Fori(0, B - 1) as b:
                turn(b, True)
            turn(B - 1, False)

        @block.vector
        def _(dve):
            dve.sem_inc(xdt_done, XD)
            dve.sem_inc(y_added, YA)
            dve.sem_inc(x_added, XA)

            def conv(f, u):
                dve.wait_ge(tap_done, NP * f + u + 1)
                for k in range(TAPS - 1):
                    back = k + 1
                    if k:
                        dve.wait_ge(tap_dve, 2 * (NP * f + u) + k)
                    for j, ch in enumerate(PAIRS[u]):
                        ins = dve.scalar_tensor_tensor(
                            cv[:, ch, back:L], bank[u % 2][:, j * L:(j + 1) * L - back],
                            conv_w[:, ch, TAPS - 1 - back:TAPS - back], cv[:, ch, back:L], ALU.mult, ALU.add)
                    ins.then_inc(tap_dve if k < TAPS - 2 else conv_done, 1)

            def g_copy(f):
                dve.wait_ge(g_ready, f + 1)
                dve.wait_ge(m_pool, TR * f + MP)
                dve.tensor_copy(gsb[:, :], bank[6][:, 0:3 * P]).then_inc(g_done, 1)

            def dt_times_x(f, v):
                q, t = divmod(v, TB)
                if v == 0:
                    dve.wait_ge(y_done, TR * f + YD)
                dve.wait_ge(xturn_done, XU * f + v + 1 + XTD)
                hs, cs = slice(HG * q, HG * q + HG), slice(q * 512, (q + 1) * 512)
                dve.tensor_tensor(xdt[:, t, cs].rearrange("p (h d) -> p h d", d=PH),
                                  stage[:, v % 2, :].rearrange("p (h d) -> p h d", d=PH),
                                  dt_tok[:, ds(TB * f + t, 1), hs].rearrange("p a h -> p (a h)").unsqueeze(2).broadcast_to([P, HG, PH]),
                                  ALU.mult).then_inc(xdt_done, 1)

            def decayed(b, tr):
                for u in range(3 * tr, 3 * tr + 2):
                    dve.wait_ge(exp_done, EU * b + u + 1 + XP)
                    s = sc[:, u % ES, :].rearrange("p (h l) -> p h l", h=2)
                    dve.tensor_tensor(s, s, gsb[:, 0:L].unsqueeze(1).broadcast_to([P, 2, L]), ALU.mult).then_inc(m_dve, 1)

            def add_y(b, g):
                dve.wait_ge(y_done, TR * b + 2 * (g + 1) + YD)
                dve.wait_ge(dx_done, XU * (b + 1) + DX)
                for t in range(TB):
                    part = yg[:, t, g * 512:(g + 1) * 512]
                    ins = dve.tensor_tensor(part, part, bank[4 + t][:, :], ALU.add)
                ins.then_inc(y_added, 1)

            def turn(b, more):
                for tr in range(TR):
                    if tr + 1 < TR:
                        decayed(b, tr + 1)
                    if tr % 2 == 0 and tr:
                        add_y(b, tr // 2 - 1)
                    if more and tr < EARLY:
                        conv(b + 1, tr)
                add_y(b, NHG - 1)
                if more:
                    for u in range(EARLY, NP):
                        conv(b + 1, u)
                dve.wait_ge(squared, TB * NHG * (b + 1) + SQ)
                dve.reduce_sum(ms[:, :], ssp[:, :, :], axis=AXX).then_inc(ss_ready, 1)
                dve.wait_ge(ss_ready, b + 1)
                dve.tensor_scalar(ms[:, :], ms[:, :], 1.0 / INTER, NORM_EPS, ALU.mult, ALU.add).then_inc(ms_ready, 1)
                dve.wait_ge(rs_ready, b + 1)
                for t in range(TB):
                    dve.wait_ge(out_ready, TB * b + t + 1 + OR)
                    xt = c.x[:, ds(TB * b + t, 1), :].rearrange("p a d -> p (a d)")
                    dve.scalar_tensor_tensor(xt, bank[4 + t][:, 0:D], rs[:, t:t + 1], xt, ALU.mult, ALU.add).then_inc(x_added, 1)
                if more:
                    g_copy(b + 1)
                    for v in range(XU):
                        dt_times_x(b + 1, v)
                    decayed(b + 1, 0)

            for u in range(NP):
                conv(0, u)
            g_copy(0)
            for v in range(XU):
                dt_times_x(0, v)
            decayed(0, 0)
            with dve.Fori(0, B - 1) as b:
                turn(b, True)
            turn(B - 1, False)
    p.retire()


def route(nc, c, tag, wT, w_router, undo_router, hidden_scale):
    with ExitStack() as inner:
        p = Core(nc, inner)
        sb, sem = (lambda n, *r: p.sb(f"{tag}_{n}", *r)), (lambda n: p.sem(f"{tag}_r_{n}"))
        bank = c.bank
        lgT = sb("lgT", [E, T])
        lg = sb("lg", [P, NT, E])
        top, tot, inv = sb("top", [P, NT]), sb("tot", [P, NT]), sb("inv", [P, NT])
        best, rest, pick = sb("best", [P, NT, TOPK]), sb("rest", [P, NT, E]), sb("pick", [P, NT, E])
        pickb = sb("pickb", [P, NT, E], BF16)
        parts, partsf = sb("parts", [P, NT, PARTS, E], BF16), sb("partsf", [P, NT, PARTS, E])
        (lg_ready, lgT_ready, turned, max_ready, sub_ready, exp_ready, sum_ready, inv_ready, prob_ready, best_ready,
         rest_ready, pick_ready, pickb_ready, wsum_ready, winv_ready, w_ready, pos_ready, kept_ready, part_ready,
         left_ready, wide_ready, w_turned, done) = (sem(n) for n in (
             "lg", "lgT", "turned", "max", "sub", "exp", "sum", "inv", "prob", "best", "rest", "pick", "pickb",
             "wsum", "winv", "w", "pos", "kept", "part", "left", "wide", "w_turned", "done"))
        wide = lambda t2: t2[:, :].unsqueeze(2).broadcast_to([P, NT, E])
        with nc.Block() as block:
            @block.tensor
            def _(pe):
                for q in range(T // 512):
                    split_matmul(pe, bank[q][0:E, :], lambda i, k: w_router[:, i, k, :],
                                 lambda i, k: c.xT[:, i, k, q * 512:(q + 1) * 512]).then_inc(lg_ready, 1)
                for t in range(NT):
                    if t % 4 == 0:
                        pe.wait_ge(lgT_ready, t // 4 + 1)
                    mm = pe.transpose(bank[4][:, t * E:(t + 1) * E], lgT[:, t * P:(t + 1) * P], c.ident[0:E, 0:E])
                mm.then_inc(turned, 1)
                pe.wait_ge(pickb_ready, 1)
                pe.matmul(bank[5][:, :], c.earlier[:, :], pickb[:, :, :], start=True, stop=True)
                for t in range(NT - 1):
                    mm = pe.matmul(bank[5][:, (t + 1) * E:], c.onesb[:, :],
                                   pickb[:, t:t + 1, :].broadcast_to([P, NT - 1 - t, E]),
                                   start=False, stop=True, skip_group_check=True)
                mm.then_inc(pos_ready, 1)
                pe.wait_ge(wide_ready, 1)
                for t in range(NT):
                    mm = pe.transpose(bank[t // 4][0:PARTS * E, (t % 4) * P:(t % 4 + 1) * P],
                                      partsf[:, t, :, :].rearrange("p i e -> p (i e)"), c.ident[:, :])
                    if t % 4 == 3:
                        mm.then_inc(w_turned, 1)

            @block.scalar
            def _(act):
                for q in range(T // 512):
                    act.wait_ge(lg_ready, q + 1)
                    act.activation(lgT[:, q * 512:(q + 1) * 512], bank[q][0:E, :], ACT.Copy,
                                   scale=undo_router[0:E, 0:1]).then_inc(lgT_ready, 1)
                act.wait_ge(sub_ready, 1)
                act.activation(lg[:, :, :], lg[:, :, :], ACT.Exp).then_inc(exp_ready, 1)
                act.wait_ge(part_ready, PARTS)
                act.activation(partsf[:, :, :, :], parts[:, :, :, :], ACT.Copy).then_inc(wide_ready, 1)
                for q in range(4):
                    act.wait_ge(w_turned, q + 1)
                    act.activation(wT[:, q * 512:(q + 1) * 512], bank[q][0:PARTS * E, :], ACT.Copy).then_inc(done, 1)

            @block.vector
            def _(dve):
                logits = bank[4][:, :].rearrange("p (t e) -> p t e", e=E)
                dve.wait_ge(turned, 1)
                dve.reduce_max(top[:, :], logits, axis=AXX).then_inc(max_ready, 1)
                dve.wait_ge(max_ready, 1)
                dve.tensor_tensor(lg[:, :, :], logits, wide(top), ALU.subtract).then_inc(sub_ready, 1)
                dve.wait_ge(exp_ready, 1)
                dve.reduce_sum(tot[:, :], lg[:, :, :], axis=AXX).then_inc(sum_ready, 1)
                dve.wait_ge(sum_ready, 1)
                dve.reciprocal(inv[:, :], tot[:, :]).then_inc(inv_ready, 1)
                dve.wait_ge(inv_ready, 1)
                dve.tensor_tensor(lg[:, :, :], lg[:, :, :], wide(inv), ALU.mult).then_inc(prob_ready, 1)
                dve.wait_ge(prob_ready, 1)
                for t in range(NT):
                    dve.max(best[:, t, :], lg[:, t, :]).then_inc(best_ready, 1)
                for t in range(NT):
                    dve.wait_ge(best_ready, t + 1)
                    dve.match_replace(out=rest[:, t, :], in_to_replace=best[:, t, :], in_values=lg[:, t, :], imm_value=-1.0).then_inc(rest_ready, 1)
                dve.wait_ge(rest_ready, NT)
                dve.tensor_scalar(pickb[:, :, :], rest[:, :, :], 0.0, None, ALU.is_lt).then_inc(pickb_ready, 1)
                dve.tensor_scalar(pick[:, :, :], rest[:, :, :], 0.0, None, ALU.is_lt).then_inc(pick_ready, 1)
                dve.reduce_sum(tot[:, :], best[:, :, :], axis=AXX).then_inc(wsum_ready, 1)
                dve.wait_ge(wsum_ready, 1)
                dve.reciprocal(inv[:, :], tot[:, :]).then_inc(winv_ready, 1)
                dve.wait_ge(winv_ready, 1)
                dve.wait_ge(pick_ready, 1)
                dve.tensor_tensor(lg[:, :, :], lg[:, :, :], wide(inv), ALU.mult).then_inc(w_ready, 1)
                dve.wait_ge(w_ready, 1)
                dve.scalar_tensor_tensor(lg[:, :, :], lg[:, :, :], hidden_scale, pick[:, :, :], ALU.mult, ALU.mult).then_inc(w_ready, 1)
                dve.wait_ge(w_ready, 2)
                dve.wait_ge(pos_ready, 1)
                dve.scalar_tensor_tensor(lg[:, :, :], bank[5][:, :].rearrange("p (t e) -> p t e", e=E), float(CAP),
                                         lg[:, :, :], ALU.is_lt, ALU.mult).then_inc(kept_ready, 1)
                dve.wait_ge(kept_ready, 1)
                for i in range(PARTS):
                    dve.tensor_copy(parts[:, :, i, :], lg[:, :, :]).then_inc(part_ready, 1)
                    if i < PARTS - 1:
                        dve.wait_ge(part_ready, i + 1)
                        dve.tensor_tensor(lg[:, :, :], lg[:, :, :], parts[:, :, i, :], ALU.subtract).then_inc(left_ready, 1)
                        dve.wait_ge(left_ready, i + 1)
        p.retire()


def experts(nc, c, tag, w_gate, w_up, w_down, w_router, k):
    with ExitStack() as inner:
        p = Core(nc, inner)
        wT = p.sb(tag + "_wT", [PARTS * E, T], BF16)
        route(nc, c, tag, wT, w_router, k["router"], k["hidden"])
        bank = c.bank
        NS, AHEAD = 4, 2
        act_g = p.sb(tag + "_act", [P, NS, GT_TOK])
        hid = p.sb(tag + "_hid", [P, NS, 2, GT_TOK], F16)
        (gate_ready, up_ready, wide_ready, silu_done, prod_done, full_done, high_done, hid_done, hid_used, x_added) = (
            p.sem(f"{tag}_{n}") for n in ("gate", "up", "wide", "silu", "prod", "full", "high", "hid", "hid_used", "x_added"))
        SD, PD, FD, HD_, HU, XA = 2, 2, 2, NS, NS, 1
        with nc.Block() as block:
            @block.tensor
            def _(pe):
                pe.sem_inc(hid_used, HU)

                def up(g, j):
                    tok = ds(g * GT_TOK, GT_TOK)
                    pe.wait_ge(silu_done, FT * g + j - 1 + SD)
                    split_matmul(pe, bank[j % 2][:, :], lambda i, k: w_gate[:, i, k, j * P:(j + 1) * P],
                                 lambda i, k: c.xT[:, i, k, tok]).then_inc(gate_ready, 1)
                    pe.wait_ge(prod_done, FT * g + j - 1 + PD)
                    split_matmul(pe, bank[2 + j % 2][:, :], lambda i, k: w_up[:, i, k, j * P:(j + 1) * P],
                                 lambda i, k: c.xT[:, i, k, tok]).then_inc(up_ready, 1)
                    pe.wait_ge(full_done, FT * g + j - 1 + FD)
                    pe.matmul(bank[4 + j % 2][:, :], c.spread[:, j * P:(j + 1) * P], wT[:, tok],
                              start=True, stop=True).then_inc(wide_ready, 1)

                def down(g, j):
                    if j == 0:
                        pe.wait_ge(x_added, g + XA)
                    pe.wait_ge(hid_done, FT * g + j + 1 + HD_)
                    for t in range(GT_TOK // P):
                        for n, (iw, ih) in enumerate(PASSES):
                            mm = pe.matmul(bank[6 + t // 2][:, (t % 2) * D:(t % 2 + 1) * D],
                                           hid[:, j % NS, ih, t * P:(t + 1) * P], w_down[:, iw, j, :],
                                           start=(j == 0 and n == 0 and t % 2 == 0), stop=(j == FT - 1 and n == 2),
                                           skip_group_check=True)
                    mm.then_inc(hid_used, 1)

                for j in range(AHEAD):
                    up(0, j)
                with pe.Fori(0, NG - 1) as g:
                    for j in range(FT):
                        if j + AHEAD < FT:
                            up(g, j + AHEAD)
                        else:
                            up(g + 1, j + AHEAD - FT)
                        down(g, j)
                for j in range(FT):
                    if j + AHEAD < FT:
                        up(NG - 1, j + AHEAD)
                    down(NG - 1, j)

            @block.scalar
            def _(act):
                act.sem_inc(silu_done, SD)

                def silu(g, j):
                    act.wait_ge(gate_ready, FT * g + j + 1)
                    act.wait_ge(hid_done, FT * g + j - NS + 1 + HD_)
                    act.activation(act_g[:, j % NS, :], bank[j % 2][:, :], ACT.Silu, scale=k["gate"]).then_inc(silu_done, 1)

                def high(g, j):
                    act.wait_ge(full_done, FT * g + j + 1 + FD)
                    act.wait_ge(hid_used, FT * g + j - NS + 1 + HU)
                    act.activation(hid[:, j % NS, 0, :], act_g[:, j % NS, :], ACT.Copy).then_inc(high_done, 1)

                silu(0, 0)
                with act.Fori(0, NG - 1) as g:
                    for j in range(FT):
                        if j + 1 < FT:
                            silu(g, j + 1)
                        else:
                            silu(g + 1, 0)
                        high(g, j)
                for j in range(FT):
                    if j + 1 < FT:
                        silu(NG - 1, j + 1)
                    high(NG - 1, j)

            @block.gpsimd
            def _(pool):
                pool.sem_inc(hid_done, HD_)
                with pool.Fori(0, NG) as g:
                    for j in range(FT):
                        pool.wait_ge(high_done, FT * g + j + 1)
                        pool.tensor_tensor(hid[:, j % NS, 1, :], act_g[:, j % NS, :], hid[:, j % NS, 0, :], ALU.subtract).then_inc(hid_done, 1)

            @block.vector
            def _(dve):
                dve.sem_inc(prod_done, PD)
                dve.sem_inc(full_done, FD)
                dve.sem_inc(x_added, XA)

                def product(g, j):
                    dve.wait_ge(silu_done, FT * g + j + 1 + SD)
                    dve.wait_ge(up_ready, FT * g + j + 1)
                    dve.tensor_tensor(act_g[:, j % NS, :], act_g[:, j % NS, :], bank[2 + j % 2][:, :], ALU.mult).then_inc(prod_done, 1)
                    dve.wait_ge(prod_done, FT * g + j + 1 + PD)
                    dve.wait_ge(wide_ready, FT * g + j + 1)
                    dve.tensor_tensor(act_g[:, j % NS, :], act_g[:, j % NS, :], bank[4 + j % 2][:, :], ALU.mult).then_inc(full_done, 1)

                def add(g):
                    dve.wait_ge(hid_used, FT * (g + 1) + HU)
                    for t in range(GT_TOK // P):
                        xt = c.x[:, ds(GT_TOK // P * g + t, 1), :].rearrange("p a d -> p (a d)")
                        ins = dve.scalar_tensor_tensor(xt, bank[6 + t // 2][:, (t % 2) * D:(t % 2 + 1) * D], k["out"], xt,
                                                       ALU.mult, ALU.add)
                    ins.then_inc(x_added, 1)

                for j in range(AHEAD):
                    product(0, j)
                with dve.Fori(0, NG - 1) as g:
                    for j in range(AHEAD, FT):
                        product(g, j)
                    for j in range(AHEAD):
                        product(g + 1, j)
                    add(g)
                for j in range(AHEAD, FT):
                    product(NG - 1, j)
                add(NG - 1)
        p.retire()


def attention(nc, c, w, wqkv, undo):
    PR, MR = 3 * HD, 3
    HH = AH // 2
    NU = 12
    NQ = 4
    ES = 6
    V1 = HD + 1
    ROW = 2.0 ** 15
    QTOP = 2.0 ** 12
    GT = 512
    with ExitStack() as inner:
        p = Core(nc, inner)
        sb, sem = (lambda n, *r: p.sb("at_" + n, *r)), (lambda n: p.sem("at_" + n))
        wo = sb("wo", [P, KD, D])
        bqk, bv, bo = sb("bqk", [P, 4]), sb("bv", [P, D]), sb("bo", [1, D])
        ones = sb("ones", [1, P])
        bmax, ball, bound, power, scale, fold, escale = (sb(n, [P, 1]) for n in (
            "bmax", "ball", "bound", "power", "scale", "fold", "escale"))
        full = sb("full", [P, 2, GT])
        parts = sb("parts", [P, 4, 2, GT], F16)
        q3, k3 = sb("q3", [64, 2, AH, L], F16), sb("k3", [64, 2, AH, L], F16)
        v_all = sb("v", [P, NT, AH, V1])
        pT = sb("probsT", [P, ES, 512])
        mx = sb("mx", [P, 2, HH, TB])
        neg, negs = sb("neg", [HH * TB, P]), [sb(f"neg_parts{g}", [HH * TB, MR, P], F16) for g in range(2)]
        unit = sb("unit", [HH * TB, P])
        rden = sb("rden", [P, TB, AH])
        y, yT = sb("y", [P, TB, D]), sb("yT", [P, KD, L])
        bank = c.bank
        qk_parts = nc.dram_tensor("qk_parts", [4, 2 * P, T], F16, kind="Internal").ap()
        mx_parts = nc.dram_tensor("mx_parts", [B, 2, MR, HH * L], F16, kind="Internal").ap()
        loaded, const, scales = sem("loaded"), sem("const"), sem("scales")
        (all_ready, proj_ready, full_ready, high_ready, low_ready, v_ready, v_done, s_ready, max_done, nbt_ready,
         neg_ready, neg_dve, neg_parts, st_ready, exp_done, pv_ready, inv_done, y_done, yT_ready, yT_done,
         out_ready, x_added) = (sem(n) for n in (
             "all", "proj", "full", "high", "low", "v_ready", "v_done", "s", "max", "nbt",
             "neg", "neg_step", "neg_parts", "st", "exp", "pv", "inv", "y", "yT_ready", "yT_done", "out", "x_added"))
        saved = [sem(f"saved{n}") for n in range(4)]
        qk_loaded = [[sem(f"qk_loaded{s}{g}") for g in range(2)] for s in range(2)]
        mx_saved = [sem(f"mx_saved{g}") for g in range(2)]
        mx_rows = [sem(f"mx_rows{g}") for g in range(2)]
        START = {"full": 2, "low": 2, "saved": 16, "v_done": 2, "max": 2, "nbt": 2, "neg": 1, "rows": 16, "exp": 2,
                 "pv": 2, "y": 1, "x": 1, "neg_parts": 1}
        FU, LO, SV, VD, MD, NB, NR, RW, XP, PV, YD, XA, NP = START.values()

        def trio(qd):
            return [(0, 4 * qd, 4), (1, 4 * qd, 2), (1, 4 * qd + 2, 2)]

        with nc.Block() as block:
            @block.sync
            def _(sp):
                for dst, src in ((bqk, w["bqk"]), (wo, w["wo"]), (bv, w["bv"].partition_broadcast(P)), (bo, w["bo"])):
                    sp.dma_start(dst[:], src).then_inc(loaded, 16)
                with sp.Fori(0, NG) as g:
                    for n in range(4):
                        sp.wait_ge(low_ready, 4 * g + n + 1 + LO)
                        sp.dma_start(qk_parts[n].rearrange("(c p) t -> p c t", p=P)[:, :, ds(g * GT, GT)],
                                     parts[:, n, :, :]).then_inc(saved[n], 16)
                sp.wait_ge(const, 4)
                for n in range(4):
                    sp.wait_ge(saved[n], 16 * NG + SV)

                def load(f, slot, g):
                    if f is not None:
                        sp.wait_ge(st_ready, NU * (f - 2) + (g + 1) * NU // 2)
                    tok = ds((slot if f is None else f) * L, L)
                    hs = slice(g * HH, (g + 1) * HH)
                    q_rows, k_rows = (qk_parts[2 * i + g].rearrange("(r h) t -> r h t", h=HH)[:, :, tok] for i in range(2))
                    done = qk_loaded[slot][g]
                    sp.dma_start(q3[0:2 * HD, slot, hs, :], q_rows[0:2 * HD]).then_inc(done, 16)
                    sp.dma_start(q3[2 * HD:PR, slot, hs, :], q_rows[0:HD]).then_inc(done, 16)
                    sp.dma_start(k3[0:HD, slot, hs, :], k_rows[0:HD]).then_inc(done, 16)
                    sp.dma_start(k3[HD:PR, slot, hs, :], k_rows[0:2 * HD]).then_inc(done, 16)

                def maxima_rows(f, slot, g):
                    sp.wait_ge(mx_saved[g], 16 * (f + 1))
                    sp.dma_start(q3[PR:PR + MR, slot, g * HH:(g + 1) * HH, :],
                                 mx_parts[ds(f, 1), g].rearrange("f c (h l) -> (f c) h l", l=L)).then_inc(mx_rows[g], 16)

                for slot in range(2):
                    for g in range(2):
                        load(None, slot, g)
                for g in range(2):
                    maxima_rows(0, 0, g)
                with sp.Fori(0, B // 2 - 1) as j:
                    for i in range(2):
                        for g in range(2):
                            load(2 * j + 2 + i, i, g)
                            maxima_rows(2 * j + 1 + i, (1 + i) % 2, g)
                for g in range(2):
                    maxima_rows(B - 1, 1, g)

            @block.gpsimd
            def _(pool):
                pool.sem_inc(neg_parts, NP)
                pool.memset(ones[:, :], 1.0).then_inc(const, 1)
                pool.memset(unit[:, :], 1.0).then_inc(const, 1)
                pool.memset(v_all[:, :, :, HD:V1], 1.0).then_inc(const, 1)
                pool.wait_ge(const, 3)
                pool.memset(k3[32:64, :, :, :], ROW).then_inc(const, 1)
                pool.wait_ge(const, 4)
                pool.wait_ge(scales, 1)
                pool.partition_all_reduce(ball[:, :], bmax[:, :], P, bass.bass_isa.ReduceOp.max).then_inc(all_ready, 1)

                def negate(f, g):
                    pool.wait_ge(mx_rows[g], 16 * f + RW)
                    pool.wait_ge(neg_ready, 2 * f + g + 1 + NR)
                    for i in range(MR):
                        last = i == MR - 1
                        pool.tensor_tensor(negs[g][:, i, :], neg[:, :], unit[:, :], ALU.mult).then_inc(neg_parts if last else neg_dve, 1)
                        if not last:
                            pool.wait_ge(neg_dve, 4 * (2 * f + g) + 2 * i + 1)
                            pool.tensor_tensor(neg[:, :], neg[:, :], negs[g][:, i, :], ALU.subtract).then_inc(neg_dve, 1)
                            pool.wait_ge(neg_dve, 4 * (2 * f + g) + 2 * i + 2)
                        else:
                            pool.wait_ge(neg_parts, 2 * f + g + 1 + NP)
                    pool.dma_start(mx_parts[ds(f, 1), g].rearrange("f c (x l) -> (f x) c l", l=P), negs[g][:, :, :]).then_inc(mx_saved[g], 16)

                pool.sem_inc(mx_rows[0], RW)
                pool.sem_inc(mx_rows[1], RW)
                with pool.Fori(0, B) as f:
                    for g in range(2):
                        negate(f, g)

            @block.tensor
            def _(pe):
                pe.sem_inc(nbt_ready, NB)
                pe.sem_inc(pv_ready, PV)
                with pe.Fori(0, NG) as g:
                    for n in range(4):
                        pe.wait_ge(full_ready, 4 * g + n - 1 + FU)
                        split_matmul(pe, bank[n % 2][:, :], lambda i, k: wqkv[:, i, k, n * P:(n + 1) * P],
                                     lambda i, k: c.xT[:, i, k, ds(g * GT, GT)]).then_inc(proj_ready, 1)
                    for n in range(2):
                        pe.wait_ge(v_done, 2 * g + n - 1 + VD)
                        for t in range(2):
                            mm = split_matmul(pe, bank[2 + n][:, t * D:(t + 1) * D],
                                              lambda i, k: c.xT[:, i, k, ds(g * GT + (2 * n + t) * P, P)],
                                              lambda i, k: wqkv[:, i, k, 2 * D:3 * D])
                        mm.then_inc(v_ready, 1)

                def scores(f, slot, u):
                    t, h, n = trio(u // 3)[u % 3]
                    w_ = (t + 1) * P
                    if u % (NU // 2) == 0:
                        pe.wait_ge(qk_loaded[slot][u // (NU // 2)], 64 * (f // 2 + 1) if isinstance(f, int) else 32 * (f - slot) + 64)
                    pe.wait_ge(max_done, NU * f + u - 1 + MD)
                    bk = bank[u % 2]
                    diag = bk[:, :].rearrange("p (j l) -> p j l", l=w_)[:, :, t * P:w_]
                    pe.matmul(diag, c.identb[:, :], c.after[:, :].unsqueeze(1).broadcast_to([P, n, P]),
                              start=True, stop=False, skip_group_check=True)
                    for j in range(n):
                        mm = pe.matmul(bk[:, j * w_:(j + 1) * w_], q3[0:PR, slot, h + j, t * P:(t + 1) * P],
                                       k3[0:PR, slot, h + j, 0:w_], start=False, stop=True, skip_group_check=True)
                    mm.then_inc(s_ready, 1)

                def maxima_turn(f, g):
                    pe.wait_ge(max_done, NU * f + (g + 1) * NU // 2 + MD)
                    pe.wait_ge(neg_ready, 2 * f + g + NR)
                    pe.transpose(bank[6][0:HH * TB, 0:P], mx[:, g, :, :].rearrange("p h t -> p (h t)"), c.ident[:, :]).then_inc(nbt_ready, 1)

                def shifted(b, slot, u):
                    qd, n = divmod(u, 3)
                    if u % (NU // 2) == 0:
                        pe.wait_ge(mx_rows[u // (NU // 2)], 16 * (b + 1) + RW)
                    pe.wait_ge(exp_done, NU * b + u - 1 + XP)
                    lo, w_, nj = (0, L, 2) if n < 2 else (P, P, 4)
                    bk = bank[2 + u % 2]
                    diag = bk[:, :].rearrange("p (j l) -> p j l", l=w_)[:, :, 0:P]
                    pe.matmul(diag, c.identb[:, :], c.before[:, :].unsqueeze(1).broadcast_to([P, nj, P]),
                              start=True, stop=False, skip_group_check=True)
                    for j in range(nj):
                        h = 4 * qd + (2 * n + j if n < 2 else j)
                        mm = pe.matmul(bk[:, j * w_:(j + 1) * w_], k3[0:PR + MR, slot, h, lo:lo + P],
                                       q3[0:PR + MR, slot, h, lo:lo + w_], start=False, stop=True, skip_group_check=True)
                    mm.then_inc(st_ready, 1)

                def values(b, qd):
                    if qd == 0:
                        pe.wait_ge(y_done, b + YD)
                    pe.wait_ge(exp_done, NU * b + 3 * (qd + 1) + XP)
                    for j in range(4):
                        h = 4 * qd + j
                        early = pT[:, (3 * qd + j // 2) % ES, (j % 2) * L:(j % 2 + 1) * L]
                        late = pT[:, (3 * qd + 2) % ES, j * P:(j + 1) * P]
                        v0, v1 = (v_all[:, ds(TB * b + s, 1), h, :].rearrange("p a d -> p (a d)") for s in range(2))
                        o = slice(h * V1, (h + 1) * V1)
                        pe.matmul(bank[4][:, o], early[:, 0:P], v0, start=True, stop=True)
                        pe.matmul(bank[5][:, o], early[:, P:L], v0, start=True, stop=False)
                        mm = pe.matmul(bank[5][:, o], late, v1, start=False, stop=True)
                    mm.then_inc(pv_ready, 1)

                def y_turn(b):
                    pe.wait_ge(y_done, b + 1 + YD)
                    pe.wait_ge(x_added, b + XA)
                    for t in range(TB):
                        for k in range(KD):
                            mm = pe.transpose(bank[7][:, (2 * t + k) * P:(2 * t + k + 1) * P], y[:, t, k * P:(k + 1) * P], c.ident[:, :])
                    mm.then_inc(yT_ready, 1)

                def project(b):
                    pe.wait_ge(yT_done, b + 1)
                    for t in range(TB):
                        o = bank[7][:, t * D:(t + 1) * D]
                        pe.matmul(o, ones[:, :], bo[:, :], start=True, stop=False)
                        for k in range(KD):
                            mm = pe.matmul(o, yT[:, k, t * P:(t + 1) * P], wo[:, k, :], start=False, stop=(k == KD - 1))
                    mm.then_inc(out_ready, 1)

                def turn(b, slot, first, more):
                    for qd in range(NQ):
                        for n in range(3):
                            shifted(b, slot, 3 * qd + n)
                            if more:
                                scores(b + 1, 1 - slot, 3 * qd + n)
                        if qd:
                            values(b, qd - 1)
                        if more and qd == 2:
                            maxima_turn(b + 1, 0)
                        if not first and qd == 0:
                            y_turn(b - 1)
                        if not first and qd == 1:
                            project(b - 1)
                    values(b, NQ - 1)
                    if more:
                        maxima_turn(b + 1, 1)

                pe.wait_ge(loaded, 64)
                pe.wait_ge(const, 4)
                for u in range(NU):
                    scores(0, 0, u)
                    if u == 8:
                        maxima_turn(0, 0)
                maxima_turn(0, 1)
                pe.wait_ge(v_done, 2 * NG + VD)
                turn(0, 0, True, True)
                with pe.Fori(0, B // 2 - 1) as j:
                    turn(2 * j + 1, 1, False, True)
                    turn(2 * j + 2, 0, False, True)
                turn(B - 1, 1, False, False)
                y_turn(B - 1)
                project(B - 1)

            @block.scalar
            def _(act):
                act.sem_inc(neg_ready, NR)
                act.sem_inc(full_ready, FU)
                act.sem_inc(exp_done, XP)
                act.wait_ge(loaded, 64)
                for n in range(4):
                    act.sem_inc(saved[n], SV)
                act.wait_ge(scales, 7)
                with act.Fori(0, NG) as g:
                    for n in range(4):
                        act.wait_ge(proj_ready, 4 * g + n + 1)
                        act.wait_ge(low_ready, 4 * g + n - 1 + LO)
                        act.activation(full[:, n % 2, :], bank[n % 2][:, :], ACT.Identity, bias=bqk[:, n:n + 1], scale=fold[:, 0:1])\
                            .then_inc(full_ready, 1)
                        act.wait_ge(full_ready, 4 * g + n + 1 + FU)
                        act.wait_ge(saved[n], 16 * g + SV)
                        act.activation(parts[:, n, 0, :], full[:, n % 2, :], ACT.Copy).then_inc(high_ready, 1)

                def exps(b, u):
                    act.wait_ge(st_ready, NU * b + u + 1)
                    if u % 3 == 0:
                        act.wait_ge(pv_ready, NQ * b + u // 3 - 1 + PV)
                    act.activation(pT[:, u % ES, :], bank[2 + u % 2][:, :], ACT.Exp, scale=escale[:, 0:1]).then_inc(exp_done, 1)

                def y_copy(b):
                    act.wait_ge(yT_ready, b + 1)
                    act.activation(yT[:, :, :].rearrange("p k (t c) -> p k t c", t=TB),
                                   bank[7][:, :].rearrange("p (t k c) -> p k t c", t=TB, k=KD), ACT.Copy).then_inc(yT_done, 1)

                def negate(f, g):
                    act.wait_ge(nbt_ready, 2 * f + g + 1 + NB)
                    act.wait_ge(neg_parts, 2 * f + g + NP)
                    act.activation(neg[:, :], bank[6][0:HH * TB, 0:P], ACT.Copy, scale=-1.0 / ROW).then_inc(neg_ready, 1)

                def turn(b, first, more):
                    for u in range(NU):
                        exps(b, u)
                        if u == 1:
                            negate(b, 1)
                        if more and u == 9:
                            negate(b + 1, 0)
                        if u == 3 and not first:
                            y_copy(b - 1)

                negate(0, 0)
                turn(0, True, True)
                with act.Fori(1, B - 1) as b:
                    turn(b, False, True)
                turn(B - 1, False, False)
                y_copy(B - 1)

            @block.vector
            def _(dve):
                dve.sem_inc(low_ready, LO)
                dve.sem_inc(v_done, VD)
                dve.sem_inc(max_done, MD)
                dve.sem_inc(y_done, YD)
                dve.sem_inc(x_added, XA)
                dve.wait_ge(loaded, 64)
                dve.wait_ge(const, 4)
                dve.reduce_max(bmax[:, :], bqk[:, :], axis=AXX, apply_absolute_value=True).then_inc(scales, 1)
                dve.wait_ge(all_ready, 1)
                dve.scalar_tensor_tensor(bound[:, :], undo, 2.0 * D * TOP * X_SCALE, ball[:, :], ALU.mult, ALU.add).then_inc(scales, 1)
                dve.wait_ge(scales, 2)
                dve.tensor_scalar(bound[:, :], bound[:, :], 2.0 ** -20, None, ALU.max).then_inc(scales, 1)
                dve.wait_ge(scales, 3)
                dve.tensor_scalar(bound[:, :].bitcast(I32), bound[:, :].bitcast(I32), EXPONENT, None, ALU.bitwise_and).then_inc(scales, 1)
                dve.wait_ge(scales, 4)
                dve.tensor_scalar(power[:, :], bound[:, :], 1.0 / QTOP, None, ALU.mult).then_inc(scales, 1)
                dve.wait_ge(scales, 5)
                dve.reciprocal(scale[:, :], power[:, :]).then_inc(scales, 1)
                dve.scalar_tensor_tensor(escale[:, :], power[:, :], SCALE, power[:, :], ALU.mult, ALU.mult).then_inc(inv_done, 1)
                dve.wait_ge(scales, 6)
                dve.tensor_scalar(bqk[:, :], bqk[:, :], scale[:, 0:1], None, ALU.mult).then_inc(inv_done, 1)
                dve.wait_ge(inv_done, 2)
                dve.tensor_tensor(fold[:, :], scale[:, :], undo, ALU.mult).then_inc(scales, 1)
                with dve.Fori(0, NG) as g:
                    for n in range(4):
                        dve.wait_ge(high_ready, 4 * g + n + 1)
                        dve.tensor_tensor(parts[:, n, 1, :], full[:, n % 2, :], parts[:, n, 0, :], ALU.subtract).then_inc(low_ready, 1)
                    for n in range(2):
                        dve.wait_ge(v_ready, 2 * g + n + 1)
                        for t in range(2):
                            ins = dve.scalar_tensor_tensor(
                                v_all[:, ds(4 * g + 2 * n + t, 1), :, 0:HD].rearrange("p a h d -> p (a h) d"),
                                bank[2 + n][:, t * D:(t + 1) * D].rearrange("p (h d) -> p h d", d=HD), undo,
                                bv[:, :].rearrange("p (h d) -> p h d", d=HD), ALU.mult, ALU.add)
                        ins.then_inc(v_done, 1)

                def maxima(f, u):
                    t, h, n = trio(u // 3)[u % 3]
                    g, hh = divmod(h, HH)
                    if u % (NU // 2) == 0:
                        dve.wait_ge(nbt_ready, 2 * f + g - 1 + NB)
                    dve.wait_ge(s_ready, NU * f + u + 1)
                    dve.reduce_max(mx[:, g, hh:hh + n, t], bank[u % 2][:, :].rearrange("p (j l) -> p j l", j=n), axis=AXX).then_inc(max_done, 1)

                def divide(b):
                    dve.wait_ge(pv_ready, NQ * (b + 1) + PV)
                    for t in range(TB):
                        o = bank[4 + t][:, 0:AH * V1].rearrange("p (h d) -> p h d", d=V1)
                        ins = dve.reciprocal(rden[:, t, :], o[:, :, HD])
                    ins.then_inc(inv_done, 1)
                    dve.wait_ge(inv_done, b + 3)
                    for t in range(TB):
                        o = bank[4 + t][:, 0:AH * V1].rearrange("p (h d) -> p h d", d=V1)
                        ins = dve.tensor_tensor(y[:, t, :].rearrange("p (h d) -> p h d", d=HD), o[:, :, 0:HD],
                                                rden[:, t, :].unsqueeze(2).broadcast_to([P, AH, HD]), ALU.mult)
                    ins.then_inc(y_done, 1)

                def add(b):
                    dve.wait_ge(out_ready, b + 1)
                    xt = c.x[:, ds(TB * b, TB), :].rearrange("p a d -> p (a d)")
                    dve.tensor_tensor(xt, xt, bank[7][:, :], ALU.add).then_inc(x_added, 1)

                def turn(b, first, more):
                    for u in range(NU):
                        if more:
                            maxima(b + 1, u)
                        if u == 8 and not first:
                            add(b - 1)
                    if not first:
                        dve.wait_ge(yT_ready, b)
                    divide(b)

                for u in range(NU):
                    maxima(0, u)
                turn(0, True, True)
                with dve.Fori(1, B - 1) as b:
                    turn(b, False, True)
                turn(B - 1, False, False)
                add(B - 1)
        p.retire()


def expert_constants(nc, c, m, a, scale, unscale):
    undo, hidden, out, both = m.sb("undo_x", [P, 5]), m.sb("hidden_scale", [P, 1]), m.sb("out_scale", [P, 1]), m.sb("gate_up", [P, 1])
    power, folded = m.sb("hidden_power", [P, 1]), m.sb("hidden_folded", [P, 1])
    undo_ready, both_ready, power_ready, inverse_ready, folded_ready, loaded = (
        m.sem("ec_" + n) for n in ("undo", "both", "power", "inverse", "folded", "loaded"))
    with nc.Block() as block:
        @block.sync
        def _(sp):
            sp.dma_start(c.spread[:, :], a["spread"]).then_inc(loaded, 16)
            sp.wait_ge(loaded, 16)

        @block.vector
        def _(dve):
            dve.tensor_scalar(undo[:, :], unscale[:, :], 1.0 / X_SCALE, None, ALU.mult).then_inc(undo_ready, 1)
            dve.tensor_tensor(both[:, :], unscale[:, 1:2], unscale[:, 2:3], ALU.mult).then_inc(both_ready, 1)
            dve.wait_ge(both_ready, 1)
            dve.tensor_scalar(power[:, :], both[:, :], (2 * D * TOP) ** 2 / 2.0 ** 15, None, ALU.mult).then_inc(power_ready, 1)
            dve.wait_ge(power_ready, 1)
            dve.reciprocal(hidden[:, :], power[:, :]).then_inc(inverse_ready, 1)
            dve.tensor_tensor(out[:, :], power[:, :], unscale[:, 3:4], ALU.mult).then_inc(inverse_ready, 1)
            dve.wait_ge(undo_ready, 1)
            dve.wait_ge(inverse_ready, 2)
            dve.tensor_tensor(folded[:, :], hidden[:, :], undo[:, 2:3], ALU.mult).then_inc(folded_ready, 1)
            dve.wait_ge(folded_ready, 1)
    return {"router": undo[:, 0:1], "gate": undo[:, 1:2], "hidden": folded[:, 0:1], "out": out[:, 0:1], "qkv": undo[:, 4:5]}


def build(nc, a, out):
    with ExitStack() as stack:
        c = Core(nc, stack)
        c.bank = [stack.enter_context(nc.psum_tensor(f"bank{i}", [P, 512], F32)) for i in range(8)]
        c.x = c.sb("x", [P, NT, D])
        c.xT = c.sb("xT", [P, 2, KD, T], F16)
        c.ident = c.sb("ident", [P, P])
        c.identb = c.sb("identb", [P, P], BF16)
        c.before = c.sb("before", [P, P], BF16)
        c.after = c.sb("after", [P, P], BF16)
        c.earlier = c.sb("earlier", [P, P], BF16)
        c.onesb = c.sb("onesb", [P, P], BF16)
        loaded = c.sem("x_loaded")
        stored = c.sem("stored")
        xv = a["x"].rearrange("(t p) d -> p t d", p=P)
        with nc.Block() as block:
            @block.sync
            def _(sp):
                sp.dma_start(c.x[:, :, :], xv).then_inc(loaded, 16)
                sp.dma_start(c.ident[:, :], a["ident"]).then_inc(loaded, 16)
                sp.dma_start(c.identb[:, :], a["identb"]).then_inc(loaded, 16)
                sp.dma_start(c.before[:, :], a["before"]).then_inc(loaded, 16)
                sp.dma_start(c.after[:, :], a["after"]).then_inc(loaded, 16)
                sp.dma_start(c.earlier[:, :], a["earlier"]).then_inc(loaded, 16)
                sp.dma_start(c.onesb[:, :], a["onesb"]).then_inc(loaded, 16)
                sp.wait_ge(loaded, 112)
        normalise(nc, "n1", c)
        mixer(nc, c, a)
        m = Core(nc, stack)
        c.spread = m.sb("spread", [PARTS * E, E * FI], BF16)
        w_gate, w_up = (m.sb(n, [P, 2, KD, E * FI], F16) for n in ("w_gate", "w_up"))
        w_down, w_router = m.sb("w_down", [P, 2, FT, D], F16), m.sb("w_router", [P, 2, KD, E], F16)
        wqkv = m.sb("wqkv", [P, 2, KD, 3 * D], F16)
        flat = lambda t: t[:, :, :].rearrange("p k n -> p (k n)")
        flat2 = lambda t: t[:, :, :, :].rearrange("p i k n -> p i (k n)")
        scale, unscale = split_weights(nc, "ew", m, [(n, flat(a["w_" + n]), flat2(t)) for n, t in (
            ("router", w_router), ("gate", w_gate), ("up", w_up), ("down", w_down), ("qkv", wqkv))])
        k = expert_constants(nc, c, m, a, scale, unscale)
        ex = (w_gate, w_up, w_down, w_router, k)
        normalise(nc, "n2", c)
        experts(nc, c, "e1", *ex)
        normalise(nc, "n3", c)
        attention(nc, c, a, wqkv, k["qkv"])
        normalise(nc, "n4", c)
        experts(nc, c, "e2", *ex)
        with nc.Block() as block:
            @block.sync
            def _(sp):
                sp.dma_start(out.rearrange("(t p) d -> p t d", p=P), c.x[:, :, :]).then_inc(stored, 16)
                sp.wait_ge(stored, 16)


def kernel(**inputs):
    import numpy as np
    import concourse.bacc as bacc
    from concourse import mybir as mb
    from concourse.bass_utils import run_bass_kernel_spmd as run

    import ml_dtypes
    bf = ml_dtypes.bfloat16
    g = lambda n: np.asarray(inputs[n])
    w_in = g("L0_attn_a_W_in")
    order = np.arange(D).reshape(2, AH // 2, HD).transpose(0, 2, 1).reshape(D)
    order = np.concatenate([order, D + order, 2 * D + np.arange(D)])
    w_qkv = g("L0_attn_b_w_qkv")[:, order].reshape(KD, P, 3 * D).transpose(1, 0, 2)
    b_qkv = g("L0_attn_b_b_qkv")[order]
    arrays = {
        "x": g("L0_attn_a_hidden_states").reshape(T, D),
        "w_in": w_in.T.reshape(KD, P, PROJ).transpose(1, 0, 2),
        "conv_w": g("L0_attn_a_conv_w").reshape(CT, P, TAPS).transpose(1, 0, 2),
        "conv_b": g("L0_attn_a_conv_b").reshape(CT, P).T,
        "dt_bias": g("L0_attn_a_dt_bias").reshape(H, 1),
        "A_log": g("L0_attn_a_A_log").reshape(H, 1),
        "D": g("L0_attn_a_D_param").reshape(H),
        "norm_w": g("L0_attn_a_norm_w").reshape(XT, P).T,
        "w_out": g("L0_attn_a_W_out").T.reshape(XT, P, D).transpose(1, 0, 2),
        "ident": np.eye(P, dtype=np.float32),
        "identb": np.eye(P).astype(bf),
        "before": (NEG * np.tril(np.ones((P, P)), -1)).astype(bf),
        "after": (NEG * np.triu(np.ones((P, P)), 1)).astype(bf),
        "earlier": np.triu(np.ones((P, P)), 1).astype(bf),
        "onesb": np.ones((P, P)).astype(bf),
        "spread": np.tile(np.repeat(np.eye(E), FI, axis=1), (PARTS, 1)).astype(bf),
        "w_router": g("L0_ffn_gate_w").reshape(KD, P, E).transpose(1, 0, 2),
        "w_gate": g("L0_ffn_w_gate").transpose(1, 0, 2).reshape(KD, P, E * FI).transpose(1, 0, 2),
        "w_up": g("L0_ffn_w_up").transpose(1, 0, 2).reshape(KD, P, E * FI).transpose(1, 0, 2),
        "w_down": g("L0_ffn_w_down").reshape(FT, P, D).transpose(1, 0, 2),
        "w_qkv": w_qkv,
        "bqk": b_qkv[0:2 * D].reshape(4, P).T,
        "bv": b_qkv[2 * D:].reshape(D),
        "wo": g("L0_attn_b_w_out").reshape(KD, P, D).transpose(1, 0, 2),
        "bo": g("L0_attn_b_b_out").reshape(1, D),
    }
    arrays = {n: np.ascontiguousarray(v) for n, v in arrays.items()}
    nc = bacc.Bacc("TRN2", target_bir_lowering=False, num_devices=1)
    a = {n: nc.dram_tensor("in_" + n, v.shape, mb.dt.from_np(v.dtype), kind="ExternalInput").ap() for n, v in arrays.items()}
    out = nc.dram_tensor("out", (T, D), F32, kind="ExternalOutput").ap()
    build(nc, a, out)
    r = run(nc, [{"in_" + n: v for n, v in arrays.items()}], core_ids=[0])
    return r.results[0]["out"].reshape(B, L, D)
```

```python
from contextlib import ExitStack

import concourse.bass as bass
from concourse import mybir

ALU = mybir.AluOpType
ACT = mybir.ActivationFunctionType
AXX = mybir.AxisListType.X
F32 = mybir.dt.float32
BF16 = mybir.dt.bfloat16
F16 = mybir.dt.float16
I32 = mybir.dt.int32
ds = bass.ds

P = 128
B, L, D = 8, 256, 256
T = B * L
NT = T // P
KD = D // P
TB = L // P
NORM_EPS = 1e-5

H, PH, N, TAPS = 32, 64, 128, 4
QUARTERS = P // H
QT = T // QUARTERS
INTER = H * PH
CONV = INTER + 2 * N
PROJ = INTER + CONV + H
CT = CONV // P
XT = INTER // P
HG = 8
NHG = H // HG

AH, HD = 16, 16
SCALE = HD ** -0.5
NEG = -1.0e30

E, FI, TOPK = 32, 96, 8
CAP = 2 * (T * TOPK // E)
FT = E * FI // P
GT_TOK = 512
NG = T // GT_TOK
PARTS = 3

X_SCALE = 1024.0
TOP = 2.0 ** 14
PASSES = ((0, 0), (0, 1), (1, 0))
EXPONENT = 0x7F800000


class Core:

    def __init__(self, nc, stack):
        self.nc, self.stack, self.sems = nc, stack, []

    def sb(self, name, shape, dt=F32):
        return self.stack.enter_context(self.nc.sbuf_tensor(name, shape, dt))

    def sem(self, name):
        self.sems.append(self.stack.enter_context(self.nc.semaphore(name)))
        return self.sems[-1]

    def retire(self):
        with self.nc.Block() as block:
            @block.gpsimd
            def _(pool):
                for s in self.sems:
                    pool.sem_clear(s)


def normalise(nc, tag, c, load=None):
    with ExitStack() as inner:
        ph = Core(nc, inner)
        st = ph.sb(tag + "_stats", [P, NT, 6])
        mean = ph.sb(tag + "_mean", [P, NT])
        half = ph.sb(tag + "_half", [P, NT])
        var = ph.sb(tag + "_var", [P, NT])
        rstd = ph.sb(tag + "_rstd", [P, NT])
        expo = ph.sb(tag + "_expo", [P, NT])
        S = 4
        xh = ph.sb(tag + "_xh", [P, S, D])
        banks = c.bank
        v = ph.sem(tag + "_v")
        expo_set = ph.sem(tag + "_expo_set")
        rstd_ready = ph.sem(tag + "_rstd_ready")
        xh_ready = ph.sem(tag + "_xh_ready")
        turned = ph.sem(tag + "_turned")
        high = ph.sem(tag + "_high")
        copied = ph.sem(tag + "_copied")
        with nc.Block() as block:
            @block.vector
            def _(dve):
                if load is not None:
                    dve.wait_ge(load, 16)
                dve.sem_inc(copied, S)
                for t in range(NT):
                    dve.bn_stats(st[:, t, :], c.x[:, t, :]).then_inc(v, 1)
                dve.wait_ge(v, NT)
                dve.tensor_tensor(mean[:, :], st[:, :, 1], st[:, :, 4], ALU.add).then_inc(v, 1)
                dve.tensor_tensor(half[:, :], st[:, :, 1], st[:, :, 4], ALU.subtract).then_inc(v, 1)
                dve.tensor_tensor(var[:, :], st[:, :, 2], st[:, :, 5], ALU.add).then_inc(v, 1)
                dve.wait_ge(v, NT + 3)
                dve.tensor_scalar(mean[:, :], mean[:, :], 0.5, None, ALU.mult).then_inc(v, 1)
                dve.scalar_tensor_tensor(half[:, :], half[:, :], 0.25, half[:, :], ALU.mult, ALU.mult).then_inc(v, 1)
                dve.tensor_scalar(var[:, :], var[:, :], 1.0 / D, NORM_EPS, ALU.mult, ALU.add).then_inc(v, 1)
                dve.wait_ge(v, NT + 6)
                dve.tensor_tensor(var[:, :], var[:, :], half[:, :], ALU.add).then_inc(v, 1)
                dve.wait_ge(v, NT + 7)
                dve.tensor_scalar(var[:, :], var[:, :], X_SCALE ** -2, None, ALU.mult).then_inc(v, 1)
                dve.wait_ge(rstd_ready, 1)

                def scaled(i, j):
                    dve.wait_ge(turned, S * i + j + 1)
                    dve.tensor_scalar(xh[:, j, :], c.x[:, ds(S * i + j, 1), :].rearrange("p a d -> p (a d)"),
                                      mean[:, ds(S * i + j, 1)], rstd[:, ds(S * i + j, 1)],
                                      ALU.subtract, ALU.mult).then_inc(xh_ready, 1)

                def low(i, j):
                    dve.wait_ge(high, S * i + j + 1)
                    tok = ds((S * i + j) * P, P)
                    dve.tensor_tensor(c.xT[:, 1, :, tok], banks[j][:, 0:D].rearrange("p (k t) -> p k t", k=KD),
                                      c.xT[:, 0, :, tok], ALU.subtract).then_inc(copied, 1)

                for j in range(S):
                    scaled(0, j)
                with dve.Fori(0, NT // S - 1) as i:
                    for j in range(S):
                        scaled(i + 1, j)
                        low(i, j)
                for j in range(S):
                    low(NT // S - 1, j)

            @block.gpsimd
            def _(pool):
                pool.wait_ge(expo_set, 1)
                pool.wait_ge(v, NT + 8)
                pool.tensor_tensor(rstd[:, :], var[:, :], expo[:, :], ALU.pow).then_inc(rstd_ready, 1)

            @block.tensor
            def _(pe):
                pe.sem_inc(turned, S)
                with pe.Fori(0, NT // S) as i:
                    for j in range(S):
                        pe.wait_ge(xh_ready, S * i + j + 1)
                        pe.wait_ge(copied, S * i + j + 1)
                        for k in range(KD):
                            mm = pe.transpose(banks[j][:, k * P:(k + 1) * P], xh[:, j, k * P:(k + 1) * P], c.ident[:, :])
                        mm.then_inc(turned, 1)

            @block.scalar
            def _(act):
                act.activation(expo[:, :], c.ident[:, 0:NT], ACT.Copy, scale=0.0, bias=-0.5).then_inc(expo_set, 1)
                with act.Fori(0, NT // S) as i:
                    for j in range(S):
                        act.wait_ge(turned, S * i + j + 1 + S)
                        act.activation(c.xT[:, 0, :, ds((S * i + j) * P, P)],
                                       banks[j][:, 0:D].rearrange("p (k t) -> p k t", k=KD), ACT.Copy).then_inc(high, 1)

        ph.retire()


class Splitting:

    def __init__(self, nc, tag, c, stack, jobs):
        self.nc, self.tag, self.jobs = nc, tag, jobs
        nj = len(jobs)
        self.scale, self.unscale = c.sb(tag + "_scale", [P, nj]), c.sb(tag + "_unscale", [P, nj])
        self.p = p = Core(nc, stack)
        self.raw = [p.sb(f"{tag}_raw_{name}", [P, parts.shape[2]]) for name, _, parts in jobs]
        self.loaded = [p.sem(f"{tag}_loaded_{name}") for name, _, _ in jobs]
        with nc.Block() as block:
            @block.sync
            def _(sp):
                for i, (_, dram, _) in enumerate(jobs):
                    sp.dma_start(self.raw[i][:, :], dram).then_inc(self.loaded[i], 16)

    def cut(self):
        nc, tag, p, jobs, raw, scale, unscale = self.nc, self.tag, self.p, self.jobs, self.raw, self.scale, self.unscale
        nj = len(jobs)
        mx, most = p.sb(tag + "_max", [P, nj]), p.sb(tag + "_most", [P, nj])
        (max_ready, most_ready, floor_ready, power_ready, inverse_ready, scale_ready, high_ready, low_ready, scaled) = (
            p.sem(f"{tag}_{n}") for n in ("max", "most", "floor", "power", "inverse", "scale", "high", "low", "scaled"))
        CH = 768
        pieces = [(i, a, min(a + CH, parts.shape[2])) for i, (_, _, parts) in enumerate(jobs)
                  for a in range(0, parts.shape[2], CH)]
        with nc.Block() as block:
            @block.gpsimd
            def _(pool):
                def lows(i):
                    for n, (job, a, b) in enumerate(pieces):
                        if job == i and n % 3 == 2:
                            pool.wait_ge(high_ready, n + 1)
                            pool.tensor_tensor(jobs[i][2][:, 1, a:b], raw[i][:, a:b], jobs[i][2][:, 0, a:b], ALU.subtract).then_inc(low_ready, 1)

                for i in range(nj):
                    pool.wait_ge(max_ready, i + 1)
                    pool.partition_all_reduce(most[:, i:i + 1], mx[:, i:i + 1], P, bass.bass_isa.ReduceOp.max).then_inc(most_ready, 1)
                    if i > 1:
                        lows(i - 2)
                for i in range(max(nj - 2, 0), nj):
                    lows(i)

            @block.vector
            def _(dve):
                def largest(i):
                    dve.wait_ge(self.loaded[i], 16)
                    dve.reduce_max(mx[:, i:i + 1], raw[i][:, :], axis=AXX, apply_absolute_value=True).then_inc(max_ready, 1)

                def scales(i):
                    m, o = most[:, i:i + 1], slice(i, i + 1)
                    dve.wait_ge(most_ready, i + 1)
                    dve.tensor_scalar(m, m, 1e-30, None, ALU.max).then_inc(floor_ready, 1)
                    dve.wait_ge(floor_ready, i + 1)
                    dve.tensor_scalar(m.bitcast(I32), m.bitcast(I32), EXPONENT, None, ALU.bitwise_and).then_inc(power_ready, 1)
                    dve.wait_ge(power_ready, i + 1)
                    dve.tensor_scalar(unscale[:, o], m, 1.0 / TOP, None, ALU.mult).then_inc(inverse_ready, 1)
                    dve.wait_ge(inverse_ready, i + 1)
                    dve.reciprocal(scale[:, o], unscale[:, o]).then_inc(scale_ready, 1)

                def lows(i):
                    dve.wait_ge(scale_ready, i + 1)
                    for n, (job, a, b) in enumerate(pieces):
                        if job == i and n % 3 < 2:
                            dve.wait_ge(high_ready, n + 1)
                            dve.scalar_tensor_tensor(jobs[i][2][:, 1, a:b], raw[i][:, a:b], scale[:, i:i + 1], jobs[i][2][:, 0, a:b],
                                                     ALU.mult, ALU.subtract).then_inc(low_ready, 1)

                largest(0)
                for i in range(nj):
                    if i + 1 < nj:
                        largest(i + 1)
                    scales(i)
                    if i:
                        lows(i - 1)
                lows(nj - 1)

            @block.scalar
            def _(act):
                for n, (i, a, b) in enumerate(pieces):
                    act.wait_ge(scale_ready, i + 1)
                    if n % 3 == 2:
                        act.activation(raw[i][:, a:b], raw[i][:, a:b], ACT.Copy, scale=scale[:, i:i + 1]).then_inc(scaled, 1)
                        act.wait_ge(scaled, n // 3 + 1)
                        act.activation(jobs[i][2][:, 0, a:b], raw[i][:, a:b], ACT.Copy).then_inc(high_ready, 1)
                    else:
                        act.activation(jobs[i][2][:, 0, a:b], raw[i][:, a:b], ACT.Copy, scale=scale[:, i:i + 1]).then_inc(high_ready, 1)
        p.retire()


def split_matmul(pe, out, w, x):
    for n, (i, j) in enumerate(PASSES):
        for k in range(KD):
            mm = pe.matmul(out, w(i, k), x(j, k), start=(n == 0 and k == 0),
                           stop=(n == len(PASSES) - 1 and k == KD - 1))
    return mm


def mixer(nc, c, w):
    with ExitStack() as outer:
        m = Core(nc, outer)
        w_in = m.sb("w_in", [P, 2, KD, PROJ], F16)
        w_out = m.sb("w_out", [P, XT, D])
        nrm_w = m.sb("nrm_w", [P, XT])
        conv_w = m.sb("conv_w_sb", [P, CT, TAPS])
        conv_b = m.sb("conv_b_sb", [P, CT])
        d_row = m.sb("d_row", [P, H])
        dt_tok = m.sb("dt_tok", [P, NT, H])
        loaded_in, loaded_dt, loaded_out = m.sem("loaded_in"), m.sem("loaded_dt"), m.sem("loaded_out")
        with ExitStack() as inner:
            weights = Splitting(nc, "mw", m, inner, [("w_in", w["w_in"].rearrange("p k n -> p (k n)"),
                                                      w_in[:, :, :, :].rearrange("p i k n -> p i (k n)"))])
            normalise(nc, "n1", c)
            weights.cut()
            unscale = weights.unscale
        undo = m.sb("undo_in", [P, 1])
        cum_parts = nc.dram_tensor("cum_parts", [PARTS, QT // L, QUARTERS * H, L], BF16, kind="Internal").ap()
        ncum_parts = nc.dram_tensor("neg_cum_parts", [PARTS, QT // L, QUARTERS * H, L], BF16, kind="Internal").ap()

        with ExitStack() as inner:
            p = Core(nc, inner)
            banks = c.bank
            z, a, e, u, lg, dt = (p.sb("pre_" + n, [QUARTERS * H, QT]) for n in ("z", "a", "e", "u", "lg", "dt"))
            r = u
            ones = p.sb("pre_ones", [QUARTERS * H, L])
            dtb, alog, aneg = (p.sb("pre_" + n, [QUARTERS * H, 1]) for n in ("dtb", "alog", "aneg"))
            part = [p.sb(f"pre_part{i}", [QUARTERS * H, QT], BF16) for i in range(PARTS)]
            npart = [p.sb(f"pre_npart{i}", [QUARTERS * H, QT], BF16) for i in range(PARTS)]
            (dt_proj, z_ready, nabs_ready, exp_ready, u_ready, ln_ready, less_ready, safe_ready, inv_ready,
             ratio_ready, tiny_ready, term_ready, sum_ready, dt_ready, a_ready, da_ready, ones_ready, cum_ready,
             part_ready, rest_ready, npart_ready, dt_turned, dt_copied, saved, undo_ready,
             taps_scaled) = (
                p.sem("pre_" + n) for n in (
                    "dt_proj", "z", "nabs", "exp", "u", "ln", "less", "safe", "inv", "ratio", "tiny", "term", "sum",
                    "dt", "a", "da", "ones", "cum", "part", "rest", "npart", "dt_turned", "dt_copied", "saved", "undo", "taps"))
            with nc.Block() as block:
                @block.sync
                def _(sp):
                    sp.dma_start(dtb[:, :], w["dt_bias"]).then_inc(loaded_dt, 16)
                    sp.dma_start(alog[:, :], w["A_log"]).then_inc(loaded_dt, 16)
                    sp.dma_start(conv_w[:, :, :], w["conv_w"]).then_inc(loaded_in, 16)
                    sp.dma_start(conv_b[:, :], w["conv_b"]).then_inc(loaded_in, 16)
                    sp.dma_start(d_row[:, :], w["D"].partition_broadcast(P)).then_inc(loaded_in, 16)
                    sp.dma_start(w_out[:, :, :], w["w_out"]).then_inc(loaded_out, 16)
                    sp.dma_start(nrm_w[:, :], w["norm_w"]).then_inc(loaded_out, 16)

                    def save(dst, src):
                        sp.dma_start(dst.rearrange("s p l -> p s l"), src[:, :].rearrange("p (s l) -> p s l", l=L)).then_inc(saved, 16)

                    for i in range(PARTS):
                        sp.wait_ge(part_ready, i + 1)
                        save(cum_parts[i], part[i])
                        sp.wait_ge(npart_ready, i + 1)
                        save(ncum_parts[i], npart[i])
                    sp.wait_ge(saved, 32 * PARTS)

                @block.gpsimd
                def _(pool):
                    pool.memset(ones[:, :], 1.0).then_inc(ones_ready, 1)

                @block.tensor
                def _(pe):
                    for q in range(QUARTERS):
                        split_matmul(pe, banks[q][q * H:(q + 1) * H, :], lambda i, k: w_in[:, i, k, PROJ - H:PROJ],
                                     lambda i, k: c.xT[:, i, k, q * QT:(q + 1) * QT]).then_inc(dt_proj, 1)
                    pe.wait_ge(dt_ready, 1)
                    for t in range(QT // P):
                        mm = pe.transpose(banks[7][:, t * P:(t + 1) * P], dt[:, t * P:(t + 1) * P], c.ident[:, :])
                    mm.then_inc(dt_turned, 1)

                @block.scalar
                def _(act):
                    act.wait_ge(loaded_dt, 32)
                    act.activation(a[:, 0:1], alog[:, :], ACT.Exp).then_inc(a_ready, 1)
                    act.wait_ge(nabs_ready, 1)
                    act.activation(e[:, :], e[:, :], ACT.Exp).then_inc(exp_ready, 1)
                    act.wait_ge(u_ready, 1)
                    act.activation(lg[:, :], u[:, :], ACT.Ln).then_inc(ln_ready, 1)
                    act.wait_ge(dt_turned, 1)
                    act.activation(dt_tok[:, :, :].rearrange("p (q t) h -> p t q h", q=QUARTERS),
                                   banks[7][:, :].rearrange("p (t q h) -> p t q h", q=QUARTERS, h=H), ACT.Copy).then_inc(dt_copied, 1)
                    for i in range(PARTS):
                        act.wait_ge(part_ready, i + 1)
                        act.activation(npart[i][:, :], part[i][:, :], ACT.Copy, scale=-1.0).then_inc(npart_ready, 1)

                @block.vector
                def _(dve):
                    dve.tensor_scalar(undo[:, :], unscale[:, :], 1.0 / X_SCALE, None, ALU.mult).then_inc(undo_ready, 1)
                    dve.wait_ge(undo_ready, 1)
                    dve.wait_ge(loaded_dt, 32)
                    dve.wait_ge(a_ready, 1)
                    dve.tensor_scalar(aneg[:, :], a[:, 0:1], -1.0, None, ALU.mult).then_inc(a_ready, 1)
                    for q in range(QUARTERS):
                        dve.wait_ge(dt_proj, q + 1)
                        hs = slice(q * H, (q + 1) * H)
                        dve.tensor_scalar(z[hs, :], banks[q][hs, :], undo[hs, 0:1], dtb[hs, 0:1],
                                          ALU.mult, ALU.add).then_inc(z_ready, 1)
                    dve.wait_ge(z_ready, QUARTERS)
                    dve.scalar_tensor_tensor(e[:, :], z[:, :], -1.0, z[:, :], ALU.mult, ALU.min).then_inc(nabs_ready, 1)
                    dve.wait_ge(exp_ready, 1)
                    dve.tensor_scalar(u[:, :], e[:, :], 1.0, None, ALU.add).then_inc(u_ready, 1)
                    dve.wait_ge(ln_ready, 1)
                    dve.tensor_scalar(a[:, :], u[:, :], -1.0, None, ALU.add).then_inc(less_ready, 1)
                    dve.wait_ge(less_ready, 1)
                    dve.scalar_tensor_tensor(r[:, :], a[:, :], 0.0, a[:, :], ALU.is_equal, ALU.add).then_inc(safe_ready, 1)
                    dve.scalar_tensor_tensor(dt[:, :], a[:, :], 0.0, e[:, :], ALU.is_equal, ALU.mult).then_inc(tiny_ready, 1)
                    dve.wait_ge(safe_ready, 1)
                    dve.reciprocal(r[:, :], r[:, :]).then_inc(inv_ready, 1)
                    dve.wait_ge(inv_ready, 1)
                    dve.tensor_tensor(r[:, :], r[:, :], e[:, :], ALU.mult).then_inc(ratio_ready, 1)
                    dve.wait_ge(ratio_ready, 1)
                    dve.tensor_tensor(lg[:, :], lg[:, :], r[:, :], ALU.mult).then_inc(term_ready, 1)
                    dve.wait_ge(term_ready, 1)
                    dve.wait_ge(tiny_ready, 1)
                    dve.tensor_tensor(lg[:, :], lg[:, :], dt[:, :], ALU.add).then_inc(sum_ready, 1)
                    dve.wait_ge(sum_ready, 1)
                    dve.scalar_tensor_tensor(dt[:, :], z[:, :], 0.0, lg[:, :], ALU.max, ALU.add).then_inc(dt_ready, 1)
                    dve.wait_ge(dt_ready, 1)
                    dve.wait_ge(a_ready, 2)
                    dve.tensor_scalar(a[:, :], dt[:, :], aneg[:, 0:1], None, ALU.mult).then_inc(da_ready, 1)
                    dve.wait_ge(da_ready, 1)
                    dve.wait_ge(ones_ready, 1)
                    dve.wait_ge(loaded_in, 48)
                    dve.tensor_scalar(conv_w[:, :, :], conv_w[:, :, :], undo[:, 0:1], None, ALU.mult).then_inc(taps_scaled, 1)
                    for b in range(QT // L):
                        dve.tensor_tensor_scan(z[:, b * L:(b + 1) * L], ones[:, :], a[:, b * L:(b + 1) * L], 0.0,
                                               ALU.mult, ALU.add).then_inc(cum_ready, 1)
                    dve.wait_ge(cum_ready, QT // L)
                    for i in range(PARTS):
                        dve.tensor_copy(part[i][:, :], z[:, :]).then_inc(part_ready, 1)
                        dve.wait_ge(part_ready, i + 1)
                        if i < PARTS - 1:
                            dve.tensor_tensor(z[:, :], z[:, :], part[i][:, :], ALU.subtract).then_inc(rest_ready, 1)
                            dve.wait_ge(rest_ready, i + 1)

            p.retire()

        with ExitStack() as inner:
            mixer_loop(nc, c, w_in, w_out, nrm_w, conv_w, conv_b, d_row, dt_tok, loaded_in, loaded_out,
                       cum_parts, ncum_parts, undo, Core(nc, inner))
        m.retire()


def mixer_loop(nc, c, w_in, w_out, nrm_w, conv_w, conv_b, d_row, dt_tok, loaded_in, loaded_out, cum_parts, ncum_parts, undo, p):
    PAIRS = [(XT, XT + 1)] + [(2 * i, 2 * i + 1) for i in range(XT // 2)]
    NP = len(PAIRS)
    GU = TB * INTER // 512
    XU = TB * XT // 4
    EU = 3 * H // 4
    TR = EU // 3
    ES = 6
    EARLY = 8

    cv = p.sb("cv", [P, CT, L])
    stage = p.sb("stage", [P, 2, 512])
    xdt = p.sb("xdt", [P, TB, INTER])
    yg = p.sb("yg", [P, TB, INTER])
    gate = p.sb("gate", [P, TB, INTER])
    sc = p.sb("sc", [P, ES, 512])
    gsb = p.sb("gsb", [P, 3 * P])
    gT = p.sb("gT", [P, TB, XT, P])
    lrow = p.sb("lrow", [2 * PARTS, 2, HG, L], BF16)
    rrow = p.sb("rrow", [2 * PARTS, 2, HG, L], BF16)
    ssp = p.sb("ssp", [P, TB, NHG])
    junk = p.sb("junk", [P, TB, 512], BF16)
    ms = p.sb("ms", [P, TB])
    rs = p.sb("rs", [P, TB])
    expo = p.sb("m_expo", [P, TB])
    bank = c.bank

    (w_scaled, consts, pair_ready, tap_done, tap_dve, conv_done, silu_done, gate_ready, gate_done, g_ready, g_done,
     xturn_ready, xturn_done, turn_ready, turn_done, xdt_done, dx_done, e_ready, exp_done, m_dve, m_pool, y_done,
     y_added, gated, squared, out_ready, x_added, ss_ready, ms_ready, rs_ready) = (p.sem("mx_" + n) for n in (
         "w_scaled", "consts", "pair_ready", "tap_done", "tap_dve", "conv_done", "silu_done", "gate_ready",
         "gate_done", "g_ready", "g_done", "xturn_ready", "xturn_done", "turn_ready", "turn_done", "xdt_done",
         "dx_done", "e_ready", "exp_done", "m_dve", "m_pool", "y_done", "y_added", "gated", "squared", "out_ready",
         "x_added", "ss_ready", "ms_ready", "rs_ready"))
    rows = [p.sem("rows0"), p.sem("rows1")]
    START = {"xturn_done": 1, "turn_done": 2, "xdt_done": 2, "dx_done": 2, "e_ready": 12, "exp_done": 2, "y_done": 2,
             "y_added": 1, "gated": 1, "squared": 2, "out_ready": 2, "x_added": 1, "gate_done": 1, "m_pool": 1}
    (XTD, TD, XD, DX, ER, XP, YD, YA, GTD, SQ, OR, XA, GD, MP) = START.values()

    with nc.Block() as block:
        @block.sync
        def _(sp):
            sp.wait_ge(consts, 3)
            with sp.Fori(0, QUARTERS) as k:
                for i in range(QT // L):
                    b = QT // L * k + i
                    for g in range(NHG):
                        heads = ds(k * H + g * HG, HG)
                        sp.wait_ge(e_ready, EU * b + 6 * g - 6 + ER)
                        sp.dma_start(rrow[0:2 * PARTS:2, g % 2, :, :], cum_parts[:, i, heads, :]).then_inc(rows[g % 2], 16)
                        sp.dma_start(lrow[1:2 * PARTS:2, g % 2, :, :], ncum_parts[:, i, heads, :]).then_inc(rows[g % 2], 16)

        @block.tensor
        def _(pe):
            pe.sem_inc(e_ready, ER)
            pe.sem_inc(y_done, YD)
            pe.sem_inc(out_ready, OR)
            pe.wait_ge(loaded_in, 48)

            def pair(f, u):
                if u < 2:
                    pe.wait_ge(gate_done, GU * f + GD)
                else:
                    pe.wait_ge(conv_done, NP * f + u - 1)
                for j, ch in enumerate(PAIRS[u]):
                    o = INTER + ch * P
                    mm = split_matmul(pe, bank[u % 2][:, j * L:(j + 1) * L], lambda i, k: w_in[:, i, k, o:o + P],
                                      lambda i, k: c.xT[:, i, k, ds(f * L, L)])
                mm.then_inc(pair_ready, 1)

            def b_times_c(f):
                pe.wait_ge(silu_done, NP * f + 1)
                pe.wait_ge(turn_done, XU * f + TD)
                pe.matmul(bank[6][:, 0:L], cv[:, XT, 0:P], cv[:, XT + 1, :], start=True, stop=True)
                pe.matmul(bank[6][:, L:L + P], cv[:, XT, P:L], cv[:, XT + 1, P:L], start=True, stop=True).then_inc(g_ready, 1)

            def gates(f, g):
                t, n = divmod(g, GU // TB)
                u = NP + g
                if g < 2:
                    pe.wait_ge(conv_done, NP * f + u - 1)
                else:
                    pe.wait_ge(gate_done, GU * f + g - 1 + GD)
                split_matmul(pe, bank[u % 2][:, :], lambda i, k: c.xT[:, i, k, ds(f * L + t * P, P)],
                             lambda i, k: w_in[:, i, k, n * 512:(n + 1) * 512]).then_inc(gate_ready, 1)

            def x_turn(f, v):
                q, t = divmod(v, TB)
                if v == 0:
                    pe.wait_ge(silu_done, NP * (f + 1))
                    pe.wait_ge(g_done, f + 1)
                elif v == 1:
                    pe.wait_ge(turn_done, XU * f + TD)
                else:
                    pe.wait_ge(xturn_done, XU * f + v - 1 + XTD)
                for j in range(4):
                    mm = pe.transpose(bank[6 + v % 2][:, j * P:(j + 1) * P], cv[:, 4 * q + j, t * P:(t + 1) * P], c.ident[:, :])
                mm.then_inc(xturn_ready, 1)

            def scores(b, tr, units=range(3)):
                g, first = tr // 2, 4 * (tr % 2)
                if tr % 2 == 0 and 0 in units:
                    pe.wait_ge(rows[g % 2], 64 * b + 32 * (g // 2 + 1))
                for n in units:
                    u = 3 * tr + n
                    pe.wait_ge(exp_done, EU * b + u - 1 + XP)
                    cols = bank[2 + u % 2][:, :].rearrange("p (j l) -> p j l", l=(L if n < 2 else P))[:, :, 0:P]
                    nj = 2 if n < 2 else 4
                    pe.matmul(cols, c.identb[:, :], c.before[:, :].unsqueeze(1).broadcast_to([P, nj, P]),
                              start=True, stop=False, skip_group_check=True)
                    for j in range(nj):
                        h = first + (2 * n + j if n < 2 else j)
                        lo, w = (0, L) if n < 2 else (P, P)
                        mm = pe.matmul(bank[2 + u % 2][:, j * w:(j + 1) * w], lrow[:, g % 2, h, lo:lo + P],
                                       rrow[:, g % 2, h, lo:lo + w], start=False, stop=True, skip_group_check=True)
                    mm.then_inc(e_ready, 1)

            def outputs(b, tr):
                g, first = tr // 2, 4 * (tr % 2)
                if tr % 2 == 0:
                    pe.wait_ge(y_added, NHG * b + g + YA)
                    pe.wait_ge(xdt_done, XU * b + 2 * (g + 1) + XD)
                if tr == 0:
                    pe.wait_ge(x_added, TB * b + XA)
                pe.wait_ge(m_dve, 2 * (TR * b + tr + 1))
                pe.wait_ge(m_pool, TR * b + tr + 1 + MP)
                base = 3 * (tr % 2)
                for j in range(4):
                    col = (first + j) * PH
                    ch = g * 512 + col
                    early = sc[:, base + j // 2, (j % 2) * L:(j % 2 + 1) * L]
                    late = sc[:, base + 2, j * P:(j + 1) * P]
                    pe.matmul(bank[4][:, col:col + PH], early[:, 0:P], xdt[:, 0, ch:ch + PH], start=True, stop=True)
                    pe.matmul(bank[5][:, col:col + PH], early[:, P:L], xdt[:, 0, ch:ch + PH], start=True, stop=False)
                    mm = pe.matmul(bank[5][:, col:col + PH], late, xdt[:, 1, ch:ch + PH], start=False, stop=True)
                mm.then_inc(y_done, 1)

            def g_turn(b, t, q):
                v = t * NHG + q
                pe.wait_ge(gated, TB * NHG * b + 2 * q + t + 1 + GTD)
                if v < 2:
                    pe.wait_ge(xturn_done, XU * b + XU - 1 + v + XTD)
                else:
                    pe.wait_ge(turn_done, XU * b + v - 1 + TD)
                for j in range(4):
                    ch = 4 * q + j
                    mm = pe.transpose(bank[6 + v % 2][:, j * P:(j + 1) * P], yg[:, t, ch * P:(ch + 1) * P], c.ident[:, :])
                mm.then_inc(turn_ready, 1)

            def project(b, t, parts=range(4)):
                if t == 0:
                    pe.wait_ge(y_added, NHG * (b + 1) + YA)
                if 0 in parts:
                    pe.wait_ge(turn_done, XU * b + (t + 1) * NHG + TD)
                for ch in (4 * i + j for i in parts for j in range(4)):
                    mm = pe.matmul(bank[4 + t][:, 0:D], gT[:, t, ch, :], w_out[:, ch, :],
                                   start=(ch == 0), stop=(ch == XT - 1))
                if 3 in parts:
                    mm.then_inc(out_ready, 1)

            def turn(b, more):
                for tr in range(TR):
                    if tr + 1 < TR:
                        scores(b, tr + 1, (0, 1))
                    if more and tr < EARLY:
                        pair(b + 1, tr)
                    if tr + 1 < TR:
                        scores(b, tr + 1, (2,))
                    outputs(b, tr)
                for q in range(NHG):
                    if more and EARLY + q < NP:
                        pair(b + 1, EARLY + q)
                    g_turn(b, 0, q)
                for q in range(NHG):
                    g_turn(b, 1, q)
                    if more and q % 2:
                        gates(b + 1, q // 2)
                if more:
                    b_times_c(b + 1)
                project(b, 0)
                if more:
                    x_turn(b + 1, 0)
                    x_turn(b + 1, 1)
                    gates(b + 1, 2)
                    x_turn(b + 1, 2)
                    gates(b + 1, 3)
                    x_turn(b + 1, 3)
                    for i in range(4):
                        project(b, 1, (i,))
                        x_turn(b + 1, 4 + i)
                    for g in range(4, GU):
                        gates(b + 1, g)
                    scores(b + 1, 0)
                else:
                    project(b, 1)

            for u in range(NP):
                pair(0, u)
            for g in range(GU):
                gates(0, g)
            b_times_c(0)
            for v in range(XU):
                x_turn(0, v)
            scores(0, 0)
            pe.wait_ge(w_scaled, 1)
            pe.wait_ge(g_done, 1)
            with pe.Fori(0, B - 1) as b:
                turn(b, True)
            turn(B - 1, False)

        @block.scalar
        def _(act):
            act.sem_inc(gate_done, GD)
            act.sem_inc(xturn_done, XTD)
            act.sem_inc(turn_done, TD)
            act.sem_inc(exp_done, XP)
            act.sem_inc(squared, SQ)
            act.wait_ge(loaded_in, 48)

            def tap(f, u):
                act.wait_ge(pair_ready, NP * f + u + 1)
                for j, ch in enumerate(PAIRS[u]):
                    ins = act.activation(cv[:, ch, :], bank[u % 2][:, j * L:(j + 1) * L], ACT.Identity,
                                         bias=conv_b[:, ch:ch + 1], scale=conv_w[:, ch, TAPS - 1:TAPS])
                ins.then_inc(tap_done, 1)

            def conv_silu(f, u):
                q = PAIRS[u]
                act.wait_ge(conv_done, NP * f + u + 1)
                act.activation(cv[:, q[0]:q[1] + 1, :], cv[:, q[0]:q[1] + 1, :], ACT.Silu).then_inc(silu_done, 1)

            def gate_silu(f, g):
                t, n = divmod(g, GU // TB)
                act.wait_ge(gate_ready, GU * f + g + 1)
                act.wait_ge(gated, TB * NHG * f + GTD)
                act.activation(gate[:, t, n * 512:(n + 1) * 512], bank[(NP + g) % 2][:, :], ACT.Silu,
                               scale=undo[:, 0:1]).then_inc(gate_done, 1)

            def x_copy(f, v):
                act.wait_ge(xturn_ready, XU * f + v + 1)
                act.wait_ge(xdt_done, XU * f + v - 1 + XD)
                act.wait_ge(dx_done, XU * f + v - 1 + DX)
                act.activation(stage[:, v % 2, :], bank[6 + v % 2][:, :], ACT.Copy).then_inc(xturn_done, 1)

            def exps(b, tr):
                for u in range(3 * tr, 3 * tr + 3):
                    act.wait_ge(e_ready, EU * b + u + 1 + ER)
                    if u % 3 == 0:
                        act.wait_ge(y_done, TR * b + tr - 1 + YD)
                    act.activation(sc[:, u % ES, :], bank[2 + u % 2][:, :], ACT.Exp).then_inc(exp_done, 1)

            def squares(b, g):
                for t in range(TB):
                    act.wait_ge(gated, TB * NHG * b + 2 * g + t + 1 + GTD)
                    act.wait_ge(squared, TB * NHG * b + 2 * g + t - 1 + SQ)
                    act.activation(junk[:, t, :], yg[:, t, g * 512:(g + 1) * 512], ACT.Square,
                                   accum_out=ssp[:, t, g:g + 1]).then_inc(squared, 1)

            def g_copy(b, t, q):
                v = t * NHG + q
                act.wait_ge(turn_ready, XU * b + v + 1)
                if q == 0:
                    act.wait_ge(out_ready, TB * b + t - 1 + OR)
                act.activation(gT[:, t, 4 * q:4 * q + 4, :], bank[6 + v % 2][:, :].rearrange("p (a t) -> p a t", a=4),
                               ACT.Copy).then_inc(turn_done, 1)

            def turn(b, more):
                for tr in range(TR):
                    if tr + 1 < TR:
                        exps(b, tr + 1)
                    if tr in (4, 6):
                        squares(b, tr // 2 - 2)
                    if more and tr < EARLY:
                        tap(b + 1, tr)
                squares(b, 2)
                for q in range(NHG):
                    if more and EARLY + q < NP:
                        tap(b + 1, EARLY + q)
                    if q == NHG - 1:
                        squares(b, 3)
                    g_copy(b, 0, q)
                for q in range(NHG):
                    g_copy(b, 1, q)
                    if more and q % 2:
                        gate_silu(b + 1, q // 2)
                if more:
                    for u in range(NP):
                        conv_silu(b + 1, u)
                    x_copy(b + 1, 0)
                    x_copy(b + 1, 1)
                    gate_silu(b + 1, 2)
                    x_copy(b + 1, 2)
                    gate_silu(b + 1, 3)
                    for v in range(3, XU):
                        x_copy(b + 1, v)
                    for g in range(4, GU):
                        gate_silu(b + 1, g)
                    exps(b + 1, 0)

            for u in range(NP):
                tap(0, u)
                if u:
                    conv_silu(0, u - 1)
            conv_silu(0, NP - 1)
            for g in range(GU):
                gate_silu(0, g)
            for v in range(XU):
                x_copy(0, v)
            exps(0, 0)
            with act.Fori(0, B - 1) as b:
                turn(b, True)
            turn(B - 1, False)

        @block.gpsimd
        def _(pool):
            pool.memset(lrow[:, :, :, :], 1.0).then_inc(consts, 1)
            pool.memset(rrow[:, :, :, :], 1.0).then_inc(consts, 1)
            pool.memset(expo[:, :], -0.5).then_inc(consts, 1)
            pool.sem_inc(dx_done, DX)
            pool.sem_inc(gated, GTD)
            pool.sem_inc(m_pool, MP)
            pool.wait_ge(loaded_in, 48)

            def d_times_x(f, v):
                q, t = divmod(v, TB)
                if v == 0:
                    pool.wait_ge(turn_done, XU * f + TD)
                    pool.wait_ge(squared, TB * NHG * f + SQ)
                pool.wait_ge(xturn_done, XU * f + v + 1 + XTD)
                hs, cs = slice(HG * q, HG * q + HG), slice(q * 512, (q + 1) * 512)
                pool.tensor_tensor(yg[:, t, cs].rearrange("p (h d) -> p h d", d=PH),
                                   stage[:, v % 2, :].rearrange("p (h d) -> p h d", d=PH),
                                   d_row[:, hs].unsqueeze(2).broadcast_to([P, HG, PH]), ALU.mult).then_inc(dx_done, 1)

            def decayed(b, tr):
                u = 3 * tr + 2
                pool.wait_ge(exp_done, EU * b + u + 1 + XP)
                pool.wait_ge(g_done, b + 1)
                s = sc[:, u % ES, :].rearrange("p (h l) -> p h l", h=4)
                pool.tensor_tensor(s, s, gsb[:, L:L + P].unsqueeze(1).broadcast_to([P, 4, P]), ALU.mult).then_inc(m_pool, 1)

            def gating(b, g):
                pool.wait_ge(y_added, NHG * b + g + 1 + YA)
                pool.wait_ge(gate_done, GU * (b + 1) + GD)
                for t in range(TB):
                    part = slice(g * 512, (g + 1) * 512)
                    pool.tensor_tensor(yg[:, t, part], yg[:, t, part], gate[:, t, part], ALU.mult).then_inc(gated, 1)

            def turn(b, more):
                for tr in range(TR):
                    if tr + 1 < TR:
                        decayed(b, tr + 1)
                    if tr % 2 == 0 and tr:
                        gating(b, tr // 2 - 1)
                gating(b, NHG - 1)
                pool.wait_ge(ms_ready, b + 1)
                pool.tensor_tensor(rs[:, :], ms[:, :], expo[:, :], ALU.pow).then_inc(rs_ready, 1)
                if more:
                    for v in range(XU):
                        d_times_x(b + 1, v)
                    decayed(b + 1, 0)

            for v in range(XU):
                d_times_x(0, v)
            decayed(0, 0)
            pool.wait_ge(loaded_out, 32)
            pool.tensor_tensor(w_out[:, :, :], w_out[:, :, :], nrm_w[:, :].unsqueeze(2).broadcast_to([P, XT, D]), ALU.mult)\
                .then_inc(w_scaled, 1)
            pool.wait_ge(consts, 3)
            with pool.Fori(0, B - 1) as b:
                turn(b, True)
            turn(B - 1, False)

        @block.vector
        def _(dve):
            dve.sem_inc(xdt_done, XD)
            dve.sem_inc(y_added, YA)
            dve.sem_inc(x_added, XA)

            def conv(f, u):
                dve.wait_ge(tap_done, NP * f + u + 1)
                for k in range(TAPS - 1):
                    back = k + 1
                    if k:
                        dve.wait_ge(tap_dve, 2 * (NP * f + u) + k)
                    for j, ch in enumerate(PAIRS[u]):
                        ins = dve.scalar_tensor_tensor(
                            cv[:, ch, back:L], bank[u % 2][:, j * L:(j + 1) * L - back],
                            conv_w[:, ch, TAPS - 1 - back:TAPS - back], cv[:, ch, back:L], ALU.mult, ALU.add)
                    ins.then_inc(tap_dve if k < TAPS - 2 else conv_done, 1)

            def g_copy(f):
                dve.wait_ge(g_ready, f + 1)
                dve.wait_ge(m_pool, TR * f + MP)
                dve.tensor_copy(gsb[:, :], bank[6][:, 0:3 * P]).then_inc(g_done, 1)

            def dt_times_x(f, v):
                q, t = divmod(v, TB)
                if v == 0:
                    dve.wait_ge(y_done, TR * f + YD)
                dve.wait_ge(xturn_done, XU * f + v + 1 + XTD)
                hs, cs = slice(HG * q, HG * q + HG), slice(q * 512, (q + 1) * 512)
                dve.tensor_tensor(xdt[:, t, cs].rearrange("p (h d) -> p h d", d=PH),
                                  stage[:, v % 2, :].rearrange("p (h d) -> p h d", d=PH),
                                  dt_tok[:, ds(TB * f + t, 1), hs].rearrange("p a h -> p (a h)").unsqueeze(2).broadcast_to([P, HG, PH]),
                                  ALU.mult).then_inc(xdt_done, 1)

            def decayed(b, tr):
                for u in range(3 * tr, 3 * tr + 2):
                    dve.wait_ge(exp_done, EU * b + u + 1 + XP)
                    s = sc[:, u % ES, :].rearrange("p (h l) -> p h l", h=2)
                    dve.tensor_tensor(s, s, gsb[:, 0:L].unsqueeze(1).broadcast_to([P, 2, L]), ALU.mult).then_inc(m_dve, 1)

            def add_y(b, g):
                dve.wait_ge(y_done, TR * b + 2 * (g + 1) + YD)
                dve.wait_ge(dx_done, XU * (b + 1) + DX)
                for t in range(TB):
                    part = yg[:, t, g * 512:(g + 1) * 512]
                    ins = dve.tensor_tensor(part, part, bank[4 + t][:, :], ALU.add)
                ins.then_inc(y_added, 1)

            def turn(b, more):
                for tr in range(TR):
                    if tr % 2 == 0 and tr:
                        add_y(b, tr // 2 - 1)
                    if tr + 1 < TR:
                        decayed(b, tr + 1)
                    if more and tr < EARLY:
                        conv(b + 1, tr)
                add_y(b, NHG - 1)
                if more:
                    for u in range(EARLY, NP):
                        conv(b + 1, u)
                    g_copy(b + 1)
                dve.wait_ge(squared, TB * NHG * (b + 1) + SQ)
                dve.reduce_sum(ms[:, :], ssp[:, :, :], axis=AXX).then_inc(ss_ready, 1)
                dve.wait_ge(ss_ready, b + 1)
                dve.tensor_scalar(ms[:, :], ms[:, :], 1.0 / INTER, NORM_EPS, ALU.mult, ALU.add).then_inc(ms_ready, 1)
                dve.wait_ge(rs_ready, b + 1)

                def add(t):
                    dve.wait_ge(out_ready, TB * b + t + 1 + OR)
                    xt = c.x[:, ds(TB * b + t, 1), :].rearrange("p a d -> p (a d)")
                    dve.scalar_tensor_tensor(xt, bank[4 + t][:, 0:D], rs[:, t:t + 1], xt, ALU.mult, ALU.add).then_inc(x_added, 1)

                add(0)
                if more:
                    for v in range(XU):
                        dt_times_x(b + 1, v)
                add(1)
                if more:
                    decayed(b + 1, 0)

            for u in range(NP):
                conv(0, u)
            g_copy(0)
            for v in range(XU):
                dt_times_x(0, v)
            decayed(0, 0)
            with dve.Fori(0, B - 1) as b:
                turn(b, True)
            turn(B - 1, False)
    p.retire()


def route(nc, c, tag, wT, w_router, undo_router, hidden_scale):
    with ExitStack() as inner:
        p = Core(nc, inner)
        sb, sem = (lambda n, *r: p.sb(f"{tag}_{n}", *r)), (lambda n: p.sem(f"{tag}_r_{n}"))
        bank = c.bank
        lgT = sb("lgT", [E, T])
        lg = sb("lg", [P, NT, E])
        top, tot, inv = sb("top", [P, NT]), sb("tot", [P, NT]), sb("inv", [P, NT])
        best, rest, pick = sb("best", [P, NT, TOPK]), sb("rest", [P, NT, E]), sb("pick", [P, NT, E])
        pickb = sb("pickb", [P, NT, E], BF16)
        parts, partsf = sb("parts", [P, NT, PARTS, E], BF16), sb("partsf", [P, NT, PARTS, E])
        (lg_ready, lgT_ready, turned, max_ready, sub_ready, exp_ready, sum_ready, inv_ready, prob_ready, best_ready,
         rest_ready, pick_ready, pickb_ready, wsum_ready, winv_ready, w_ready, pos_ready, kept_ready, part_ready,
         left_ready, wide_ready, w_turned, done) = (sem(n) for n in (
             "lg", "lgT", "turned", "max", "sub", "exp", "sum", "inv", "prob", "best", "rest", "pick", "pickb",
             "wsum", "winv", "w", "pos", "kept", "part", "left", "wide", "w_turned", "done"))
        wide = lambda t2: t2[:, :].unsqueeze(2).broadcast_to([P, NT, E])
        with nc.Block() as block:
            @block.tensor
            def _(pe):
                for q in range(T // 512):
                    split_matmul(pe, bank[q][0:E, :], lambda i, k: w_router[:, i, k, :],
                                 lambda i, k: c.xT[:, i, k, q * 512:(q + 1) * 512]).then_inc(lg_ready, 1)
                for t in range(NT):
                    if t % 4 == 0:
                        pe.wait_ge(lgT_ready, t // 4 + 1)
                    mm = pe.transpose(bank[4][:, t * E:(t + 1) * E], lgT[:, t * P:(t + 1) * P], c.ident[0:E, 0:E])
                mm.then_inc(turned, 1)
                pe.wait_ge(pickb_ready, 1)
                pe.matmul(bank[5][:, :], c.earlier[:, :], pickb[:, :, :], start=True, stop=True)
                for t in range(NT - 1):
                    mm = pe.matmul(bank[5][:, (t + 1) * E:], c.onesb[:, :],
                                   pickb[:, t:t + 1, :].broadcast_to([P, NT - 1 - t, E]),
                                   start=False, stop=True, skip_group_check=True)
                mm.then_inc(pos_ready, 1)
                pe.wait_ge(wide_ready, 1)
                for t in range(NT):
                    mm = pe.transpose(bank[t // 4][0:PARTS * E, (t % 4) * P:(t % 4 + 1) * P],
                                      partsf[:, t, :, :].rearrange("p i e -> p (i e)"), c.ident[:, :])
                    if t % 4 == 3:
                        mm.then_inc(w_turned, 1)

            @block.scalar
            def _(act):
                for q in range(T // 512):
                    act.wait_ge(lg_ready, q + 1)
                    act.activation(lgT[:, q * 512:(q + 1) * 512], bank[q][0:E, :], ACT.Copy,
                                   scale=undo_router[0:E, 0:1]).then_inc(lgT_ready, 1)
                act.wait_ge(sub_ready, 1)
                act.activation(lg[:, :, :], lg[:, :, :], ACT.Exp).then_inc(exp_ready, 1)
                act.wait_ge(part_ready, PARTS)
                act.activation(partsf[:, :, :, :], parts[:, :, :, :], ACT.Copy).then_inc(wide_ready, 1)
                for q in range(4):
                    act.wait_ge(w_turned, q + 1)
                    act.activation(wT[:, q * 512:(q + 1) * 512], bank[q][0:PARTS * E, :], ACT.Copy).then_inc(done, 1)

            @block.vector
            def _(dve):
                logits = bank[4][:, :].rearrange("p (t e) -> p t e", e=E)
                dve.wait_ge(turned, 1)
                dve.reduce_max(top[:, :], logits, axis=AXX).then_inc(max_ready, 1)
                dve.wait_ge(max_ready, 1)
                dve.tensor_tensor(lg[:, :, :], logits, wide(top), ALU.subtract).then_inc(sub_ready, 1)
                dve.wait_ge(exp_ready, 1)
                dve.reduce_sum(tot[:, :], lg[:, :, :], axis=AXX).then_inc(sum_ready, 1)
                dve.wait_ge(sum_ready, 1)
                dve.reciprocal(inv[:, :], tot[:, :]).then_inc(inv_ready, 1)
                dve.wait_ge(inv_ready, 1)
                dve.tensor_tensor(lg[:, :, :], lg[:, :, :], wide(inv), ALU.mult).then_inc(prob_ready, 1)
                dve.wait_ge(prob_ready, 1)
                for t in range(NT):
                    dve.max(best[:, t, :], lg[:, t, :]).then_inc(best_ready, 1)
                for t in range(NT):
                    dve.wait_ge(best_ready, t + 1)
                    dve.match_replace(out=rest[:, t, :], in_to_replace=best[:, t, :], in_values=lg[:, t, :], imm_value=-1.0).then_inc(rest_ready, 1)
                dve.wait_ge(rest_ready, NT)
                dve.tensor_scalar(pickb[:, :, :], rest[:, :, :], 0.0, None, ALU.is_lt).then_inc(pickb_ready, 1)
                dve.tensor_scalar(pick[:, :, :], rest[:, :, :], 0.0, None, ALU.is_lt).then_inc(pick_ready, 1)
                dve.reduce_sum(tot[:, :], best[:, :, :], axis=AXX).then_inc(wsum_ready, 1)
                dve.wait_ge(wsum_ready, 1)
                dve.reciprocal(inv[:, :], tot[:, :]).then_inc(winv_ready, 1)
                dve.wait_ge(winv_ready, 1)
                dve.wait_ge(pick_ready, 1)
                dve.tensor_tensor(lg[:, :, :], lg[:, :, :], wide(inv), ALU.mult).then_inc(w_ready, 1)
                dve.wait_ge(w_ready, 1)
                dve.scalar_tensor_tensor(lg[:, :, :], lg[:, :, :], hidden_scale, pick[:, :, :], ALU.mult, ALU.mult).then_inc(w_ready, 1)
                dve.wait_ge(w_ready, 2)
                dve.wait_ge(pos_ready, 1)
                dve.scalar_tensor_tensor(lg[:, :, :], bank[5][:, :].rearrange("p (t e) -> p t e", e=E), float(CAP),
                                         lg[:, :, :], ALU.is_lt, ALU.mult).then_inc(kept_ready, 1)
                dve.wait_ge(kept_ready, 1)
                for i in range(PARTS):
                    dve.tensor_copy(parts[:, :, i, :], lg[:, :, :]).then_inc(part_ready, 1)
                    if i < PARTS - 1:
                        dve.wait_ge(part_ready, i + 1)
                        dve.tensor_tensor(lg[:, :, :], lg[:, :, :], parts[:, :, i, :], ALU.subtract).then_inc(left_ready, 1)
                        dve.wait_ge(left_ready, i + 1)
        p.retire()


def experts(nc, c, tag, w_gate, w_up, w_down, w_router, k):
    with ExitStack() as inner:
        p = Core(nc, inner)
        wT = p.sb(tag + "_wT", [PARTS * E, T], BF16)
        route(nc, c, tag, wT, w_router, k["router"], k["hidden"])
        bank = c.bank
        NS, AHEAD = 4, 2
        act_g = p.sb(tag + "_act", [P, NS, GT_TOK])
        hid = p.sb(tag + "_hid", [P, NS, 2, GT_TOK], F16)
        (gate_ready, up_ready, wide_ready, silu_done, prod_done, full_done, high_done, hid_done, hid_used, x_added) = (
            p.sem(f"{tag}_{n}") for n in ("gate", "up", "wide", "silu", "prod", "full", "high", "hid", "hid_used", "x_added"))
        SD, PD, FD, HD_, HU, XA = 2, 2, 2, NS, NS, 1
        with nc.Block() as block:
            @block.tensor
            def _(pe):
                pe.sem_inc(hid_used, HU)

                def up(g, j):
                    tok = ds(g * GT_TOK, GT_TOK)
                    pe.wait_ge(silu_done, FT * g + j - 1 + SD)
                    split_matmul(pe, bank[j % 2][:, :], lambda i, k: w_gate[:, i, k, j * P:(j + 1) * P],
                                 lambda i, k: c.xT[:, i, k, tok]).then_inc(gate_ready, 1)
                    pe.wait_ge(prod_done, FT * g + j - 1 + PD)
                    split_matmul(pe, bank[2 + j % 2][:, :], lambda i, k: w_up[:, i, k, j * P:(j + 1) * P],
                                 lambda i, k: c.xT[:, i, k, tok]).then_inc(up_ready, 1)
                    pe.wait_ge(full_done, FT * g + j - 1 + FD)
                    pe.matmul(bank[4 + j % 2][:, :], c.spread[:, j * P:(j + 1) * P], wT[:, tok],
                              start=True, stop=True).then_inc(wide_ready, 1)

                def down(g, j):
                    if j == 0:
                        pe.wait_ge(x_added, g + XA)
                    pe.wait_ge(hid_done, FT * g + j + 1 + HD_)
                    for t in range(GT_TOK // P):
                        for n, (iw, ih) in enumerate(PASSES):
                            mm = pe.matmul(bank[6 + t // 2][:, (t % 2) * D:(t % 2 + 1) * D],
                                           hid[:, j % NS, ih, t * P:(t + 1) * P], w_down[:, iw, j, :],
                                           start=(j == 0 and n == 0 and t % 2 == 0), stop=(j == FT - 1 and n == 2),
                                           skip_group_check=True)
                    mm.then_inc(hid_used, 1)

                for j in range(AHEAD):
                    up(0, j)
                with pe.Fori(0, NG - 1) as g:
                    for j in range(FT):
                        if j + AHEAD < FT:
                            up(g, j + AHEAD)
                        else:
                            up(g + 1, j + AHEAD - FT)
                        down(g, j)
                for j in range(FT):
                    if j + AHEAD < FT:
                        up(NG - 1, j + AHEAD)
                    down(NG - 1, j)

            @block.scalar
            def _(act):
                act.sem_inc(silu_done, SD)

                def silu(g, j):
                    act.wait_ge(gate_ready, FT * g + j + 1)
                    act.wait_ge(hid_done, FT * g + j - NS + 1 + HD_)
                    act.activation(act_g[:, j % NS, :], bank[j % 2][:, :], ACT.Silu, scale=k["gate"]).then_inc(silu_done, 1)

                def high(g, j):
                    act.wait_ge(full_done, FT * g + j + 1 + FD)
                    act.wait_ge(hid_used, FT * g + j - NS + 1 + HU)
                    act.activation(hid[:, j % NS, 0, :], act_g[:, j % NS, :], ACT.Copy).then_inc(high_done, 1)

                silu(0, 0)
                with act.Fori(0, NG - 1) as g:
                    for j in range(FT):
                        if j + 1 < FT:
                            silu(g, j + 1)
                        else:
                            silu(g + 1, 0)
                        high(g, j)
                for j in range(FT):
                    if j + 1 < FT:
                        silu(NG - 1, j + 1)
                    high(NG - 1, j)

            @block.gpsimd
            def _(pool):
                pool.sem_inc(hid_done, HD_)
                with pool.Fori(0, NG) as g:
                    for j in range(FT):
                        pool.wait_ge(high_done, FT * g + j + 1)
                        pool.tensor_tensor(hid[:, j % NS, 1, :], act_g[:, j % NS, :], hid[:, j % NS, 0, :], ALU.subtract).then_inc(hid_done, 1)

            @block.vector
            def _(dve):
                dve.sem_inc(prod_done, PD)
                dve.sem_inc(full_done, FD)
                dve.sem_inc(x_added, XA)

                def product(g, j):
                    dve.wait_ge(silu_done, FT * g + j + 1 + SD)
                    dve.wait_ge(up_ready, FT * g + j + 1)
                    dve.tensor_tensor(act_g[:, j % NS, :], act_g[:, j % NS, :], bank[2 + j % 2][:, :], ALU.mult).then_inc(prod_done, 1)
                    dve.wait_ge(prod_done, FT * g + j + 1 + PD)
                    dve.wait_ge(wide_ready, FT * g + j + 1)
                    dve.tensor_tensor(act_g[:, j % NS, :], act_g[:, j % NS, :], bank[4 + j % 2][:, :], ALU.mult).then_inc(full_done, 1)

                def add(g):
                    dve.wait_ge(hid_used, FT * (g + 1) + HU)
                    for t in range(GT_TOK // P):
                        xt = c.x[:, ds(GT_TOK // P * g + t, 1), :].rearrange("p a d -> p (a d)")
                        ins = dve.scalar_tensor_tensor(xt, bank[6 + t // 2][:, (t % 2) * D:(t % 2 + 1) * D], k["out"], xt,
                                                       ALU.mult, ALU.add)
                    ins.then_inc(x_added, 1)

                for j in range(AHEAD):
                    product(0, j)
                with dve.Fori(0, NG - 1) as g:
                    for j in range(AHEAD, FT):
                        product(g, j)
                    for j in range(AHEAD):
                        product(g + 1, j)
                    add(g)
                for j in range(AHEAD, FT):
                    product(NG - 1, j)
                add(NG - 1)
        p.retire()


def attention(nc, c, w, wqkv, undo):
    PR, MR = 3 * HD, 3
    HH = AH // 2
    NU = 12
    NQ = 4
    ES = 6
    V1, VW = HD + 1, 2 * HD + 1
    ROW = 2.0 ** 15
    QTOP = 2.0 ** 12
    GT = 512
    DELAY = 8
    with ExitStack() as inner:
        p = Core(nc, inner)
        sb, sem = (lambda n, *r: p.sb("at_" + n, *r)), (lambda n: p.sem("at_" + n))
        wo = sb("wo", [P, KD, D])
        bqk, bv, bo = sb("bqk", [P, 4]), sb("bv", [P, D]), sb("bo", [P, D])
        bmax, bmax_v = sb("bmax", [P, 1]), sb("bmax_v", [P, 1])
        ball, bound, power, scale, fold, escale = (sb(n, [P, 1]) for n in (
            "ball", "bound", "power", "scale", "fold", "escale"))
        parts = sb("parts", [P, 4, 2, GT], F16)
        q3, k3 = sb("q3", [64, 2, AH, L], F16), sb("k3", [64, 2, AH, L], F16)
        v_all = sb("v", [P, NT, AH, VW], F16)
        ex = sb("exps", [P, 3, 512])
        full, v_full = ex[:, 0:2, :], ex[:, 2, :].rearrange("p (a d) -> p a d", a=2)
        pT = sb("exp_parts", [P, ES, 2, 512], F16)
        mx = sb("mx", [P, 2, HH, TB])
        neg, negs = sb("neg", [HH * TB, P]), [sb(f"neg_parts{g}", [HH * TB, MR, P], F16) for g in range(2)]
        rden = sb("rden", [P, TB, HH])
        y, yT = sb("y", [P, TB, D]), sb("yT", [P, KD, L])
        bank = c.bank
        qk_parts = nc.dram_tensor("qk_parts", [4, 2 * P, T], F16, kind="Internal").ap()
        mx_parts = nc.dram_tensor("mx_parts", [B, 2, MR, HH * L], F16, kind="Internal").ap()
        loaded, const, scales = sem("loaded"), sem("const"), sem("scales")
        (all_ready, proj_ready, full_ready, high_ready, low_ready, v_ready, v_done, s_ready, max_done, nbt_ready,
         neg_ready, neg_dve, neg_parts, st_ready, exp_done, hi_done, lo_pool, lo_dve, v_full_ready,
         v_high, v_step, pv_ready, pv_read, pv_sum, inv_done, y_done, yT_ready, yT_done,
         out_ready, x_added, bias_added) = (sem(n) for n in (
             "all", "proj", "full", "high", "low", "v_ready", "v_done", "s", "max", "nbt",
             "neg", "neg_step", "neg_parts", "st", "exp", "hi", "lo_pool", "lo_dve", "v_full",
             "v_high", "v_step", "pv", "pv_read", "pv_sum", "inv", "y", "yT_ready", "yT_done", "out", "x_added", "bias_added"))
        saved = [sem(f"saved{n}") for n in range(4)]
        qk_loaded = [[sem(f"qk_loaded{s}{g}") for g in range(2)] for s in range(2)]
        mx_saved = [sem(f"mx_saved{g}") for g in range(2)]
        mx_rows = [sem(f"mx_rows{g}") for g in range(2)]
        START = {"full": 2, "low": 2, "saved": 16, "v_done": 2, "max": 2, "nbt": 2, "neg": 1, "rows": 16, "exp": 2,
                 "pv": 2, "x": 1, "neg_parts": 1, "lo_pool": 2, "lo_dve": 1, "pv_read": 1, "yT": 1}
        FU, LO, SV, VD, MD, NB, NR, RW, XP, PV, XA, NP, LP, LD, PVR, YT = START.values()

        def trio(qd):
            return [(0, 4 * qd, 4), (1, 4 * qd, 2), (1, 4 * qd + 2, 2)]

        with nc.Block() as block:
            @block.sync
            def _(sp):
                for dst, src in ((bqk, w["bqk"]), (wo, w["wo"]), (bv, w["bv"].partition_broadcast(P)), (bo, w["bo"].partition_broadcast(P))):
                    sp.dma_start(dst[:], src).then_inc(loaded, 16)
                with sp.Fori(0, NG) as g:
                    for n in range(4):
                        sp.wait_ge(low_ready, 4 * g + n + 1 + LO)
                        sp.dma_start(qk_parts[n].rearrange("(c p) t -> p c t", p=P)[:, :, ds(g * GT, GT)],
                                     parts[:, n, :, :]).then_inc(saved[n], 16)
                sp.wait_ge(const, 2)
                for n in range(4):
                    sp.wait_ge(saved[n], 16 * NG + SV)

                def load(f, slot, g):
                    if f is not None:
                        sp.wait_ge(st_ready, NU * (f - 2) + (g + 1) * NU // 2)
                    tok = ds((slot if f is None else f) * L, L)
                    hs = slice(g * HH, (g + 1) * HH)
                    q_rows, k_rows = (qk_parts[2 * i + g].rearrange("(r h) t -> r h t", h=HH)[:, :, tok] for i in range(2))
                    done = qk_loaded[slot][g]
                    sp.dma_start(q3[0:2 * HD, slot, hs, :], q_rows[0:2 * HD]).then_inc(done, 16)
                    sp.dma_start(q3[2 * HD:PR, slot, hs, :], q_rows[0:HD]).then_inc(done, 16)
                    sp.dma_start(k3[0:HD, slot, hs, :], k_rows[0:HD]).then_inc(done, 16)
                    sp.dma_start(k3[HD:PR, slot, hs, :], k_rows[0:2 * HD]).then_inc(done, 16)

                def maxima_rows(f, slot, g):
                    sp.wait_ge(neg_parts, 2 * f + g + 1 + NP)
                    sp.dma_start(mx_parts[ds(f, 1), g].rearrange("f c (x l) -> (f x) c l", l=P), negs[g][:, :, :]).then_inc(mx_saved[g], 16)
                    sp.wait_ge(mx_saved[g], 16 * (f + 1))
                    sp.dma_start(q3[PR:PR + MR, slot, g * HH:(g + 1) * HH, :],
                                 mx_parts[ds(f, 1), g].rearrange("f c (h l) -> (f c) h l", l=L)).then_inc(mx_rows[g], 16)

                for slot in range(2):
                    for g in range(2):
                        load(None, slot, g)
                for g in range(2):
                    maxima_rows(0, 0, g)
                with sp.Fori(0, B // 2 - 1) as j:
                    for i in range(2):
                        for g in range(2):
                            load(2 * j + 2 + i, i, g)
                            maxima_rows(2 * j + 1 + i, (1 + i) % 2, g)
                for g in range(2):
                    maxima_rows(B - 1, 1, g)

            @block.gpsimd
            def _(pool):
                pool.memset(v_all[:, :, :, HD:V1], 1.0).then_inc(const, 1)
                pool.wait_ge(const, 1)
                pool.memset(k3[32:64, :, :, :], ROW).then_inc(const, 1)
                pool.wait_ge(const, 2)
                pool.wait_ge(scales, 1)
                pool.partition_all_reduce(ball[:, :], bmax[:, :], P, bass.bass_isa.ReduceOp.max).then_inc(all_ready, 1)

                pool.sem_inc(mx_rows[0], RW)
                pool.sem_inc(mx_rows[1], RW)
                pool.sem_inc(lo_pool, LP)
                pool.wait_ge(loaded, 64)

                def low(b, u):
                    pool.wait_ge(hi_done, NU * b + u + 1)
                    pool.tensor_tensor(pT[:, u % ES, 1, :], ex[:, u % 3, :], pT[:, u % ES, 0, :], ALU.subtract).then_inc(lo_pool, 1)

                def turn(b):
                    xt = c.x[:, ds(TB * b, TB), :]
                    pool.tensor_tensor(xt, xt, bo[:, :].unsqueeze(1).broadcast_to([P, TB, D]), ALU.add).then_inc(bias_added, 1)
                    for qd in range(NQ):
                        low(b, 3 * qd)
                        low(b, 3 * qd + 2)

                with pool.Fori(0, B) as b:
                    turn(b)

            @block.tensor
            def _(pe):
                pe.sem_inc(nbt_ready, NB)
                pe.sem_inc(pv_ready, PV)
                pe.sem_inc(yT_ready, YT)
                with pe.Fori(0, NG) as g:
                    for n in range(4):
                        pe.wait_ge(full_ready, 4 * g + n - 1 + FU)
                        split_matmul(pe, bank[n % 2][:, :], lambda i, k: wqkv[:, i, k, n * P:(n + 1) * P],
                                     lambda i, k: c.xT[:, i, k, ds(g * GT, GT)]).then_inc(proj_ready, 1)
                    for n in range(2):
                        pe.wait_ge(v_done, 2 * g + n - 1 + VD)
                        for t in range(2):
                            mm = split_matmul(pe, bank[2 + n][:, t * D:(t + 1) * D],
                                              lambda i, k: c.xT[:, i, k, ds(g * GT + (2 * n + t) * P, P)],
                                              lambda i, k: wqkv[:, i, k, 2 * D:3 * D])
                        mm.then_inc(v_ready, 1)

                def scores(f, slot, u, beside=lambda: None):
                    t, h, n = trio(u // 3)[u % 3]
                    w_ = (t + 1) * P
                    if u % (NU // 2) == 0:
                        pe.wait_ge(qk_loaded[slot][u // (NU // 2)], 64 * (f // 2 + 1) if isinstance(f, int) else 32 * (f - slot) + 64)
                    pe.wait_ge(max_done, NU * f + u - 1 + MD)
                    bk = bank[u % 2]
                    diag = bk[:, :].rearrange("p (j l) -> p j l", l=w_)[:, :, t * P:w_]
                    pe.matmul(diag, c.identb[:, :], c.after[:, :].unsqueeze(1).broadcast_to([P, n, P]),
                              start=True, stop=False, skip_group_check=True)
                    beside()
                    for j in range(n):
                        mm = pe.matmul(bk[:, j * w_:(j + 1) * w_], q3[0:PR, slot, h + j, t * P:(t + 1) * P],
                                       k3[0:PR, slot, h + j, 0:w_], start=False, stop=True, skip_group_check=True)
                        if j < n - 1:
                            beside()
                    mm.then_inc(s_ready, 1)
                    beside()

                def maxima_turn(f, g):
                    pe.wait_ge(max_done, NU * f + (g + 1) * NU // 2 + MD)
                    pe.wait_ge(neg_ready, 2 * f + g + NR)
                    pe.transpose(bank[6][0:HH * TB, 0:P], mx[:, g, :, :].rearrange("p h t -> p (h t)"), c.ident[:, :]).then_inc(nbt_ready, 1)

                def shifted(b, slot, u, beside):
                    qd, n = divmod(u, 3)
                    if u % (NU // 2) == 0:
                        pe.wait_ge(mx_rows[u // (NU // 2)], 16 * (b + 1) + RW)
                    pe.wait_ge(exp_done, NU * b + u - 1 + XP)
                    lo, w_, nj = (0, L, 2) if n < 2 else (P, P, 4)
                    bk = bank[2 + u % 2]
                    diag = bk[:, :].rearrange("p (j l) -> p j l", l=w_)[:, :, 0:P]
                    pe.matmul(diag, c.identb[:, :], c.before[:, :].unsqueeze(1).broadcast_to([P, nj, P]),
                              start=True, stop=False, skip_group_check=True)
                    beside()
                    for j in range(nj):
                        h = 4 * qd + (2 * n + j if n < 2 else j)
                        mm = pe.matmul(bk[:, j * w_:(j + 1) * w_], k3[0:PR + MR, slot, h, lo:lo + P],
                                       q3[0:PR + MR, slot, h, lo:lo + w_], start=False, stop=True, skip_group_check=True)
                        if j < nj - 1:
                            beside()
                    mm.then_inc(st_ready, 1)
                    beside()

                def value(b, qd, i):
                    if i == 0:
                        if qd % 2 == 0:
                            pe.wait_ge(pv_read, 2 * b + qd // 2 + PVR)
                        pe.wait_ge(lo_pool, 8 * b + 2 * qd + 1 + LP)
                        pe.wait_ge(lo_dve, NQ * b + qd + 1 + LD)
                    if i == 16:
                        pe.wait_ge(lo_pool, 8 * b + 2 * (qd + 1) + LP)
                    if i < 16:
                        s = 0
                        j, t, part = i // 4, (i // 2) % 2, i % 2
                        w_ = pT[:, (3 * qd + j // 2) % ES, part, (j % 2) * L + t * P:(j % 2) * L + (t + 1) * P]
                    else:
                        s = t = 1
                        j, part = (i - 16) // 2, i % 2
                        w_ = pT[:, (3 * qd + 2) % ES, part, j * P:(j + 1) * P]
                    v_ = v_all[:, ds(TB * b + s, 1), 4 * qd + j, 0:(VW, V1)[part]].rearrange("p a d -> p (a d)")
                    o = slice((4 * (qd % 2) + j) * VW, (4 * (qd % 2) + j) * VW + (VW, V1)[part])
                    mm = pe.matmul(bank[4 + t][:, o], w_, v_, start=(qd % 2 == 0 and i in (0, 2)), stop=True, skip_group_check=True)
                    if i == 23:
                        mm.then_inc(pv_ready, 1)

                def y_turn(b):
                    pe.wait_ge(y_done, 2 * (b + 1))
                    pe.wait_ge(x_added, b + XA)
                    for t in range(TB):
                        for k in range(KD):
                            mm = pe.transpose(bank[7][:, (2 * t + k) * P:(2 * t + k + 1) * P], y[:, t, k * P:(k + 1) * P], c.ident[:, :])
                    mm.then_inc(yT_ready, 1)

                def project(b):
                    pe.wait_ge(yT_done, b + 1)
                    for t in range(TB):
                        o = bank[7][:, t * D:(t + 1) * D]
                        for k in range(KD):
                            mm = pe.matmul(o, yT[:, k, t * P:(t + 1) * P], wo[:, k, :], start=(k == 0), stop=(k == KD - 1))
                    mm.then_inc(out_ready, 1)

                def turn(b, slot, first, more):
                    for qd in range(NQ):
                        vb, vq = (b, qd - 1) if qd else (b - 1, NQ - 1)
                        small, wide = iter(range(24)), iter(range(30))

                        def beside():
                            k = next(wide)
                            if (first and qd == 0) or k < (DELAY if more else 3):
                                return
                            for _ in range(2):
                                i = next(small, None)
                                if i is not None:
                                    value(vb, vq, i)

                        for n in range(3):
                            shifted(b, slot, 3 * qd + n, beside)
                            if more:
                                scores(b + 1, 1 - slot, 3 * qd + n, beside)
                            if (qd, n) == (0, 0):
                                maxima_turn(b, 1)
                            if more and (qd, n) == (2, 0):
                                maxima_turn(b + 1, 0)
                        if not (first and qd == 0):
                            for i in small:
                                value(vb, vq, i)
                        if not first and qd == 1:
                            y_turn(b - 1)
                        if not first and qd == 2:
                            project(b - 1)
                pe.wait_ge(loaded, 64)
                pe.wait_ge(const, 2)
                for u in range(NU):
                    scores(0, 0, u)
                    if u == 8:
                        maxima_turn(0, 0)
                pe.wait_ge(v_done, 2 * NG + VD)
                turn(0, 0, True, True)
                with pe.Fori(0, B // 2 - 1) as j:
                    turn(2 * j + 1, 1, False, True)
                    turn(2 * j + 2, 0, False, True)
                turn(B - 1, 1, False, False)
                for i in range(24):
                    value(B - 1, NQ - 1, i)
                y_turn(B - 1)
                project(B - 1)

            @block.scalar
            def _(act):
                act.sem_inc(neg_ready, NR)
                act.sem_inc(full_ready, FU)
                act.sem_inc(exp_done, XP)
                act.wait_ge(loaded, 64)
                for n in range(4):
                    act.sem_inc(saved[n], SV)
                act.wait_ge(scales, 7)
                with act.Fori(0, NG) as g:
                    for n in range(4):
                        act.wait_ge(proj_ready, 4 * g + n + 1)
                        act.wait_ge(low_ready, 4 * g + n - 1 + LO)
                        act.activation(full[:, n % 2, :], bank[n % 2][:, :], ACT.Identity, bias=bqk[:, n:n + 1], scale=fold[:, 0:1])\
                            .then_inc(full_ready, 1)
                        act.wait_ge(full_ready, 4 * g + n + 1 + FU)
                        act.wait_ge(saved[n], 16 * g + SV)
                        act.activation(parts[:, n, 0, :], full[:, n % 2, :], ACT.Copy).then_inc(high_ready, 1)
                    for n in range(2):
                        act.wait_ge(v_full_ready, 2 * g + n + 1)
                        act.activation(v_all[:, ds(4 * g + 2 * n, 2), :, 0:HD].rearrange("p a h d -> p (a h) d"),
                                       v_full[:, :, :].rearrange("p a (h d) -> p (a h) d", d=HD), ACT.Copy).then_inc(v_high, 1)

                def exps(b, u):
                    act.wait_ge(st_ready, NU * b + u + 1)
                    if u % 3 != 1:
                        act.wait_ge(lo_pool, 8 * b + 2 * (u // 3) + u % 3 // 2 - 1 + LP)
                    else:
                        act.wait_ge(lo_dve, NQ * b + u // 3 + LD)
                    act.activation(ex[:, u % 3, :], bank[2 + u % 2][:, :], ACT.Exp, scale=escale[:, 0:1]).then_inc(exp_done, 1)

                def high(b, u):
                    act.wait_ge(exp_done, NU * b + u + 1 + XP)
                    if u % 3 == 0:
                        act.wait_ge(pv_ready, NQ * b + u // 3 - 1 + PV)
                    act.activation(pT[:, u % ES, 0, :], ex[:, u % 3, :], ACT.Copy).then_inc(hi_done, 1)

                def y_copy(b):
                    act.wait_ge(yT_ready, b + 1 + YT)
                    act.activation(yT[:, :, :].rearrange("p k (t c) -> p k t c", t=TB),
                                   bank[7][:, :].rearrange("p (t k c) -> p k t c", t=TB, k=KD), ACT.Copy).then_inc(yT_done, 1)

                def negate(f, g):
                    act.wait_ge(nbt_ready, 2 * f + g + 1 + NB)
                    act.wait_ge(neg_parts, 2 * f + g + NP)
                    act.activation(neg[:, :], bank[6][0:HH * TB, 0:P], ACT.Copy, scale=-1.0 / ROW).then_inc(neg_ready, 1)

                def turn(b, first, more):
                    for u in range(NU):
                        exps(b, u)
                        if u:
                            high(b, u - 1)
                        if u == 1:
                            negate(b, 1)
                        if more and u == 7:
                            negate(b + 1, 0)
                        if u == 6 and not first:
                            y_copy(b - 1)
                    high(b, NU - 1)

                negate(0, 0)
                act.wait_ge(low_ready, 4 * NG + LO)
                act.wait_ge(v_done, 2 * NG + VD)
                turn(0, True, True)
                with act.Fori(1, B - 1) as b:
                    turn(b, False, True)
                turn(B - 1, False, False)
                y_copy(B - 1)

            @block.vector
            def _(dve):
                dve.sem_inc(low_ready, LO)
                dve.sem_inc(v_done, VD)
                dve.sem_inc(max_done, MD)
                dve.sem_inc(lo_dve, LD)
                dve.sem_inc(neg_parts, NP)
                dve.sem_inc(pv_read, PVR)
                dve.sem_inc(x_added, XA)
                dve.wait_ge(loaded, 64)
                dve.wait_ge(const, 2)
                dve.reduce_max(bmax[:, :], bqk[:, :], axis=AXX, apply_absolute_value=True).then_inc(v_step, 1)
                dve.reduce_max(bmax_v[:, :], bv[:, :], axis=AXX, apply_absolute_value=True).then_inc(v_step, 1)
                dve.wait_ge(v_step, 2)
                dve.tensor_tensor(bmax[:, :], bmax[:, :], bmax_v[:, :], ALU.max).then_inc(scales, 1)
                dve.wait_ge(all_ready, 1)
                dve.scalar_tensor_tensor(bound[:, :], undo, 2.0 * D * TOP * X_SCALE, ball[:, :], ALU.mult, ALU.add).then_inc(scales, 1)
                dve.wait_ge(scales, 2)
                dve.tensor_scalar(bound[:, :], bound[:, :], 2.0 ** -20, None, ALU.max).then_inc(scales, 1)
                dve.wait_ge(scales, 3)
                dve.tensor_scalar(bound[:, :].bitcast(I32), bound[:, :].bitcast(I32), EXPONENT, None, ALU.bitwise_and).then_inc(scales, 1)
                dve.wait_ge(scales, 4)
                dve.tensor_scalar(power[:, :], bound[:, :], 1.0 / QTOP, None, ALU.mult).then_inc(scales, 1)
                dve.wait_ge(scales, 5)
                dve.reciprocal(scale[:, :], power[:, :]).then_inc(scales, 1)
                dve.scalar_tensor_tensor(escale[:, :], power[:, :], SCALE, power[:, :], ALU.mult, ALU.mult).then_inc(inv_done, 1)
                dve.wait_ge(scales, 6)
                dve.tensor_scalar(bqk[:, :], bqk[:, :], scale[:, 0:1], None, ALU.mult).then_inc(inv_done, 1)
                dve.tensor_scalar(bv[:, :], bv[:, :], scale[:, 0:1], None, ALU.mult).then_inc(inv_done, 1)
                dve.wait_ge(inv_done, 3)
                dve.tensor_tensor(fold[:, :], scale[:, :], undo, ALU.mult).then_inc(scales, 1)
                dve.wait_ge(scales, 7)
                with dve.Fori(0, NG) as g:
                    for n in range(4):
                        dve.wait_ge(high_ready, 4 * g + n + 1)
                        dve.tensor_tensor(parts[:, n, 1, :], full[:, n % 2, :], parts[:, n, 0, :], ALU.subtract).then_inc(low_ready, 1)
                    for n in range(2):
                        dve.wait_ge(v_ready, 2 * g + n + 1)
                        for t in range(2):
                            ins = dve.scalar_tensor_tensor(v_full[:, t, :], bank[2 + n][:, t * D:(t + 1) * D], fold[:, 0:1], bv[:, :],
                                                           ALU.mult, ALU.add)
                        ins.then_inc(v_full_ready, 1)
                        dve.wait_ge(v_high, 2 * g + n + 1)
                        va = v_all[:, ds(4 * g + 2 * n, 2), :, :].rearrange("p a h d -> p (a h) d")
                        ins = dve.tensor_tensor(va[:, :, V1:VW], v_full[:, :, :].rearrange("p a (h d) -> p (a h) d", d=HD),
                                                va[:, :, 0:HD], ALU.subtract)
                        ins.then_inc(v_done, 1)
                        dve.wait_ge(v_done, 2 * g + n + 1 + VD)

                def maxima(f, u):
                    t, h, n = trio(u // 3)[u % 3]
                    g, hh = divmod(h, HH)
                    if u % (NU // 2) == 0:
                        dve.wait_ge(nbt_ready, 2 * f + g - 1 + NB)
                    dve.wait_ge(s_ready, NU * f + u + 1)
                    dve.reduce_max(mx[:, g, hh:hh + n, t], bank[u % 2][:, :].rearrange("p (j l) -> p j l", j=n), axis=AXX).then_inc(max_done, 1)

                def low(b, u):
                    dve.wait_ge(hi_done, NU * b + u + 1)
                    dve.tensor_tensor(pT[:, u % ES, 1, :], ex[:, u % 3, :], pT[:, u % ES, 0, :], ALU.subtract).then_inc(lo_dve, 1)

                def split_maxima(f, g):
                    dve.wait_ge(mx_rows[g], 16 * f + RW)
                    dve.wait_ge(neg_ready, 2 * f + g + 1 + NR)
                    for i in range(MR):
                        last = i == MR - 1
                        dve.tensor_copy(negs[g][:, i, :], neg[:, :]).then_inc(neg_parts if last else neg_dve, 1)
                        if not last:
                            dve.wait_ge(neg_dve, 4 * (2 * f + g) + 2 * i + 1)
                            dve.tensor_tensor(neg[:, :], neg[:, :], negs[g][:, i, :], ALU.subtract).then_inc(neg_dve, 1)
                            dve.wait_ge(neg_dve, 4 * (2 * f + g) + 2 * i + 2)

                def divide(b, g):
                    dve.wait_ge(pv_ready, NQ * b + 2 * (g + 1) + PV)
                    if g == 0:
                        dve.wait_ge(yT_ready, b + YT)
                    o = [bank[4 + t][:, 0:HH * VW].rearrange("p (h d) -> p h d", d=VW) for t in range(TB)]
                    yh = [y[:, t, g * P:(g + 1) * P].rearrange("p (h d) -> p h d", d=HD) for t in range(TB)]
                    for t in range(TB):
                        dve.tensor_copy(yh[t], o[t][:, :, 0:HD]).then_inc(pv_sum, 1)
                        dve.reciprocal(rden[:, t, :], o[t][:, :, HD]).then_inc(pv_sum, 1)
                    dve.wait_ge(pv_sum, 4 * (2 * b + g) + 4)
                    for t in range(TB):
                        ins = dve.tensor_tensor(yh[t], yh[t], o[t][:, :, V1:VW], ALU.add)
                    ins.then_inc(pv_read, 1)
                    dve.wait_ge(pv_read, 2 * b + g + 1 + PVR)
                    for t in range(TB):
                        ins = dve.scalar_tensor_tensor(yh[t], yh[t], power[:, 0:1], rden[:, t, :].unsqueeze(2).broadcast_to([P, HH, HD]),
                                                       ALU.mult, ALU.mult)
                    ins.then_inc(y_done, 1)
                    dve.wait_ge(y_done, 2 * b + g + 1)

                def add(b):
                    dve.wait_ge(bias_added, b + 1)
                    dve.wait_ge(out_ready, b + 1)
                    xt = c.x[:, ds(TB * b, TB), :].rearrange("p a d -> p (a d)")
                    dve.tensor_tensor(xt, xt, bank[7][:, :], ALU.add).then_inc(x_added, 1)

                def turn(b, first, more):
                    for u in range(NU):
                        if u % 3 == 2:
                            low(b, u - 1)
                        if u == 2 and not first:
                            divide(b - 1, 1)
                        if u == 8:
                            if more:
                                split_maxima(b + 1, 0)
                            divide(b, 0)
                        if more:
                            maxima(b + 1, u)
                        if u == 1:
                            split_maxima(b, 1)
                        if u == 10 and not first:
                            add(b - 1)

                for u in range(NU):
                    maxima(0, u)
                split_maxima(0, 0)
                turn(0, True, True)
                with dve.Fori(1, B - 1) as b:
                    turn(b, False, True)
                turn(B - 1, False, False)
                divide(B - 1, 1)
                add(B - 1)
        p.retire()


def expert_constants(nc, c, m, a, unscale):
    undo, hidden, out, both = m.sb("undo_x", [P, 5]), m.sb("hidden_scale", [P, 1]), m.sb("out_scale", [P, 1]), m.sb("gate_up", [P, 1])
    power, folded = m.sb("hidden_power", [P, 1]), m.sb("hidden_folded", [P, 1])
    undo_ready, both_ready, power_ready, inverse_ready, folded_ready, loaded = (
        m.sem("ec_" + n) for n in ("undo", "both", "power", "inverse", "folded", "loaded"))
    with nc.Block() as block:
        @block.sync
        def _(sp):
            sp.dma_start(c.spread[:, :], a["spread"]).then_inc(loaded, 16)
            sp.wait_ge(loaded, 16)

        @block.vector
        def _(dve):
            dve.tensor_scalar(undo[:, :], unscale[:, :], 1.0 / X_SCALE, None, ALU.mult).then_inc(undo_ready, 1)
            dve.tensor_tensor(both[:, :], unscale[:, 2:3], unscale[:, 3:4], ALU.mult).then_inc(both_ready, 1)
            dve.wait_ge(both_ready, 1)
            dve.tensor_scalar(power[:, :], both[:, :], (2 * D * TOP) ** 2 / 2.0 ** 15, None, ALU.mult).then_inc(power_ready, 1)
            dve.wait_ge(power_ready, 1)
            dve.reciprocal(hidden[:, :], power[:, :]).then_inc(inverse_ready, 1)
            dve.tensor_tensor(out[:, :], power[:, :], unscale[:, 4:5], ALU.mult).then_inc(inverse_ready, 1)
            dve.wait_ge(undo_ready, 1)
            dve.wait_ge(inverse_ready, 2)
            dve.tensor_tensor(folded[:, :], hidden[:, :], undo[:, 3:4], ALU.mult).then_inc(folded_ready, 1)
            dve.wait_ge(folded_ready, 1)
    return {"router": undo[:, 0:1], "gate": undo[:, 2:3], "hidden": folded[:, 0:1], "out": out[:, 0:1], "qkv": undo[:, 1:2]}


def build(nc, a, out):
    with ExitStack() as stack:
        c = Core(nc, stack)
        c.bank = [stack.enter_context(nc.psum_tensor(f"bank{i}", [P, 512], F32)) for i in range(8)]
        c.x = c.sb("x", [P, NT, D])
        c.xT = c.sb("xT", [P, 2, KD, T], F16)
        c.ident = c.sb("ident", [P, P])
        c.identb = c.sb("identb", [P, P], BF16)
        c.before = c.sb("before", [P, P], BF16)
        c.after = c.sb("after", [P, P], BF16)
        c.earlier = c.sb("earlier", [P, P], BF16)
        c.onesb = c.sb("onesb", [P, P], BF16)
        loaded = c.sem("x_loaded")
        stored = c.sem("stored")
        xv = a["x"].rearrange("(t p) d -> p t d", p=P)
        with nc.Block() as block:
            @block.sync
            def _(sp):
                sp.dma_start(c.x[:, :, :], xv).then_inc(loaded, 16)
                sp.dma_start(c.ident[:, :], a["ident"]).then_inc(loaded, 16)
                sp.dma_start(c.identb[:, :], a["identb"]).then_inc(loaded, 16)
                sp.dma_start(c.before[:, :], a["before"]).then_inc(loaded, 16)
                sp.dma_start(c.after[:, :], a["after"]).then_inc(loaded, 16)
                sp.dma_start(c.earlier[:, :], a["earlier"]).then_inc(loaded, 16)
                sp.dma_start(c.onesb[:, :], a["onesb"]).then_inc(loaded, 16)
                sp.wait_ge(loaded, 112)
        mixer(nc, c, a)
        m = Core(nc, stack)
        c.spread = m.sb("spread", [PARTS * E, E * FI], BF16)
        w_gate, w_up = (m.sb(n, [P, 2, KD, E * FI], F16) for n in ("w_gate", "w_up"))
        w_down, w_router = m.sb("w_down", [P, 2, FT, D], F16), m.sb("w_router", [P, 2, KD, E], F16)
        wqkv = m.sb("wqkv", [P, 2, KD, 3 * D], F16)
        flat = lambda t: t[:, :, :].rearrange("p k n -> p (k n)")
        flat2 = lambda t: t[:, :, :, :].rearrange("p i k n -> p i (k n)")
        with ExitStack() as inner:
            weights = Splitting(nc, "ew", m, inner, [(n, flat(a["w_" + n]), flat2(t)) for n, t in (
                ("router", w_router), ("qkv", wqkv), ("gate", w_gate), ("up", w_up), ("down", w_down))])
            normalise(nc, "n2", c)
            weights.cut()
        k = expert_constants(nc, c, m, a, weights.unscale)
        ex = (w_gate, w_up, w_down, w_router, k)
        experts(nc, c, "e1", *ex)
        normalise(nc, "n3", c)
        attention(nc, c, a, wqkv, k["qkv"])
        normalise(nc, "n4", c)
        experts(nc, c, "e2", *ex)
        with nc.Block() as block:
            @block.sync
            def _(sp):
                sp.dma_start(out.rearrange("(t p) d -> p t d", p=P), c.x[:, :, :]).then_inc(stored, 16)
                sp.wait_ge(stored, 16)


def kernel(**inputs):
    import numpy as np
    import concourse.bacc as bacc
    from concourse import mybir as mb
    from concourse.bass_utils import run_bass_kernel_spmd as run

    import ml_dtypes
    bf = ml_dtypes.bfloat16
    g = lambda n: np.asarray(inputs[n])
    w_in = g("L0_attn_a_W_in")
    order = np.arange(D).reshape(2, AH // 2, HD).transpose(0, 2, 1).reshape(D)
    order = np.concatenate([order, D + order, 2 * D + np.arange(D)])
    w_qkv = g("L0_attn_b_w_qkv")[:, order].reshape(KD, P, 3 * D).transpose(1, 0, 2)
    b_qkv = g("L0_attn_b_b_qkv")[order]
    arrays = {
        "x": g("L0_attn_a_hidden_states").reshape(T, D),
        "w_in": w_in.T.reshape(KD, P, PROJ).transpose(1, 0, 2),
        "conv_w": g("L0_attn_a_conv_w").reshape(CT, P, TAPS).transpose(1, 0, 2),
        "conv_b": g("L0_attn_a_conv_b").reshape(CT, P).T,
        "dt_bias": np.tile(g("L0_attn_a_dt_bias"), QUARTERS).reshape(P, 1),
        "A_log": np.tile(g("L0_attn_a_A_log"), QUARTERS).reshape(P, 1),
        "D": g("L0_attn_a_D_param").reshape(H),
        "norm_w": g("L0_attn_a_norm_w").reshape(XT, P).T,
        "w_out": g("L0_attn_a_W_out").T.reshape(XT, P, D).transpose(1, 0, 2),
        "ident": np.eye(P, dtype=np.float32),
        "identb": np.eye(P).astype(bf),
        "before": (NEG * np.tril(np.ones((P, P)), -1)).astype(bf),
        "after": (NEG * np.triu(np.ones((P, P)), 1)).astype(bf),
        "earlier": np.triu(np.ones((P, P)), 1).astype(bf),
        "onesb": np.ones((P, P)).astype(bf),
        "spread": np.tile(np.repeat(np.eye(E), FI, axis=1), (PARTS, 1)).astype(bf),
        "w_router": g("L0_ffn_gate_w").reshape(KD, P, E).transpose(1, 0, 2),
        "w_gate": g("L0_ffn_w_gate").transpose(1, 0, 2).reshape(KD, P, E * FI).transpose(1, 0, 2),
        "w_up": g("L0_ffn_w_up").transpose(1, 0, 2).reshape(KD, P, E * FI).transpose(1, 0, 2),
        "w_down": g("L0_ffn_w_down").reshape(FT, P, D).transpose(1, 0, 2),
        "w_qkv": w_qkv,
        "bqk": b_qkv[0:2 * D].reshape(4, P).T,
        "bv": b_qkv[2 * D:].reshape(D),
        "wo": g("L0_attn_b_w_out").reshape(KD, P, D).transpose(1, 0, 2),
        "bo": g("L0_attn_b_b_out").reshape(D),
    }
    arrays = {n: np.ascontiguousarray(v) for n, v in arrays.items()}
    nc = bacc.Bacc("TRN2", target_bir_lowering=False, num_devices=1)
    a = {n: nc.dram_tensor("in_" + n, v.shape, mb.dt.from_np(v.dtype), kind="ExternalInput").ap() for n, v in arrays.items()}
    out = nc.dram_tensor("out", (T, D), F32, kind="ExternalOutput").ap()
    build(nc, a, out)
    r = run(nc, [{"in_" + n: v for n, v in arrays.items()}], core_ids=[0])
    return r.results[0]["out"].reshape(B, L, D)
```
